# Optimizing a Trainium2 kernel written in Bass

```python
import numpy as np
import jax
import jax.numpy as jnp

def _softmax(x, axis=-1):
    return jax.nn.softmax(x, axis=axis)

def _gelu(x):
    return jax.nn.gelu(x, approximate=True)

def _silu(x):
    return jax.nn.silu(x)

def _sigmoid(x):
    return jax.nn.sigmoid(x)

def _layernorm(x, axis=-1, eps=1e-05):
    m = jnp.mean(x, axis=axis, keepdims=True)
    v = jnp.var(x, axis=axis, keepdims=True)
    return (x - m) / jnp.sqrt(v + eps)

def _scatter_add(tgt, idx, src, axis=0):
    return tgt.at[idx].add(src)

def _segment_sum(src, seg, n):
    return jax.ops.segment_sum(src, seg, n)
kernel_name = 'mk_cond_seq_d4_seqx_r8_6aba9f'

def setup_inputs(seed: int=0):
    np.random.seed(seed)
    _w = jnp.asarray

    def _rec_inputs():
        import jax
        import jax.numpy as jnp
        _rk = jax.random.key(seed)
        x = -0.000125 + 0.9999 * jax.random.normal(jax.random.fold_in(_rk, 1), (2, 512, 128), jnp.float32)
        _lenS = 512 - jax.random.randint(jax.random.fold_in(_rk, 7), (2,), 0, max(1, 512 // 4) + 1, jnp.int32)
        _lenS2 = 512 - jax.random.randint(jax.random.fold_in(_rk, 8), (2,), 0, max(1, 512 // 4) + 1, jnp.int32)
        itok_B_0_15 = jax.random.randint(jax.random.fold_in(_rk, 11), (2,), 0, 16, jnp.int32)
        condB_theta = jax.random.uniform(jax.random.fold_in(_rk, 12), (2,), jnp.float32, 0.0, 0.983423)
        condB_phi = jax.random.uniform(jax.random.fold_in(_rk, 13), (2,), jnp.float32, 0.0, 0.961312)
        itok_B_34_63 = jax.random.randint(jax.random.fold_in(_rk, 15), (2,), 34, 64, jnp.int32)
        fside_Bx16xSxS_0 = -1.47943e-05 + 1.00017 * jax.random.normal(jax.random.fold_in(_rk, 16), (2, 16, 512, 512), jnp.float32)
        itok_B_6_14 = jax.random.randint(jax.random.fold_in(_rk, 17), (2,), 6, 15, jnp.int32)
        _validS = jnp.arange(512)[None, :] < _lenS[:, None]
        _validS2 = jnp.arange(512)[None, :] < _lenS2[:, None]
        _causal = jnp.tril(jnp.ones((512, 512), dtype=bool))
        mask_Bx1xSxS_bk0 = jnp.logical_not(jnp.broadcast_to(_validS[:, None, None, :], (2, 1, 512, 512)))
        return (x, itok_B_0_15, condB_theta, condB_phi, itok_B_34_63, fside_Bx16xSxS_0, itok_B_6_14, mask_Bx1xSxS_bk0)
    x, itok_B_0_15, condB_theta, condB_phi, itok_B_34_63, fside_Bx16xSxS_0, itok_B_6_14, mask_Bx1xSxS_bk0 = _rec_inputs()

    def _L0_cond_setup():
        import jax, jax.numpy as jnp
        import numpy as np
        B, S, D = (32, 128, 128)
        A = 32
        E = 16
        LN_EPS = 1e-05
        key = jax.random.key(seed)
        ks = jax.random.split(key, 10)
        s = lambda fan_in: 1.0 / np.sqrt(fan_in)
        return {'hidden_states': jax.random.normal(ks[0], (B, S, D), dtype=jnp.float32), 'domain_id': jax.random.randint(ks[1], (B,), 0, E, dtype=jnp.int64), 'down_W': jax.random.uniform(ks[2], (A, D), jnp.float32, -s(D), s(D)), 'down_b': jax.random.uniform(ks[3], (A,), jnp.float32, -s(D), s(D)), 'up_W': jax.random.uniform(ks[4], (D, A), jnp.float32, -s(A), s(A)), 'up_b': jax.random.uniform(ks[5], (D,), jnp.float32, -s(A), s(A)), 'expert_W': jax.random.uniform(ks[6], (E, A, A), jnp.float32, -s(A), s(A)), 'expert_b': jax.random.uniform(ks[7], (E, A), jnp.float32, -s(A), s(A)), 'domain_emb': jax.random.normal(ks[8], (E, A), dtype=jnp.float32), 'ln_gamma': jnp.ones((D,), jnp.float32), 'ln_beta': jnp.zeros((D,), jnp.float32)}
    _L0_cond_all = _L0_cond_setup()
    _L0_cond_in = {k: v for k, v in _L0_cond_all.items() if k in ('down_W', 'down_b', 'up_W', 'up_b', 'expert_W', 'expert_b', 'domain_emb', 'ln_gamma', 'ln_beta')}
    del _L0_cond_all

    def _L1_cond_setup():
        import jax, jax.numpy as jnp
        import numpy as np
        key = jax.random.key(seed)
        k1, k2, k3 = jax.random.split(key, 3)
        B, N, D = (16, 512, 128)
        embeddings = jax.random.normal(k1, (B, N, D), dtype=jnp.float32)
        theta = jax.random.uniform(k2, (B,), dtype=jnp.float32)
        phi = jax.random.uniform(k3, (B,), dtype=jnp.float32)
        return {'embeddings': embeddings, 'theta': theta, 'phi': phi}
    _L1_cond_all = _L1_cond_setup()
    _L1_cond_in = {k: v for k, v in _L1_cond_all.items() if k in ()}
    del _L1_cond_all

    def _L2_cond_setup():
        import jax, jax.numpy as jnp
        import numpy as np
        import math
        D_MODEL = 128
        N_HEAD = 16
        HEAD_DIM = D_MODEL // N_HEAD
        D_FF = 512
        NUM_STEPS = 100.0
        RESCALE = 4000.0
        EPS = 1e-05

        def _sin_emb(t):
            half = D_MODEL // 2
            x = t.astype(jnp.float32) / NUM_STEPS * RESCALE
            freqs = jnp.exp(jnp.arange(half, dtype=jnp.float32) * (-math.log(10000.0) / (half - 1)))
            e = x[:, None] * freqs[None, :]
            return jnp.concatenate([jnp.sin(e), jnp.cos(e)], axis=-1)

        def _ln(x):
            m = jnp.mean(x, axis=-1, keepdims=True)
            v = jnp.var(x, axis=-1, keepdims=True)
            return (x - m) / jnp.sqrt(v + EPS)

        def _gelu2(x):
            return x * jax.nn.sigmoid(1.702 * x)
        key = jax.random.key(seed)
        ks = jax.random.split(key, 24)
        B, S, D, F = (4, 64, D_MODEL, D_FF)
        std = 0.02
        inp = {'src': jax.random.normal(ks[0], (B, S, D), dtype=jnp.float32), 'src_mask': jax.random.randint(ks[1], (B, 1, S, S), 0, 2).astype(bool), 'timestep': jax.random.randint(ks[2], (B,), 0, 100, dtype=jnp.int32), 'attention_bias': jax.random.normal(ks[3], (B, N_HEAD, S, S), dtype=jnp.float32), 'W_ada': jax.random.normal(ks[4], (D, 2 * D), dtype=jnp.float32) * std, 'b_ada': jnp.zeros((2 * D,), dtype=jnp.float32), 'Wq': jax.random.normal(ks[5], (D, D), dtype=jnp.float32) * std, 'bq': jnp.zeros((D,), dtype=jnp.float32), 'Wk': jax.random.normal(ks[6], (D, D), dtype=jnp.float32) * std, 'bk': jnp.zeros((D,), dtype=jnp.float32), 'Wv': jax.random.normal(ks[7], (D, D), dtype=jnp.float32) * std, 'bv': jnp.zeros((D,), dtype=jnp.float32), 'Wo': jax.random.normal(ks[8], (D, D), dtype=jnp.float32) * std, 'bo': jnp.zeros((D,), dtype=jnp.float32), 'W1': jax.random.normal(ks[9], (D, F), dtype=jnp.float32) * std, 'b1': jnp.zeros((F,), dtype=jnp.float32), 'W2': jax.random.normal(ks[10], (F, D), dtype=jnp.float32) * std, 'b2': jnp.zeros((D,), dtype=jnp.float32), 'g2': jnp.ones((D,), dtype=jnp.float32), 'beta2': jnp.zeros((D,), dtype=jnp.float32)}
        return inp
    _L2_cond_all = _L2_cond_setup()
    _L2_cond_in = {k: v for k, v in _L2_cond_all.items() if k in ('W_ada', 'b_ada', 'Wq', 'bq', 'Wk', 'bk', 'Wv', 'bv', 'Wo', 'bo', 'W1', 'b1', 'W2', 'b2', 'g2', 'beta2')}
    del _L2_cond_all

    def _L3_cond_setup():
        import jax, jax.numpy as jnp
        import numpy as np
        D = 128
        E = 8
        FF = 512
        TOPK = 2
        S = 32
        SE = 64
        SH = 128
        B, T = (2, 256)

        def _forward(x, subject_ids, ln_g, ln_b, subj_emb, hyp_w1, hyp_b1, hyp_w2, hyp_b2, sty_w1, sty_b1, sty_w2, sty_b2, router_w, exp_w1, exp_b1, exp_w2, exp_b2):
            mu = x.mean(-1, keepdims=True)
            var = x.var(-1, keepdims=True)
            h = (x - mu) * jax.lax.rsqrt(var + 1e-05) * ln_g + ln_b
            m_t = h.mean(1, keepdims=True)
            v_t = h.var(1, keepdims=True)
            h_norm = (h - m_t) * jax.lax.rsqrt(v_t + 1e-08)
            se = subj_emb[subject_ids]
            hyp = jax.nn.relu(se @ hyp_w1 + hyp_b1) @ hyp_w2 + hyp_b2
            sty = jax.nn.relu(hyp @ sty_w1 + sty_b1) @ sty_w2 + sty_b2
            gamma, beta = jnp.split(sty, 2, axis=-1)
            gamma = jax.nn.softplus(gamma) + 1e-08
            h = h_norm * gamma[:, None, :] + beta[:, None, :]
            h_flat = h.reshape(-1, D)
            probs = jax.nn.softmax(h_flat @ router_w, axis=-1)
            gates, idx = jax.lax.top_k(probs, TOPK)
            gates = gates / gates.sum(-1, keepdims=True)
            N = h_flat.shape[0]
            combine = jnp.zeros((N, E), h_flat.dtype).at[jnp.arange(N)[:, None], idx].add(gates)
            hid = jax.nn.relu(jnp.einsum('nd,edf->nef', h_flat, exp_w1) + exp_b1)
            eout = jnp.einsum('nef,efd->ned', hid, exp_w2) + exp_b2
            y = jnp.einsum('ned,ne->nd', eout, combine)
            return x + y.reshape(x.shape)
        key = jax.random.key(seed)
        ks = jax.random.split(key, 16)
        n = lambda k, sh, s=0.02: jax.random.normal(k, sh, dtype=jnp.float32) * s
        return {'x': jax.random.normal(ks[0], (B, T, D), dtype=jnp.float32), 'subject_ids': jax.random.randint(ks[1], (B,), 0, S), 'ln_g': jnp.ones((D,), jnp.float32), 'ln_b': jnp.zeros((D,), jnp.float32), 'subj_emb': n(ks[2], (S, SE)), 'hyp_w1': n(ks[3], (SE, SH), 1.0 / np.sqrt(SE)), 'hyp_b1': jnp.zeros((SH,), jnp.float32), 'hyp_w2': n(ks[4], (SH, SH), 1.0 / np.sqrt(SH)), 'hyp_b2': jnp.zeros((SH,), jnp.float32), 'sty_w1': n(ks[5], (SH, SH // 2), 1.0 / np.sqrt(SH)), 'sty_b1': jnp.zeros((SH // 2,), jnp.float32), 'sty_w2': n(ks[6], (SH // 2, 2 * D), 1.0 / np.sqrt(SH // 2)), 'sty_b2': jnp.zeros((2 * D,), jnp.float32), 'router_w': n(ks[7], (D, E), 1.0 / np.sqrt(D)), 'exp_w1': n(ks[8], (E, D, FF), 1.0 / np.sqrt(D)), 'exp_b1': jnp.zeros((E, FF), jnp.float32), 'exp_w2': n(ks[9], (E, FF, D), 1.0 / np.sqrt(FF)), 'exp_b2': jnp.zeros((E, D), jnp.float32)}
    _L3_cond_all = _L3_cond_setup()
    _L3_cond_in = {k: v for k, v in _L3_cond_all.items() if k in ('ln_g', 'ln_b', 'subj_emb', 'hyp_w1', 'hyp_b1', 'hyp_w2', 'hyp_b2', 'sty_w1', 'sty_b1', 'sty_w2', 'sty_b2', 'router_w', 'exp_w1', 'exp_b1', 'exp_w2', 'exp_b2')}
    del _L3_cond_all
    return {'x': x, 'itok_B_0_15': itok_B_0_15, 'condB_theta': condB_theta, 'condB_phi': condB_phi, 'itok_B_34_63': itok_B_34_63, 'fside_Bx16xSxS_0': fside_Bx16xSxS_0, 'itok_B_6_14': itok_B_6_14, 'mask_Bx1xSxS_bk0': mask_Bx1xSxS_bk0, 'L0_cond_down_W': _L0_cond_in['down_W'], 'L0_cond_down_b': _L0_cond_in['down_b'], 'L0_cond_up_W': _L0_cond_in['up_W'], 'L0_cond_up_b': _L0_cond_in['up_b'], 'L0_cond_expert_W': _L0_cond_in['expert_W'], 'L0_cond_expert_b': _L0_cond_in['expert_b'], 'L0_cond_domain_emb': _L0_cond_in['domain_emb'], 'L0_cond_ln_gamma': _L0_cond_in['ln_gamma'], 'L0_cond_ln_beta': _L0_cond_in['ln_beta'], 'L2_cond_W_ada': _L2_cond_in['W_ada'], 'L2_cond_b_ada': _L2_cond_in['b_ada'], 'L2_cond_Wq': _L2_cond_in['Wq'], 'L2_cond_bq': _L2_cond_in['bq'], 'L2_cond_Wk': _L2_cond_in['Wk'], 'L2_cond_bk': _L2_cond_in['bk'], 'L2_cond_Wv': _L2_cond_in['Wv'], 'L2_cond_bv': _L2_cond_in['bv'], 'L2_cond_Wo': _L2_cond_in['Wo'], 'L2_cond_bo': _L2_cond_in['bo'], 'L2_cond_W1': _L2_cond_in['W1'], 'L2_cond_b1': _L2_cond_in['b1'], 'L2_cond_W2': _L2_cond_in['W2'], 'L2_cond_b2': _L2_cond_in['b2'], 'L2_cond_g2': _L2_cond_in['g2'], 'L2_cond_beta2': _L2_cond_in['beta2'], 'L3_cond_ln_g': _L3_cond_in['ln_g'], 'L3_cond_ln_b': _L3_cond_in['ln_b'], 'L3_cond_subj_emb': _L3_cond_in['subj_emb'], 'L3_cond_hyp_w1': _L3_cond_in['hyp_w1'], 'L3_cond_hyp_b1': _L3_cond_in['hyp_b1'], 'L3_cond_hyp_w2': _L3_cond_in['hyp_w2'], 'L3_cond_hyp_b2': _L3_cond_in['hyp_b2'], 'L3_cond_sty_w1': _L3_cond_in['sty_w1'], 'L3_cond_sty_b1': _L3_cond_in['sty_b1'], 'L3_cond_sty_w2': _L3_cond_in['sty_w2'], 'L3_cond_sty_b2': _L3_cond_in['sty_b2'], 'L3_cond_router_w': _L3_cond_in['router_w'], 'L3_cond_exp_w1': _L3_cond_in['exp_w1'], 'L3_cond_exp_b1': _L3_cond_in['exp_b1'], 'L3_cond_exp_w2': _L3_cond_in['exp_w2'], 'L3_cond_exp_b2': _L3_cond_in['exp_b2']}

def reference(x, itok_B_0_15, condB_theta, condB_phi, itok_B_34_63, fside_Bx16xSxS_0, itok_B_6_14, mask_Bx1xSxS_bk0, L0_cond_down_W, L0_cond_down_b, L0_cond_up_W, L0_cond_up_b, L0_cond_expert_W, L0_cond_expert_b, L0_cond_domain_emb, L0_cond_ln_gamma, L0_cond_ln_beta, L2_cond_W_ada, L2_cond_b_ada, L2_cond_Wq, L2_cond_bq, L2_cond_Wk, L2_cond_bk, L2_cond_Wv, L2_cond_bv, L2_cond_Wo, L2_cond_bo, L2_cond_W1, L2_cond_b1, L2_cond_W2, L2_cond_b2, L2_cond_g2, L2_cond_beta2, L3_cond_ln_g, L3_cond_ln_b, L3_cond_subj_emb, L3_cond_hyp_w1, L3_cond_hyp_b1, L3_cond_hyp_w2, L3_cond_hyp_b2, L3_cond_sty_w1, L3_cond_sty_b1, L3_cond_sty_w2, L3_cond_sty_b2, L3_cond_router_w, L3_cond_exp_w1, L3_cond_exp_b1, L3_cond_exp_w2, L3_cond_exp_b2):
    import jax
    import jax.numpy as jnp

    def _L0_cond_ref(hidden_states, domain_id, down_W, down_b, up_W, up_b, expert_W, expert_b, domain_emb, ln_gamma, ln_beta):
        import jax, jax.numpy as jnp
        import numpy as np
        B, S, D = (32, 128, 128)
        A = 32
        E = 16
        LN_EPS = 1e-05
        residual = hidden_states
        hidden = jnp.einsum('bsd,ad->bsa', hidden_states, down_W) + down_b
        hidden = jax.nn.gelu(hidden, approximate=False)
        valid = (domain_id >= 0) & (domain_id < E)
        idx = jnp.clip(domain_id, 0, E - 1)
        Wsel = expert_W[idx]
        bsel = expert_b[idx]
        expert_out = jnp.einsum('bsa,boa->bso', hidden, Wsel) + bsel[:, None, :]
        domain_output = jnp.where(valid[:, None, None], expert_out, hidden)
        hidden = domain_output + domain_emb[idx][:, None, :]
        hidden = jnp.einsum('bsa,da->bsd', hidden, up_W) + up_b
        x = hidden + residual
        mu = jnp.mean(x, axis=-1, keepdims=True)
        var = jnp.mean(jnp.square(x - mu), axis=-1, keepdims=True)
        return (x - mu) * jax.lax.rsqrt(var + LN_EPS) * ln_gamma + ln_beta

    def _L1_cond_ref(embeddings, theta, phi):
        import jax, jax.numpy as jnp
        import numpy as np
        B, N, D = embeddings.shape
        e = embeddings.reshape(B, N, D // 4, 4)
        ct = jnp.cos(theta)[:, None, None]
        st = jnp.sin(theta)[:, None, None]
        cp = jnp.cos(phi)[:, None, None]
        sp = jnp.sin(phi)[:, None, None]
        x0, x1, x2, x3 = (e[..., 0], e[..., 1], e[..., 2], e[..., 3])
        out = jnp.stack([x0 * ct + x1 * st, -x0 * st + x1 * ct, x2 * cp + x3 * sp, -x2 * sp + x3 * cp], axis=-1)
        return out.reshape(B, N, D)

    def _L2_cond_ref(src, src_mask, timestep, attention_bias, W_ada, b_ada, Wq, bq, Wk, bk, Wv, bv, Wo, bo, W1, b1, W2, b2, g2, beta2):
        import jax, jax.numpy as jnp
        import numpy as np
        import math
        D_MODEL = 128
        N_HEAD = 16
        HEAD_DIM = D_MODEL // N_HEAD
        D_FF = 512
        NUM_STEPS = 100.0
        RESCALE = 4000.0
        EPS = 1e-05

        def _sin_emb(t):
            half = D_MODEL // 2
            x = t.astype(jnp.float32) / NUM_STEPS * RESCALE
            freqs = jnp.exp(jnp.arange(half, dtype=jnp.float32) * (-math.log(10000.0) / (half - 1)))
            e = x[:, None] * freqs[None, :]
            return jnp.concatenate([jnp.sin(e), jnp.cos(e)], axis=-1)

        def _ln(x):
            m = jnp.mean(x, axis=-1, keepdims=True)
            v = jnp.var(x, axis=-1, keepdims=True)
            return (x - m) / jnp.sqrt(v + EPS)

        def _gelu2(x):
            return x * jax.nn.sigmoid(1.702 * x)
        B, S, D = src.shape
        emb = jax.nn.silu(_sin_emb(timestep)) @ W_ada + b_ada
        scale, shift = jnp.split(emb[:, None, :], 2, axis=-1)
        x = _ln(src) * (1.0 + scale) + shift
        q = (x @ Wq + bq).reshape(B, S, N_HEAD, HEAD_DIM).transpose(0, 2, 1, 3)
        k = (x @ Wk + bk).reshape(B, S, N_HEAD, HEAD_DIM).transpose(0, 2, 1, 3)
        v = (x @ Wv + bv).reshape(B, S, N_HEAD, HEAD_DIM).transpose(0, 2, 1, 3)
        scores = jnp.einsum('bhqd,bhkd->bhqk', q / math.sqrt(HEAD_DIM), k)
        scores = scores + attention_bias
        scores = jnp.where(src_mask, -jnp.inf, scores.astype(jnp.float32))
        probs = jax.nn.softmax(scores, axis=-1).astype(v.dtype)
        ctx = jnp.einsum('bhqk,bhkd->bhqd', probs, v)
        ctx = ctx.transpose(0, 2, 1, 3).reshape(B, S, D)
        x = x + (ctx @ Wo + bo)
        h = _ln(x) * g2 + beta2
        ff = _gelu2(h @ W1 + b1) @ W2 + b2
        return x + ff

    def _L3_cond_ref(x, subject_ids, ln_g, ln_b, subj_emb, hyp_w1, hyp_b1, hyp_w2, hyp_b2, sty_w1, sty_b1, sty_w2, sty_b2, router_w, exp_w1, exp_b1, exp_w2, exp_b2):
        import jax, jax.numpy as jnp
        import numpy as np
        D = 128
        E = 8
        FF = 512
        TOPK = 2
        S = 32
        SE = 64
        SH = 128
        B, T = (2, 256)

        def _forward(x, subject_ids, ln_g, ln_b, subj_emb, hyp_w1, hyp_b1, hyp_w2, hyp_b2, sty_w1, sty_b1, sty_w2, sty_b2, router_w, exp_w1, exp_b1, exp_w2, exp_b2):
            mu = x.mean(-1, keepdims=True)
            var = x.var(-1, keepdims=True)
            h = (x - mu) * jax.lax.rsqrt(var + 1e-05) * ln_g + ln_b
            m_t = h.mean(1, keepdims=True)
            v_t = h.var(1, keepdims=True)
            h_norm = (h - m_t) * jax.lax.rsqrt(v_t + 1e-08)
            se = subj_emb[subject_ids]
            hyp = jax.nn.relu(se @ hyp_w1 + hyp_b1) @ hyp_w2 + hyp_b2
            sty = jax.nn.relu(hyp @ sty_w1 + sty_b1) @ sty_w2 + sty_b2
            gamma, beta = jnp.split(sty, 2, axis=-1)
            gamma = jax.nn.softplus(gamma) + 1e-08
            h = h_norm * gamma[:, None, :] + beta[:, None, :]
            h_flat = h.reshape(-1, D)
            probs = jax.nn.softmax(h_flat @ router_w, axis=-1)
            gates, idx = jax.lax.top_k(probs, TOPK)
            gates = gates / gates.sum(-1, keepdims=True)
            N = h_flat.shape[0]
            combine = jnp.zeros((N, E), h_flat.dtype).at[jnp.arange(N)[:, None], idx].add(gates)
            hid = jax.nn.relu(jnp.einsum('nd,edf->nef', h_flat, exp_w1) + exp_b1)
            eout = jnp.einsum('nef,efd->ned', hid, exp_w2) + exp_b2
            y = jnp.einsum('ned,ne->nd', eout, combine)
            return x + y.reshape(x.shape)
        return _forward(x, subject_ids, ln_g, ln_b, subj_emb, hyp_w1, hyp_b1, hyp_w2, hyp_b2, sty_w1, sty_b1, sty_w2, sty_b2, router_w, exp_w1, exp_b1, exp_w2, exp_b2)
    x = _L0_cond_ref(x, itok_B_0_15, L0_cond_down_W, L0_cond_down_b, L0_cond_up_W, L0_cond_up_b, L0_cond_expert_W, L0_cond_expert_b, L0_cond_domain_emb, L0_cond_ln_gamma, L0_cond_ln_beta)
    x = _L1_cond_ref(x, condB_theta, condB_phi)
    x = _L2_cond_ref(x, mask_Bx1xSxS_bk0, itok_B_34_63, fside_Bx16xSxS_0, L2_cond_W_ada, L2_cond_b_ada, L2_cond_Wq, L2_cond_bq, L2_cond_Wk, L2_cond_bk, L2_cond_Wv, L2_cond_bv, L2_cond_Wo, L2_cond_bo, L2_cond_W1, L2_cond_b1, L2_cond_W2, L2_cond_b2, L2_cond_g2, L2_cond_beta2)
    x = _L3_cond_ref(x, itok_B_6_14, L3_cond_ln_g, L3_cond_ln_b, L3_cond_subj_emb, L3_cond_hyp_w1, L3_cond_hyp_b1, L3_cond_hyp_w2, L3_cond_hyp_b2, L3_cond_sty_w1, L3_cond_sty_b1, L3_cond_sty_w2, L3_cond_sty_b2, L3_cond_router_w, L3_cond_exp_w1, L3_cond_exp_b1, L3_cond_exp_w2, L3_cond_exp_b2)
    return x

_drawn_inputs = setup_inputs


def setup_inputs(seed=0):
    import zlib

    import numpy as np

    out = dict(_drawn_inputs(seed))
    spreads = {'L0_cond_ln_gamma': (1.0, 0.2),
     'L0_cond_ln_beta': (0.0, 0.1),
     'L2_cond_b_ada': (0.0, 0.1),
     'L2_cond_bq': (0.0, 0.8),
     'L2_cond_bk': (0.0, 0.8),
     'L2_cond_bv': (0.0, 0.37),
     'L2_cond_bo': (0.0, 0.1),
     'L2_cond_b1': (0.0, 0.1),
     'L2_cond_b2': (0.0, 0.1),
     'L2_cond_g2': (1.0, 0.2),
     'L2_cond_beta2': (0.0, 0.8),
     'L3_cond_ln_g': (1.0, 0.6),
     'L3_cond_ln_b': (0.0, 0.8),
     'L3_cond_hyp_b1': (0.0, 0.1),
     'L3_cond_hyp_b2': (0.0, 0.1),
     'L3_cond_sty_b1': (0.0, 0.1),
     'L3_cond_sty_b2': (0.0, 0.1),
     'L3_cond_exp_b1': (0.0, 0.1),
     'L3_cond_exp_b2': (0.0, 0.1)}
    factors = {'fside_Bx16xSxS_0': 3.422, 'L2_cond_Wq': 8.0, 'L2_cond_Wk': 8.0}
    for name, (base, spread) in spreads.items():
        noise = np.random.default_rng([zlib.crc32(name.encode()), seed]).standard_normal(out[name].shape)
        drawn = base * np.exp(spread * noise) if base else spread * noise
        out[name] = jnp.asarray(drawn.astype(out[name].dtype))
    for name, factor in factors.items():
        out[name] = (out[name] * factor).astype(out[name].dtype)
    return out
```

```python
import math
from contextlib import ExitStack

import numpy as np
import concourse.bass as bass
from concourse import mybir
from concourse.alu_op_type import AluOpType as ALU

F32 = mybir.dt.float32
BF16 = mybir.dt.bfloat16
I32 = mybir.dt.int32
U8 = mybir.dt.uint8
ACT = mybir.ActivationFunctionType
AX_X = mybir.AxisListType.X

P = 128
B, S, D = 2, 512, 128
TOK = B * S
NT = TOK // P
QT = S // P
A = 32
E0 = 16
NH, DH = 16, 8
HG = 4
NG = B * NH // HG
FF = 512
FT = FF // P
NE = 8
SUBJ, SE = 32, 64
VW = DH + 1
PARTS = 3
STACK = PARTS * PARTS * DH
LN_EPS = 1e-5
MASKED = -1e30
ROUND = 1.5 * 2.0 ** 23
TWO_PI = (6.28125, 0.00193500518798828125, 2 * math.pi - 6.28125 - 0.00193500518798828125)
PI_BELOW = 3.1415925

EARLY = (("ident", P), ("freq", 1), ("iota16", E0), ("row", 1), ("down", A))
LATE = (("w_ada", 2 * D), ("b_ada", 2), ("wq", D), ("wk", D), ("wv", D), ("wo", D), ("bq", 1), ("bk", 1),
        ("g2", 1), ("beta2", 1), ("ln_g", 1), ("ln_b", 1), ("router", NE), ("hyp_w2", D), ("hyp_b1", 1),
        ("hyp_b2", 1), ("sty_w1", D // 2), ("sty_b2", 2), ("b1", FT), ("exp_b1", NE * FT), ("w1", FF), ("w2", FF))
PACK32 = (("expert_w", E0 * A), ("expert_b", E0), ("emb", E0), ("down_b", 1), ("subj", SE), ("eye", A))
PACK64 = (("hyp_w1", D), ("sty_b1", 1), ("sty_w2", 2 * D))
ROWS = (("gamma", D), ("beta", D), ("bv", D), ("bo", D), ("b2", D))


def width(columns):
    return sum(n for _, n in columns)


def columns_of(tile, columns):
    out, at = {}, 0
    for name, n in columns:
        out[name] = tile[:, at:at + n]
        at += n
    return out


def build(nc, x_n, x_t, early_d, late_d, pack32_d, up_d, pack64_d, rows_d, ids_d, ang_d, bias_d, mask_d,
          w1_d, w2_d, eb2_d, out_d):
    with ExitStack() as ctx:
        def sb(name, shape, dt=F32):
            return ctx.enter_context(nc.sbuf_tensor(name, shape, dt))

        def sem(name):
            return ctx.enter_context(nc.semaphore(name))

        bank = [ctx.enter_context(nc.psum_tensor(f"bank{i}", [P, 512], F32)) for i in range(8)]
        score_ps, turned_ps, ctx_ps = bank[0:4], bank[4:6], bank[6:8]

        q_dram = nc.dram_tensor("q_parts", (B, PARTS * PARTS, D, S), BF16).ap()
        k_dram = nc.dram_tensor("k_parts", (B, PARTS * PARTS, D, S), BF16).ap()

        early = sb("early", [P, width(EARLY)])
        late = sb("late", [P, width(LATE)])
        pack32 = sb("pack32", [A, width(PACK32)])
        pack64 = sb("pack64", [SE, width(PACK64)])
        rows = sb("rows", [P, width(ROWS)])
        up = sb("up", [A + 1, D])
        ids_i = sb("ids_i", [P, 6], I32)
        angles = sb("angles", [P, 4])
        eb2 = sb("eb2", [NE, D])
        C, L, W32, W64, R = (columns_of(early, EARLY), columns_of(late, LATE), columns_of(pack32, PACK32),
                             columns_of(pack64, PACK64), columns_of(rows, ROWS))
        ident = C["ident"]

        ring = sb("ring", [P, 8, HG, S])
        probs = sb("probs", [P, 2, HG, QT, S])
        q_st = sb("q_st", [P, 2, HG, S], BF16)
        k_st = sb("k_st", [P, 2, HG, S], BF16)
        v_all = sb("v_all", [P, NG, QT, HG, VW])
        v_st = sb("v_st", [P, 2, QT, HG, 32])
        mask_u8 = probs[:, 0, 0, 0:2, :].rearrange("p a n -> p (a n)").bitcast(U8)
        mask_bf = sb("mask_bf", [P, B, QT, S], BF16)
        ctx_t = sb("ctx_t", [P, NG, S])
        row_max = sb("row_max", [P, 8 * HG])
        diag_masked = sb("diag_masked", [P, P], BF16)
        all_masked = sb("all_masked", [P, 3, NT])
        xt = sb("xt", [P, TOK])
        xn = sb("xn", [P, NT, D])
        zn = sb("zn", [P, NT, D])
        stats = sb("stats", [P, NT, 6])
        moments = sb("moments", [P, NT, 2])
        rstd = sb("rstd", [P, NT])
        small = sb("small", [P, 64])

        flat = probs[:, :, :, :, :].rearrange("p a h k s -> p (a h k s)")
        hid_e = flat[:, 0:2 * FT * TOK].rearrange("p (e f n) -> p e f n", e=2, f=FT)
        pre = flat[:, 4096:16384]
        sel_prod = pre[0:A, 0:B * A * E0].rearrange("p (b o e) -> p b o e", b=B, o=A)
        sel_w = pre[0:A, 1024:1024 + B * A].rearrange("p (b o) -> p b o", b=B)
        ad_h = pre[0:A, 4096:4096 + TOK]
        ad_e = pre[0:A + 1, 5120:6144]
        rot_a, rot_b, rot_c = (pre[:, 6144 + 256 * i:6400 + 256 * i].rearrange("p (b d) -> p b d", b=B)
                               for i in range(3))
        swapped = pre[:, 7168:8192].rearrange("p (t d) -> p t d", t=NT)
        qk_f = pre[:, 8192:12288].rearrange("p (n c) -> p n c", n=8)
        late_free = ring[:, :, :, :].rearrange("p u h s -> p (u h s)")
        w1_e = late_free[:, 0:2 * FF].rearrange("p (e f) -> p e f", e=2)
        w2_e = late_free[:, 1024:1024 + 2 * FF].rearrange("p (e f d) -> p e f d", e=2, f=FT)
        h_t = late_free[:, 2048:2048 + TOK]
        ff_g = late_free[:, 3072:3072 + 4096].rearrange("p (f n) -> p f n", f=FT)
        ff_a = late_free[:, 7168:7168 + 4096].rearrange("p (f n) -> p f n", f=FT)
        acc = late_free[:, 11264:11264 + TOK].rearrange("p (t d) -> p t d", t=NT)
        ctx_n = late_free[:, 12288:13312].rearrange("p (t d) -> p t d", t=NT)
        ctx_nt = late_free[:, 13312:14336]
        h3_t = late_free[:, 14336:15360]
        route = late_free[:, 15360:15360 + 12 * NT * NE].rearrange("p (a t e) -> p a t e", a=12, t=NT)
        comb_t = flat[0:NE, 8192:8192 + TOK]
        parts_q, parts_k = (flat[:, 8192 + 1536 * i:9728 + 1536 * i].bitcast(BF16)
                            .rearrange("p (b n s) -> p b n s", b=B, n=PARTS) for i in range(2))

        in_xt, in_early, in_ids, in_p32, in_up, in_rows, in_xn = (
            sem(n) for n in ("in_xt", "in_early", "in_ids", "in_p32", "in_up", "in_rows", "in_xn"))
        in_late, in_p64, in_mask, in_eb2 = (sem(n) for n in ("in_late", "in_p64", "in_mask", "in_eb2"))
        bias_in = [sem(f"bias_in{i}") for i in range(8)]
        experts_in = [sem(f"experts_in{i}") for i in range(2)]
        stacks_out = [sem(f"stacks_out{b}") for b in range(B)]
        stack_in = [sem(f"stack_in{i}") for i in range(2)]
        dve_step, act_step, pool_step = sem("dve_step"), sem("act_step"), sem("pool_step")
        (trig_ready, sin_done, silu_exp_done, silu_ready, ada_done, ada_ready, sel_ready, down_done,
         gelu_ready, expert_done, expert_ready, up_done) = (
            sem(n) for n in ("trig_ready", "sin_done", "silu_exp_done", "silu_ready", "ada_done", "ada_ready",
                             "sel_ready", "down_done", "gelu_ready", "expert_done", "expert_ready",
                             "up_done"))
        var_ready, sqrt_done, norm_ready, turned, xt_ready = (
            sem(n) for n in ("var_ready", "sqrt_done", "norm_ready", "turned", "xt_ready"))
        qk_proj, qk_float, part_hi, rest_ready, part_mid, part_lo, v_proj, v_ready, qk_free = (
            sem(n) for n in ("qk_proj", "qk_float", "part_hi", "rest_ready", "part_mid", "part_lo", "v_proj",
                             "v_ready", "qk_free"))
        (mask_ready, pad_ready, qk_done, sum_done, shift_done, tr_done, exp_done, v_staged, pv_done,
         ctx_copied) = (
            sem(n) for n in ("mask_ready", "pad_ready", "qk_done", "sum_done", "shift_done", "tr_done",
                             "exp_done", "v_staged", "pv_done", "ctx_copied"))
        ctx_turned, ctx_scaled, ctx_back, ctx_back_copied, wo_done, res_ready = (
            sem(n) for n in ("ctx_turned", "ctx_scaled", "ctx_back", "ctx_back_copied", "wo_done", "res_ready"))
        ff1_done, ff_gate, ff_ready, ff2_done, ff_out = (
            sem(n) for n in ("ff1_done", "ff_gate", "ff_ready", "ff2_done", "ff_out"))
        hyp_in, hyp_mm, hyp_ready, softplus_in, softplus_done, style_ready = (
            sem(n) for n in ("hyp_in", "hyp_mm", "hyp_ready", "softplus_in", "softplus_done", "style_ready"))
        (route_in, logits_done, logit_max, logit_exp, comb_ready, comb_turned, comb_t_ready, eb2_done) = (
            sem(n) for n in ("route_in", "logits_done", "logit_max", "logit_exp", "comb_ready", "comb_turned",
                             "comb_t_ready", "eb2_done"))
        up_e_done, hid_ready, down_e_done, acc_done = (
            sem(n) for n in ("up_e_done", "hid_ready", "down_e_done", "acc_done"))

        rot_done, t_var_ready, t_sqrt_done, out_written = (
            sem(n) for n in ("rot_done", "t_var_ready", "t_sqrt_done",
                             "out_written"))
        sb_token = sb("token", [P, 8, NT])

        block = ctx.enter_context(nc.Block())

        def wait(eng, semaphore, value):
            if isinstance(value, int) and value <= 0:
                return
            eng.wait_ge(semaphore, value)

        def chained(eng, semaphore):
            count = [0]

            def link(instruction):
                count[0] += 1
                instruction.then_inc(semaphore, 1)
                eng.wait_ge(semaphore, count[0])

            return link

        id_f, dom, wrap, style_hot, style_cmp = (small[:, 0:6], small[:, 6:8], small[:, 8:10], small[:, 10:12],
                                                 small[:, 12:14])
        valid, ada, trig_x, trig_k = small[:, 14:16], small[:, 16:20], small[:, 20:26], small[:, 26:32]
        trig, neg_sin = small[:, 32:42], small[:, 42:46]
        silu_e, silu = small[:, 46:48], small[:, 48:50]
        emb_b = small[0:A, 50:54]
        softp = small[:, 56:64]
        hot = sb("hot", [A, B, E0])
        hot_prod = sb("hot_prod", [A, 4, E0])
        style = sb("style", [P, 24])
        seT, hid1, hid2, hid3 = style[0:SE, 0:2], style[:, 2:4], style[:, 4:6], style[0:SE, 6:8]
        gam, bet, soft_a, soft_e, soft_l = (style[:, 8:10], style[:, 10:12], style[:, 12:14], style[:, 14:16],
                                            style[:, 16:18])
        t_stats = sb("t_stats", [P, B, 6])
        t_mom = sb("t_mom", [P, B, 2])
        t_coef = sb("t_coef", [P, 4, B])
        b1_sig = sb("b1_sig", [P, FT])

        @block.sync
        def _(sp):
            sp.dma_start(xt[:, :], x_t).then_inc(in_xt, 16)
            sp.dma_start(early[:, :], early_d).then_inc(in_early, 16)
            sp.dma_start(ids_i[:, :], ids_d.partition_broadcast(P)).then_inc(in_ids, 16)
            sp.dma_start(angles[:, :], ang_d.partition_broadcast(P)).then_inc(in_ids, 16)
            sp.dma_start(pack32[:, :], pack32_d).then_inc(in_p32, 16)
            sp.dma_start(up[:, :], up_d).then_inc(in_up, 16)
            sp.dma_start(rows[:, :], rows_d.partition_broadcast(P)).then_inc(in_rows, 16)
            sp.dma_start(xn[:, :, :], x_n.rearrange("(t p) d -> p t d", p=P)).then_inc(in_xn, 16)
            sp.dma_start(late[:, :], late_d).then_inc(in_late, 16)
            sp.dma_start(pack64[:, :], pack64_d).then_inc(in_p64, 16)
            sp.dma_start(eb2[:, :], eb2_d).then_inc(in_eb2, 16)
            sp.dma_start(mask_u8.rearrange("p (u k) -> p u k", u=NT),
                         mask_d.rearrange("b (t p) k -> p (b t) k", p=P)).then_inc(in_mask, 16)

            def load_bias(unit, slot):
                group, tile = unit
                sp.dma_start(ring[:, slot, :, :],
                             bias_d[group, :, tile * P:(tile + 1) * P, :].rearrange("h p k -> p h k")
                             ).then_inc(bias_in[slot], 16)

            def load_stack(b, group, slot):
                for stack, dram in ((q_st, q_dram), (k_st, k_dram)):
                    rows_of = dram[b].rearrange("r (g h c) s -> r g h c s", g=NH // HG, h=HG)
                    for h in range(HG):
                        sp.dma_start(stack[0:STACK, slot, h, :], rows_of[:, group, h]
                                     ).then_inc(stack_in[slot], 16)

            for u in range(8):
                load_bias((u // QT, u % QT), u)

            sp.wait_ge(pad_ready, 1)
            for b in range(B):
                for kind, parts, dram in ((0, parts_q, q_dram), (1, parts_k, k_dram)):
                    sp.wait_ge(part_lo, 2 * b + kind + 1)
                    for r in range(PARTS * PARTS):
                        part = r // PARTS if kind == 0 else r % PARTS
                        sp.dma_start(dram[b, r], parts[:, b, part, :]).then_inc(stacks_out[b], 16)
                sp.wait_ge(stacks_out[b], 16 * 2 * PARTS * PARTS)
                if b == 0:
                    load_stack(0, 0, 0)
                    load_stack(0, 1, 1)
            for it in range(1, NG // 2):
                for v in range(8):
                    sp.wait_ge(tr_done, it * 32 + (4 * (v + 1) - 32))
                    load_bias((it * 2 + v // QT, v % QT), v)
                    if v in (2, 6):
                        sp.wait_ge(qk_done, it * 32 + (16 * (v // QT + 1) - 32))
                        load_stack(it // 2, (it % 2) * 2 + v // QT, v // QT)

            sp.wait_ge(tr_done, 128)

            def load_expert(e, slot):
                sp.dma_start(w1_e[:, slot, :], w1_d[e]).then_inc(experts_in[slot], 16)
                sp.dma_start(w2_e[:, slot, :, :], w2_d[e].rearrange("(f p) d -> p f d", p=P)
                             ).then_inc(experts_in[slot], 16)

            load_expert(0, 0)
            load_expert(1, 1)
            for it in range(1, NE // 2):
                for slot in range(2):
                    sp.wait_ge(down_e_done, it * (2 * B) + (slot - 1) * B)
                    load_expert(it * 2 + slot, slot)

            for b in range(B):
                sp.wait_ge(acc_done, NE * B + b + 1)
                sp.dma_start(out_d[b].rearrange("(t p) d -> p t d", p=P),
                             acc[:, 4 * b:4 * b + 4, :]).then_inc(out_written, 16)
            sp.wait_ge(out_written, 32)

        @block.gpsimd
        def _(pool):
            link = chained(pool, pool_step)
            pool.memset(q_st[:, :, :, :], 0.0)
            pool.memset(k_st[:, :, :, :], 0.0).then_inc(pad_ready, 1)
            pool.memset(v_st[:, :, :, :, :], 0.0)
            pool.memset(v_all[:, :, :, :, :], 1.0).then_inc(pad_ready, 1)
            pool.wait_ge(in_early, 16)
            pool.tensor_scalar(diag_masked[:, :], ident, MASKED, 0.0, ALU.mult, ALU.add).then_inc(pad_ready, 1)
            pool.wait_ge(in_mask, 16)
            pool.tensor_copy(mask_bf[:, :, :, :].rearrange("p b t k -> p (b t k)"), mask_u8).then_inc(mask_ready, 1)

            for b in range(B):
                pool.wait_ge(norm_ready, b + 1)
                pool.wait_ge(trig_ready, 2)
                z = zn[:, 4 * b:4 * b + 4, :].rearrange("p t (i e) -> p t i e", e=2)
                o = swapped[:, 4 * b:4 * b + 4, :].rearrange("p t (i e) -> p t i e", e=2)
                w = rot_b[:, b:b + 1, :].to_broadcast([P, QT, D]).rearrange("p t (i e) -> p t i e", e=2)
                for e in range(2):
                    last = pool.tensor_tensor(o[:, :, :, e], z[:, :, :, 1 - e], w[:, :, :, e], ALU.mult)
                last.then_inc(rot_done, 1)

            def shift(it):
                for v in range(8):
                    for j in range(HG):
                        n = 4 * v + j
                        pool.wait_ge(sum_done, it * 32 + (n + 1))
                        pool.tensor_scalar(ring[:, v, j, :], ring[:, v, j, :], -1.0, row_max[:, n:n + 1],
                                           ALU.mult, ALU.add).then_inc(shift_done, 1)

            for it in range(0, NG // 2):
                shift(it)

        @block.scalar
        def _(act):
            link = chained(act, act_step)
            act.wait_ge(trig_ready, 1)
            act.activation(trig, trig, ACT.Sin).then_inc(sin_done, 1)
            act.wait_ge(sin_done, 1)
            act.activation(silu_e, trig[:, 0:2], ACT.Exp, scale=-1.0).then_inc(silu_exp_done, 1)
            for b in range(B):
                act.wait_ge(down_done, b + 1)
                act.wait_ge(in_p32, 16)
                act.activation(ad_h[:, b * S:(b + 1) * S], bank[b][0:A, :], ACT.Gelu, bias=W32["down_b"]
                               ).then_inc(gelu_ready, 1)

            def root(n):
                act.wait_ge(var_ready, n + 1)
                b = n % 2
                act.activation(rstd[:, 4 * b:4 * b + 4], rstd[:, 4 * b:4 * b + 4], ACT.Sqrt).then_inc(sqrt_done, 1)

            for b in range(B):
                root(b)
            for b in range(B):
                root(2 + b)
            for b in range(B):
                act.wait_ge(turned, b + 1)
                act.wait_ge(ada_ready, 1)
                act.activation(xt[:, b * S:(b + 1) * S], bank[b][:, :], ACT.Identity, bias=ada[:, 2 + b:3 + b],
                               scale=ada[:, b:b + 1]).then_inc(xt_ready, 1)
            for n in range(4):
                parts = (parts_q, parts_k)[n % 2]
                act.wait_ge(qk_float, n + 1)
                act.activation(parts[:, n // 2, 0, :], qk_f[:, 2 * n, 0:S], ACT.Copy).then_inc(part_hi, 1)
                act.wait_ge(rest_ready, n + 1)
                act.activation(parts[:, n // 2, 1, :], qk_f[:, 2 * n + 1, 0:S], ACT.Copy).then_inc(part_mid, 1)

            def exps(it):
                for v in range(8):
                    par, qt = v // QT, v % QT
                    if qt == 0:
                        wait(act, pv_done, it * 8 + (4 * (par + 1) - 8))
                        if isinstance(it, int) and it == 0 and par == 0:
                            act.wait_ge(v_ready, 2)
                            act.wait_ge(pad_ready, 3)
                        if isinstance(it, int) and it == 0 and par == 1:
                            act.wait_ge(stacks_out[1], 16 * 2 * PARTS * PARTS)
                        act.activation(v_st[:, par, :, :, 0:VW].rearrange("p k h c -> p (k h) c"),
                                       v_all[:, it * 2 + par, :, :, :].rearrange("p k h c -> p (k h) c"),
                                       ACT.Copy).then_inc(v_staged, 1)
                    for j in range(HG):
                        act.wait_ge(tr_done, it * 32 + (4 * v + j + 1))
                        act.activation(probs[:, par, j, :, qt * P:(qt + 1) * P],
                                       turned_ps[j % 2][:, :].rearrange("p (k q) -> p k q", k=QT),
                                       ACT.Exp, scale=-1.0).then_inc(exp_done, 1)
                    if qt == 0 and not (isinstance(it, int) and it == 0):
                        copy_ctx(it * 2 + (par - 2), par)

            def copy_ctx(group, par):
                act.wait_ge(pv_done, group * 4 + 4)
                act.activation(ctx_t[:, group, :], ctx_ps[par][:, :], ACT.Copy).then_inc(ctx_copied, 1)

            exps(0)
            for it in range(1, NG // 2):
                exps(it)
            copy_ctx(NG - 2, 0)
            copy_ctx(NG - 1, 1)

            for t in range(NT):
                act.wait_ge(ctx_back, t + 1)
                act.activation(ctx_nt[:, t * P:(t + 1) * P], bank[2 + t % 2][:, 0:P], ACT.Copy
                               ).then_inc(ctx_back_copied, 1)
            for b in range(B):
                root(4 + b)
            for b in range(B):
                act.wait_ge(turned, 3 + b)
                act.activation(h_t[:, b * S:(b + 1) * S], bank[4 + b][:, :], ACT.Identity, bias=L["beta2"],
                               scale=L["g2"]).then_inc(xt_ready, 1)
            for b in range(B):
                for f in range(FT):
                    n = b * FT + f
                    act.wait_ge(ff1_done, n + 1)
                    act.activation(ff_g[:, f, b * S:(b + 1) * S], bank[n % 4][:, :], ACT.Sigmoid,
                                   bias=b1_sig[:, f:f + 1], scale=1.702).then_inc(ff_gate, 1)
            for b in range(B):
                root(6 + b)
            for b in range(B):
                act.wait_ge(turned, 5 + b)
                act.activation(h_t[:, b * S:(b + 1) * S], bank[2 + b][:, :], ACT.Identity, bias=L["ln_b"],
                               scale=L["ln_g"]).then_inc(xt_ready, 1)
            act.wait_ge(t_var_ready, 1)
            act.activation(t_coef[:, 0, :], t_coef[:, 0, :], ACT.Sqrt).then_inc(t_sqrt_done, 1)
            act.wait_ge(softplus_in, 1)
            act.activation(soft_e, soft_a, ACT.Exp, scale=-1.0).then_inc(softplus_done, 1)
            act.wait_ge(softplus_done, 1)
            act.activation(soft_l, soft_e, ACT.Ln, bias=1.0).then_inc(softplus_done, 1)
            act.wait_ge(logit_max, 1)
            act.activation(route[:, 1, :, :], route[:, 0, :, :], ACT.Exp).then_inc(logit_exp, 1)

            def hidden(it):
                for slot in range(2):
                    for f in range(FT):
                        for b in range(B):
                            n = (slot * FT + f) * B + b
                            act.wait_ge(up_e_done, it * 16 + (n + 1))
                            wait(act, down_e_done, it * (2 * B) + (slot - 1) * B)
                            act.activation(hid_e[:, slot, f, b * S:(b + 1) * S], bank[n % 4][:, :], ACT.Relu,
                                           bias=L["exp_b1"][:, bass.ds(it * (2 * FT) + (slot * FT + f), 1)]
                                           ).then_inc(hid_ready, 1)

            hidden(0)
            for it in range(1, NE // 2):
                hidden(it)

        @block.tensor
        def _(pe):
            def turn(b, dest):
                for t in range(QT):
                    last = pe.transpose(dest[:, t * P:(t + 1) * P], zn[:, QT * b + t, :], ident)
                last.then_inc(turned, 1)

            pe.wait_ge(in_xt, 16)
            pe.wait_ge(in_early, 16)
            for b in range(B):
                pe.matmul(bank[b][0:A, :], C["down"], xt[:, b * S:(b + 1) * S], start=True, stop=True
                          ).then_inc(down_done, 1)
            pe.wait_ge(in_late, 16)
            pe.wait_ge(silu_ready, 1)
            for i in range(2):
                last = pe.matmul(bank[6][:, 2 * i:2 * i + 2], L["w_ada"][:, i * D:(i + 1) * D], silu,
                                 start=True, stop=True)
            last.then_inc(ada_done, 1)
            pe.wait_ge(sel_ready, 1)
            for b in range(B):
                pe.wait_ge(gelu_ready, b + 1)
                pe.matmul(bank[2 + b][0:A, :], sel_w[:, b, :], ad_h[:, b * S:(b + 1) * S], start=True, stop=True
                          ).then_inc(expert_done, 1)
            pe.wait_ge(in_up, 16)
            for b in range(B):
                pe.wait_ge(expert_ready, b + 1)
                for t in range(QT):
                    at = (QT * b + t) * P
                    last = pe.matmul(bank[4 + b][:, t * P:(t + 1) * P], ad_e[:, at:at + P], up[:, :],
                                     start=True, stop=True)
                last.then_inc(up_done, 1)
            for b in range(B):
                pe.wait_ge(norm_ready, B + b + 1)
                turn(b, bank[b])
            for b in range(B):
                pe.wait_ge(xt_ready, b + 1)
                half = xt[:, b * S:(b + 1) * S]
                for i, w in enumerate(("wq", "wk")):
                    pe.matmul(bank[2 + 2 * b + i][:, :], L[w], half, start=True, stop=True).then_inc(qk_proj, 1)
            pe.wait_ge(ada_ready, 1)
            for b in range(B):
                for t in range(QT):
                    at = (QT * b + t) * P
                    last = pe.matmul(bank[6 + b][:, t * P:(t + 1) * P], xt[:, at:at + P], L["wv"],
                                     start=True, stop=True)
                last.then_inc(v_proj, 1)
            pe.wait_ge(in_p32, 16)
            pe.wait_ge(in_p64, 16)
            steps = ((SE, W32["subj"], style_hot[0:SUBJ, :]), (P, W64["hyp_w1"], seT), (P, L["hyp_w2"], hid1),
                     (SE, L["sty_w1"], hid2))
            for i, (m, w, x) in enumerate(steps):
                pe.wait_ge(hyp_in, i + 1)
                pe.matmul(bank[0][0:m, 2 * i:2 * i + 2], w, x, start=True, stop=True).then_inc(hyp_mm, 1)
            pe.wait_ge(hyp_in, 5)
            for i in range(2):
                last = pe.matmul(bank[0][:, 8 + 2 * i:10 + 2 * i], W64["sty_w2"][:, i * D:(i + 1) * D], hid3,
                                 start=True, stop=True)
            last.then_inc(hyp_mm, 1)
            pe.wait_ge(hyp_in, 6)
            pe.wait_ge(v_ready, 2)
            pe.wait_ge(qk_float, 4)
            pe.wait_ge(mask_ready, 1)
            pe.wait_ge(pad_ready, 3)

            def turn_scores(j, slot, n):
                pe.wait_ge(shift_done, n + 1)
                wait(pe, exp_done, n - 1)
                for k in range(QT):
                    last = pe.transpose(turned_ps[j % 2][:, k * P:(k + 1) * P],
                                        ring[:, slot, j, k * P:(k + 1) * P], ident)
                last.then_inc(tr_done, 1)

            def values(par, k, group):
                if k == 0:
                    pe.wait_ge(exp_done, group * 16 + 16)
                    pe.wait_ge(v_staged, group + 1)
                    wait(pe, ctx_copied, group - 1)
                for j in range(HG):
                    last = pe.matmul(ctx_ps[par][32 * j:32 * j + 32, :], v_st[:, par, k, j, :],
                                     probs[:, par, j, k, :], start=(k == 0), stop=(k == QT - 1))
                last.then_inc(pv_done, 1)

            def attend(it):
                first = isinstance(it, int) and it == 0
                for v in range(8):
                    par, qt = v // QT, v % QT
                    if qt == 0:
                        pe.wait_ge(stack_in[par], it * (16 * 2 * HG) + 16 * 2 * HG)
                    for j in range(HG):
                        n = 4 * v + j
                        wait(pe, sum_done, it * 32 + (n - 3))
                        pe.matmul(score_ps[j][:, :], q_st[:, par, j, qt * P:(qt + 1) * P], k_st[:, par, j, :],
                                  start=True, stop=False)
                        pe.matmul(score_ps[j][:, :], diag_masked[:, :], mask_bf[:, it // 2, qt, :],
                                  start=False, stop=True).then_inc(qk_done, 1)
                        if not (first and v == 0):
                            turn_scores(j, (v - 1) % 8, it * 32 + (n - 4))
                    if not (first and v < 5):
                        values(((v - 5) // QT) % 2, (v - 5) % QT, it * 2 + (v - 5) // QT)

            attend(0)
            for it in range(1, NG // 2):
                attend(it)
            for j in range(HG):
                turn_scores(j, 7, 124 + j)
            values(0, 3, NG - 2)
            for k in range(QT):
                values(1, k, NG - 1)

            pe.wait_ge(ctx_copied, NG)

            def turn_ctx(t):
                wait(pe, ctx_scaled, t - 1)
                for g in range(NH // HG):
                    last = pe.transpose(bank[t % 2][:, g * P:(g + 1) * P],
                                        ctx_t[:, (t // QT) * (NH // HG) + g, (t % QT) * P:(t % QT + 1) * P], ident)
                last.then_inc(ctx_turned, 1)

            def turn_back(t):
                pe.wait_ge(ctx_scaled, t + 1)
                wait(pe, ctx_back_copied, t - 1)
                pe.transpose(bank[2 + t % 2][:, 0:P], ctx_n[:, t, :], ident).then_inc(ctx_back, 1)

            def project(t):
                pe.wait_ge(ctx_back_copied, t + 1)
                dest = bank[4 + t // QT][:, (t % QT) * P:(t % QT + 1) * P]
                pe.matmul(dest, xt[:, t * P:(t + 1) * P], ident, start=True, stop=False)
                pe.matmul(dest, ctx_nt[:, t * P:(t + 1) * P], L["wo"], start=False, stop=True).then_inc(wo_done, 1)

            for t in range(NT + 2):
                if t < NT:
                    turn_ctx(t)
                if 1 <= t <= NT:
                    turn_back(t - 1)
                if t >= 2:
                    project(t - 2)

            for b in range(B):
                pe.wait_ge(norm_ready, 2 * B + b + 1)
                turn(b, bank[4 + b])
            for b in range(B):
                pe.wait_ge(xt_ready, B + b + 1)
                for f in range(FT):
                    n = b * FT + f
                    if n < 4:
                        pe.wait_ge(ctx_back_copied, NT)
                    wait(pe, ff_ready, n - 3)
                    pe.matmul(bank[n % 4][:, :], L["w1"][:, f * P:(f + 1) * P], h_t[:, b * S:(b + 1) * S],
                              start=True, stop=True).then_inc(ff1_done, 1)
            for b in range(B):
                pe.wait_ge(ff_ready, FT * (b + 1))
                for t in range(QT):
                    at = (QT * b + t) * P
                    for f in range(FT):
                        last = pe.matmul(bank[6 + b][:, t * P:(t + 1) * P], ff_a[:, f, at:at + P],
                                         L["w2"][:, f * P:(f + 1) * P], start=(f == 0), stop=(f == FT - 1))
                last.then_inc(ff2_done, 1)

            for b in range(B):
                pe.wait_ge(norm_ready, 3 * B + b + 1)
                turn(b, bank[2 + b])
            pe.wait_ge(route_in, 2)
            for t in range(NT):
                last = pe.matmul(bank[6][:, t * NE:(t + 1) * NE], h3_t[:, t * P:(t + 1) * P], L["router"],
                                 start=True, stop=True)
            last.then_inc(logits_done, 1)

            def layer1(it, slot):
                pe.wait_ge(experts_in[slot], it * 32 + 32)
                for f in range(FT):
                    for b in range(B):
                        n = (slot * FT + f) * B + b
                        wait(pe, hid_ready, it * 16 + (n - 3))
                        pe.matmul(bank[n % 4][:, :], w1_e[:, slot, f * P:(f + 1) * P],
                                  h3_t[:, b * S:(b + 1) * S], start=True, stop=True).then_inc(up_e_done, 1)

            def layer2(it, slot):
                for b in range(B):
                    pe.wait_ge(hid_ready, it * 16 + ((slot * FT + FT - 1) * B + b + 1))
                    wait(pe, acc_done, it * 4 + (2 * slot + b - 1))
                    for t in range(QT):
                        at = (QT * b + t) * P
                        for f in range(FT):
                            last = pe.matmul(bank[4 + 2 * slot + b][:, t * P:(t + 1) * P],
                                             hid_e[:, slot, f, at:at + P], w2_e[:, slot, f, :],
                                             start=(f == 0), stop=(f == FT - 1))
                    last.then_inc(down_e_done, 1)

            layer1(0, 0)
            pe.wait_ge(comb_ready, 1)
            for t in range(NT):
                last = pe.transpose(bank[6 + t // QT][0:NE, (t % QT) * P:(t % QT + 1) * P],
                                    route[:, 11, t, :], ident)
            last.then_inc(comb_turned, 1)
            layer1(0, 1)
            pe.wait_ge(comb_t_ready, 1)
            pe.wait_ge(in_eb2, 16)
            for t in range(NT):
                last = pe.matmul(bank[6 + t // QT][:, (t % QT) * P:(t % QT + 1) * P],
                                 comb_t[:, t * P:(t + 1) * P], eb2[:, :], start=True, stop=True)
            last.then_inc(eb2_done, 1)
            layer2(0, 0)
            for it in range(1, NE // 2):
                layer1(it, 0)
                layer2(it - 1, 1)
                layer1(it, 1)
                layer2(it, 0)
            layer2(NE // 2 - 1, 1)

        @block.vector
        def _(dve):
            link = chained(dve, dve_step)

            dve.wait_ge(in_ids, 32)
            link(dve.tensor_copy(id_f, ids_i[:, :]))
            link(dve.tensor_copy(trig_x[:, 2:6], angles[:, :]))
            link(dve.tensor_scalar(trig_x[:, 0:2], id_f[:, 2:4], 0.01, 4000.0, ALU.mult, ALU.mult))
            dve.wait_ge(in_early, 16)
            link(dve.tensor_scalar(trig_x[:, 0:2], trig_x[:, 0:2], C["freq"], None, ALU.mult))
            link(dve.tensor_scalar(trig_k, trig_x, 1 / (2 * math.pi), ROUND, ALU.mult, ALU.add))
            link(dve.tensor_scalar(trig_k, trig_k, ROUND, None, ALU.subtract))
            for part in TWO_PI:
                link(dve.scalar_tensor_tensor(trig_x, trig_k, -part, trig_x, ALU.mult, ALU.add))
            link(dve.tensor_scalar(trig_x, trig_x, PI_BELOW, -PI_BELOW, ALU.min, ALU.max))
            link(dve.scalar_tensor_tensor(trig_k, trig_x, -1.0, trig_x, ALU.mult, ALU.min))
            link(dve.tensor_scalar(trig_k, trig_k, math.pi / 2, None, ALU.add))
            link(dve.tensor_copy(trig[0:SE, 0:2], trig_x[0:SE, 0:2]))
            link(dve.tensor_copy(trig[SE:P, 0:2], trig_k[SE:P, 0:2]))
            link(dve.tensor_copy(trig[:, 2:6], trig_x[:, 2:6]))
            dve.tensor_copy(trig[:, 6:10], trig_k[:, 2:6]).then_inc(trig_ready, 1)

            dve.wait_ge(in_p32, 16)

            link(dve.tensor_scalar(dom, id_f[:, 0:2], 0.0, float(E0 - 1), ALU.max, ALU.min))
            link(dve.tensor_tensor(valid, dom, id_f[:, 0:2], ALU.is_equal))
            for b in range(B):
                link(dve.tensor_scalar(hot[:, b, :], C["iota16"][0:A, :], dom[0:A, b:b + 1], None, ALU.is_equal))
                link(dve.tensor_tensor(sel_prod[:, b, :, :],
                                       W32["expert_w"].rearrange("a (o e) -> a o e", e=E0),
                                       hot[:, b:b + 1, :].to_broadcast([A, A, E0]), ALU.mult))
                link(dve.tensor_reduce(sel_w[:, b, :], sel_prod[:, b, :, :], AX_X, ALU.add))
                link(dve.tensor_tensor(sel_w[:, b, :], sel_w[:, b, :], W32["eye"], ALU.subtract))
                link(dve.scalar_tensor_tensor(sel_w[:, b, :], sel_w[:, b, :], valid[0:A, b:b + 1], W32["eye"],
                                              ALU.mult, ALU.add))
                link(dve.tensor_tensor(hot_prod[:, 2 * b, :], W32["expert_b"], hot[:, b, :], ALU.mult))
                link(dve.tensor_tensor(hot_prod[:, 2 * b + 1, :], W32["emb"], hot[:, b, :], ALU.mult))
                link(dve.tensor_reduce(emb_b[:, 2 * b:2 * b + 2], hot_prod[:, 2 * b:2 * b + 2, :], AX_X, ALU.add))
                link(dve.scalar_tensor_tensor(emb_b[:, 2 * b:2 * b + 1], emb_b[:, 2 * b:2 * b + 1],
                                              valid[0:A, b:b + 1], emb_b[:, 2 * b + 1:2 * b + 2],
                                              ALU.mult, ALU.add))
            dve.memset(ad_e[A:A + 1, :], 1.0).then_inc(sel_ready, 1)

            dve.wait_ge(silu_exp_done, 1)
            link(dve.tensor_scalar(silu, silu_e, 1.0, None, ALU.add))
            link(dve.reciprocal(silu, silu))
            dve.tensor_tensor(silu, silu, trig[:, 0:2], ALU.mult).then_inc(silu_ready, 1)

            dve.wait_ge(in_rows, 16)
            link(dve.tensor_scalar(neg_sin, trig[:, 2:6], -1.0, None, ALU.mult))

            def quads(ap):
                return ap.rearrange("p (i q e) -> p i q e", q=2, e=2)

            gamma, beta = quads(R["gamma"]), quads(R["beta"])
            for b in range(B):
                for q in range(2):
                    cos = trig[:, 6 + 2 * q + b:7 + 2 * q + b]
                    sines = trig[:, 2 + 2 * q + b:3 + 2 * q + b], neg_sin[:, 2 * q + b:2 * q + b + 1]
                    ra, rb, rc = (quads(r[:, b, :]) for r in (rot_a, rot_b, rot_c))
                    dve.tensor_scalar(ra[:, :, q, :], gamma[:, :, q, :], cos, None, ALU.mult)
                    link(dve.tensor_scalar(rc[:, :, q, :], beta[:, :, q, :], cos, None, ALU.mult))
                    for e in range(2):
                        dve.tensor_scalar(rb[:, :, q, e], gamma[:, :, q, 1 - e], sines[e], None, ALU.mult)
                        link(dve.scalar_tensor_tensor(rc[:, :, q, e], beta[:, :, q, 1 - e], sines[e],
                                                      rc[:, :, q, e], ALU.mult, ALU.add))
            dve.tensor_copy(small[:, 55:56], neg_sin[:, 0:1]).then_inc(trig_ready, 1)

            dve.wait_ge(ada_done, 1)
            link(dve.tensor_scalar(ada[:, 0:2], bank[6][:, 0:2], L["b_ada"][:, 0:1], 1.0, ALU.add, ALU.add))
            dve.tensor_scalar(ada[:, 2:4], bank[6][:, 2:4], L["b_ada"][:, 1:2], None, ALU.add
                              ).then_inc(ada_ready, 1)

            for b in range(B):
                dve.wait_ge(expert_done, b + 1)
                dve.tensor_scalar(ad_e[0:A, b * S:(b + 1) * S], bank[2 + b][0:A, :], emb_b[:, 2 * b:2 * b + 1],
                                  None, ALU.add).then_inc(expert_ready, 1)

            def moments_of(n):
                b = n % B
                half = slice(QT * b, QT * b + QT)
                for t in range(QT * b, QT * b + QT):
                    last = dve.bn_stats(stats[:, t, :], xn[:, t, :])
                link(last)
                for t in range(QT * b, QT * b + QT):
                    last = dve.bn_aggr(moments[:, t, :], stats[:, t, :])
                link(last)
                dve.tensor_scalar(rstd[:, half], moments[:, half, 1], LN_EPS, None, ALU.add).then_inc(var_ready, 1)

            def normalise(n):
                b = n % B
                half = slice(QT * b, QT * b + QT)
                dve.wait_ge(sqrt_done, n + 1)
                link(dve.reciprocal(rstd[:, half], rstd[:, half]))
                for t in range(QT * b, QT * b + QT):
                    last = dve.tensor_scalar(zn[:, t, :], xn[:, t, :], moments[:, t, 0:1], rstd[:, t:t + 1],
                                             ALU.subtract, ALU.mult)
                last.then_inc(norm_ready, 1)

            dve.wait_ge(in_xn, 16)
            for b in range(B):
                half = xn[:, QT * b:QT * b + QT, :]
                dve.wait_ge(up_done, b + 1)
                link(dve.tensor_tensor(half, bank[4 + b][:, :].rearrange("p (t d) -> p t d", t=QT), half, ALU.add))
                moments_of(b)
            for b in range(B):
                normalise(b)
            for b in range(B):
                half = slice(QT * b, QT * b + QT)
                dve.wait_ge(norm_ready, b + 1)
                link(dve.tensor_tensor(xn[:, half, :], zn[:, half, :],
                                       rot_a[:, b:b + 1, :].to_broadcast([P, QT, D]), ALU.mult))
                link(dve.tensor_tensor(xn[:, half, :], xn[:, half, :],
                                       rot_c[:, b:b + 1, :].to_broadcast([P, QT, D]), ALU.add))
                dve.wait_ge(rot_done, b + 1)
                link(dve.tensor_tensor(xn[:, half, :], xn[:, half, :], swapped[:, half, :], ALU.add))
                moments_of(B + b)
            for b in range(B):
                normalise(B + b)

            for b in range(B):
                for i, (bias, scale) in enumerate(((L["bq"], 1 / math.sqrt(DH)), (L["bk"], 1.0))):
                    n = 2 * b + i
                    dve.wait_ge(qk_proj, n + 1)
                    dve.tensor_scalar(qk_f[:, 2 * n, :], bank[2 + n][:, :], bias, scale, ALU.add, ALU.mult
                                      ).then_inc(qk_float, 1)
                for i in range(2):
                    n = 2 * b + i
                    parts = (parts_q, parts_k)[i]
                    dve.wait_ge(part_hi, n + 1)
                    dve.tensor_tensor(qk_f[:, 2 * n + 1, :], qk_f[:, 2 * n, :], parts[:, b, 0, :], ALU.subtract
                                      ).then_inc(rest_ready, 1)
                for i in range(2):
                    n = 2 * b + i
                    parts = (parts_q, parts_k)[i]
                    dve.wait_ge(part_mid, n + 1)
                    dve.tensor_tensor(parts[:, b, 2, :], qk_f[:, 2 * n + 1, :], parts[:, b, 1, :], ALU.subtract
                                      ).then_inc(part_lo, 1)
            dve.wait_ge(pad_ready, 2)
            for b in range(B):
                dve.wait_ge(v_proj, b + 1)
                for k in range(QT):
                    last = dve.tensor_tensor(
                        v_all[:, (NH // HG) * b:(NH // HG) * (b + 1), k, :, 0:DH],
                        bank[6 + b][:, k * P:(k + 1) * P].rearrange("p (g h c) -> p g h c", g=NH // HG, h=HG),
                        R["bv"].rearrange("p (g h c) -> p g h c", g=NH // HG, h=HG), ALU.add)
                last.then_inc(v_ready, 1)

            link(dve.tensor_scalar(wrap, id_f[:, 4:6], 0.0, float(SUBJ), ALU.is_lt, ALU.mult))
            link(dve.tensor_tensor(style_cmp, id_f[:, 4:6], wrap, ALU.add))
            link(dve.tensor_scalar(style_cmp, style_cmp, 0.0, float(SUBJ - 1), ALU.max, ALU.min))
            dve.tensor_scalar(style_hot, style_cmp, C["row"], None, ALU.is_equal).then_inc(hyp_in, 1)
            ps = bank[0]
            dve.wait_ge(hyp_mm, 1)
            dve.tensor_copy(seT, ps[0:SE, 0:2]).then_inc(hyp_in, 1)
            dve.wait_ge(hyp_mm, 2)
            dve.tensor_scalar(hid1, ps[:, 2:4], L["hyp_b1"], 0.0, ALU.add, ALU.max).then_inc(hyp_in, 1)
            dve.wait_ge(hyp_mm, 3)
            dve.tensor_scalar(hid2, ps[:, 4:6], L["hyp_b2"], None, ALU.add).then_inc(hyp_in, 1)
            dve.wait_ge(hyp_mm, 4)
            dve.tensor_scalar(hid3, ps[0:SE, 6:8], W64["sty_b1"], 0.0, ALU.add, ALU.max).then_inc(hyp_in, 1)
            dve.wait_ge(hyp_mm, 5)
            link(dve.tensor_scalar(gam, ps[:, 8:10], L["sty_b2"][:, 0:1], None, ALU.add))
            dve.tensor_scalar(bet, ps[:, 10:12], L["sty_b2"][:, 1:2], None, ALU.add).then_inc(hyp_in, 1)
            dve.scalar_tensor_tensor(soft_a, gam, -1.0, gam, ALU.mult, ALU.max).then_inc(softplus_in, 1)
            link(dve.tensor_scalar(b1_sig[:, :], L["b1"], 1.702, None, ALU.mult))

            dve.wait_ge(mask_ready, 1)
            link(dve.tensor_reduce(all_masked[:, 0, :], mask_bf[:, :, :, :].rearrange("p b t k -> p (b t) k"),
                                   AX_X, ALU.min))
            link(dve.tensor_scalar(all_masked[:, 1, :], all_masked[:, 0, :], -1.0, 1.0, ALU.mult, ALU.add))
            link(dve.reciprocal(all_masked[:, 2, :], all_masked[:, 1, :]))
            link(dve.tensor_scalar(all_masked[:, 2, :], all_masked[:, 2, :], 0.0, None, ALU.mult))

            def add_bias(it):
                for v in range(8):
                    dve.wait_ge(bias_in[v], it * 16 + 16)
                    for j in range(HG):
                        n = 4 * v + j
                        dve.wait_ge(qk_done, it * 32 + (n + 1))
                        dve.tensor_tensor_reduce(ring[:, v, j, :], score_ps[j][:, :], ring[:, v, j, :], 1.0,
                                                 -3.0e38, ALU.add, ALU.max, row_max[:, n:n + 1]
                                                 ).then_inc(sum_done, 1)

            for it in range(0, NG // 2):
                add_bias(it)

            recip = route[:, 0:2, :, :].rearrange("p a t e -> p (a t e)")
            for t in range(NT):
                dve.wait_ge(ctx_turned, t + 1)
                turned_ctx = bank[t % 2][:, :].rearrange("p (h c) -> p h c", c=32)
                r = recip[:, NH * t:NH * t + NH]
                link(dve.reciprocal(r, turned_ctx[:, :, DH]))
                link(dve.tensor_scalar(r, r, all_masked[:, 2, t:t + 1], None, ALU.add))
                dve.tensor_tensor(ctx_n[:, t, :].rearrange("p (h c) -> p h c", c=DH), turned_ctx[:, :, 0:DH],
                                  r.unsqueeze(2).to_broadcast([P, NH, DH]), ALU.mult).then_inc(ctx_scaled, 1)
            for b in range(B):
                dve.wait_ge(wo_done, QT * (b + 1))
                half = slice(QT * b, QT * b + QT)
                bo = R["bo"].unsqueeze(1).to_broadcast([P, QT, D])
                link(dve.tensor_tensor(xn[:, half, :], bank[4 + b][:, :].rearrange("p (t d) -> p t d", t=QT), bo,
                                       ALU.add))
                moments_of(2 * B + b)
            for b in range(B):
                normalise(2 * B + b)
            for b in range(B):
                half = slice(QT * b, QT * b + QT)
                link(dve.tensor_tensor(xn[:, half, :], xn[:, half, :],
                                       R["b2"].unsqueeze(1).to_broadcast([P, QT, D]), ALU.add))
            for b in range(B):
                for f in range(FT):
                    n = b * FT + f
                    dve.wait_ge(ff_gate, n + 1)
                    dve.scalar_tensor_tensor(ff_a[:, f, b * S:(b + 1) * S], bank[n % 4][:, :],
                                             L["b1"][:, f:f + 1], ff_g[:, f, b * S:(b + 1) * S],
                                             ALU.add, ALU.mult).then_inc(ff_ready, 1)
            for b in range(B):
                half = xn[:, QT * b:QT * b + QT, :]
                dve.wait_ge(ff2_done, b + 1)
                link(dve.tensor_tensor(half, bank[6 + b][:, :].rearrange("p (t d) -> p t d", t=QT), half, ALU.add))
                moments_of(3 * B + b)
            for b in range(B):
                normalise(3 * B + b)

            for b in range(B):
                dve.wait_ge(xt_ready, 2 * B + b + 1)
                link(dve.bn_stats(t_stats[:, b, :], h_t[:, b * S:(b + 1) * S]))
                link(dve.bn_aggr(t_mom[:, b, :], t_stats[:, b, :]))
            dve.tensor_scalar(t_coef[:, 0, :], t_mom[:, :, 1], 1e-8, None, ALU.add).then_inc(t_var_ready, 1)
            dve.wait_ge(t_sqrt_done, 1)
            link(dve.reciprocal(t_coef[:, 1, :], t_coef[:, 0, :]))
            dve.wait_ge(softplus_done, 2)
            link(dve.tensor_scalar(gam, gam, 0.0, 1e-8, ALU.max, ALU.add))
            link(dve.tensor_tensor(gam, gam, soft_l, ALU.add))
            link(dve.tensor_tensor(t_coef[:, 1, :], t_coef[:, 1, :], gam, ALU.mult))
            link(dve.tensor_tensor(t_coef[:, 2, :], t_coef[:, 1, :], t_mom[:, :, 0], ALU.mult))
            link(dve.tensor_tensor(t_coef[:, 2, :], bet, t_coef[:, 2, :], ALU.subtract))
            for b in range(B):
                dve.tensor_scalar(h3_t[:, b * S:(b + 1) * S], h_t[:, b * S:(b + 1) * S], t_coef[:, 1, b:b + 1],
                                  t_coef[:, 2, b:b + 1], ALU.mult, ALU.add).then_inc(route_in, 1)

            def rt(i):
                return route[:, i, :, :]

            def per_token(ap):
                return ap.unsqueeze(2).to_broadcast([P, NT, NE])

            token = sb_token
            dve.wait_ge(logits_done, 1)
            logits = bank[6][:, 0:NT * NE].rearrange("p (t e) -> p t e", e=NE)
            link(dve.tensor_reduce(token[:, 0, :], logits, AX_X, ALU.max))
            dve.tensor_tensor(rt(0), logits, per_token(token[:, 0, :]), ALU.subtract).then_inc(logit_max, 1)
            dve.wait_ge(logit_exp, 1)
            link(dve.tensor_reduce(token[:, 1, :], rt(1), AX_X, ALU.add))
            link(dve.reciprocal(token[:, 1, :], token[:, 1, :]))
            link(dve.tensor_tensor(rt(2), rt(1), per_token(token[:, 1, :]), ALU.mult))
            order = C["iota16"][:, 0:NE].unsqueeze(1).to_broadcast([P, NT, NE])
            left = rt(2)
            for i in range(2):
                top, first = token[:, 2 + i, :], token[:, 4 + i, :]
                equal, key, hot_e = rt(3 + 4 * i), rt(4 + 4 * i), rt(5 + 4 * i)
                link(dve.tensor_reduce(top, left, AX_X, ALU.max))
                link(dve.tensor_tensor(equal, left, per_token(top), ALU.is_equal))
                link(dve.scalar_tensor_tensor(key, equal, 100.0, order, ALU.mult, ALU.subtract))
                link(dve.tensor_reduce(first, key, AX_X, ALU.max))
                link(dve.tensor_tensor(hot_e, key, per_token(first), ALU.is_equal))
                if i == 0:
                    link(dve.scalar_tensor_tensor(rt(6), hot_e, -2.0, left, ALU.mult, ALU.add))
                    left = rt(6)
            link(dve.tensor_tensor(token[:, 6, :], token[:, 2, :], token[:, 3, :], ALU.add))
            link(dve.reciprocal(token[:, 6, :], token[:, 6, :]))
            link(dve.tensor_tensor(rt(10), rt(5), rt(9), ALU.add))
            link(dve.tensor_tensor(rt(10), rt(10), rt(2), ALU.mult))
            dve.tensor_tensor(rt(11), rt(10), per_token(token[:, 6, :]), ALU.mult).then_inc(comb_ready, 1)
            dve.wait_ge(comb_turned, 1)
            for b in range(B):
                last = dve.tensor_copy(comb_t[:, b * S:(b + 1) * S], bank[6 + b][0:NE, :])
            last.then_inc(comb_t_ready, 1)
            dve.wait_ge(eb2_done, 1)
            for b in range(B):
                half = slice(QT * b, QT * b + QT)
                dve.tensor_tensor(acc[:, half, :], bank[6 + b][:, :].rearrange("p (t d) -> p t d", t=QT),
                                  xn[:, half, :], ALU.add).then_inc(acc_done, 1)

            def add_expert(it, slot):
                for b in range(B):
                    dve.wait_ge(down_e_done, it * 4 + (2 * slot + b + 1))
                    dve.wait_ge(acc_done, it * 4 + (2 * slot + b + 1))
                    for t in range(QT * b, QT * b + QT):
                        gate = route[:, 11, t, :][:, bass.ds(it * 2 + slot, 1)]
                        last = dve.scalar_tensor_tensor(
                            acc[:, t, :], bank[4 + 2 * slot + b][:, (t % QT) * P:(t % QT + 1) * P], gate,
                            acc[:, t, :], ALU.mult, ALU.add)
                    last.then_inc(acc_done, 1)

            for it in range(0, NE // 2):
                for slot in range(2):
                    add_expert(it, slot)


def kernel(**inputs):
    import concourse.bacc as bacc
    from concourse.bass_utils import run_bass_kernel_spmd

    def arr(name):
        return np.ascontiguousarray(np.asarray(inputs[name]))

    def l0(name):
        return arr("L0_cond_" + name)

    def l2(name):
        return arr("L2_cond_" + name)

    def l3(name):
        return arr("L3_cond_" + name)

    def pack(columns, parts):
        out = [parts[name].reshape(parts[name].shape[0], -1) for name, _ in columns]
        assert [p.shape[1] for p in out] == [n for _, n in columns]
        return np.ascontiguousarray(np.concatenate(out, axis=1), dtype=np.float32)

    x = arr("x").reshape(TOK, D)
    f32 = np.float32
    half = D // 2
    freq = np.exp(np.arange(half, dtype=f32) * f32(-math.log(10000.0) / (half - 1)))
    early = pack(EARLY, {
        "ident": np.eye(P, dtype=f32), "freq": np.concatenate([freq, freq])[:, None],
        "iota16": np.tile(np.arange(E0, dtype=f32), (P, 1)), "row": np.arange(P, dtype=f32)[:, None],
        "down": l0("down_W").T})
    late = pack(LATE, {
        "w_ada": l2("W_ada"), "b_ada": l2("b_ada").reshape(2, D).T, "wq": l2("Wq"), "wk": l2("Wk"),
        "wv": l2("Wv"), "wo": l2("Wo"), "bq": l2("bq")[:, None], "bk": l2("bk")[:, None],
        "g2": l2("g2")[:, None], "beta2": l2("beta2")[:, None], "ln_g": l3("ln_g")[:, None],
        "ln_b": l3("ln_b")[:, None], "router": l3("router_w"), "hyp_w2": l3("hyp_w2"),
        "hyp_b1": l3("hyp_b1")[:, None], "hyp_b2": l3("hyp_b2")[:, None], "sty_w1": l3("sty_w1"),
        "sty_b2": l3("sty_b2").reshape(2, D).T, "b1": l2("b1").reshape(FT, P).T,
        "exp_b1": l3("exp_b1").reshape(NE * FT, P).T, "w1": l2("W1"),
        "w2": l2("W2").reshape(FT, P, D).transpose(1, 0, 2)})
    pack32 = pack(PACK32, {
        "expert_w": l0("expert_W").transpose(2, 1, 0), "expert_b": l0("expert_b").T,
        "emb": l0("domain_emb").T, "down_b": l0("down_b")[:, None], "subj": l3("subj_emb"),
        "eye": np.eye(A, dtype=f32)})
    pack64 = pack(PACK64, {"hyp_w1": l3("hyp_w1"), "sty_b1": l3("sty_b1")[:, None], "sty_w2": l3("sty_w2")})
    rows = np.concatenate([l0("ln_gamma"), l0("ln_beta"), l2("bv"), l2("bo"), l2("b2")])
    arrays = {
        "x_n": x, "x_t": np.ascontiguousarray(x.T), "early": early, "late": late, "pack32": pack32,
        "up": np.concatenate([l0("up_W").T, l0("up_b")[None, :]]), "pack64": pack64, "rows": rows,
        "ids": np.concatenate([arr("itok_B_0_15"), arr("itok_B_34_63"), arr("itok_B_6_14")]),
        "ang": np.concatenate([arr("condB_theta"), arr("condB_phi")]),
        "bias": arr("fside_Bx16xSxS_0").reshape(NG, HG, S, S),
        "mask": arr("mask_Bx1xSxS_bk0").reshape(B, S, S),
        "w1": l3("exp_w1"), "w2": l3("exp_w2"), "eb2": l3("exp_b2"),
    }
    nc = bacc.Bacc("TRN2", target_bir_lowering=False, num_devices=1)
    args = [nc.dram_tensor(f"in_{n}", a.shape, mybir.dt.from_np(a.dtype), kind="ExternalInput").ap()
            for n, a in arrays.items()]
    args.append(nc.dram_tensor("out", (B, S, D), F32, kind="ExternalOutput").ap())
    build(nc, *args)
    r = run_bass_kernel_spmd(nc, [{f"in_{n}": a for n, a in arrays.items()}], core_ids=[0])
    return r.results[0]["out"]
```

```python
import math
from contextlib import ExitStack

import numpy as np
import concourse.bass as bass
from concourse import mybir
from concourse.alu_op_type import AluOpType as ALU

F32 = mybir.dt.float32
BF16 = mybir.dt.bfloat16
I32 = mybir.dt.int32
U8 = mybir.dt.uint8
ACT = mybir.ActivationFunctionType
AX_X = mybir.AxisListType.X

P = 128
B, S, D = 2, 512, 128
TOK = B * S
NT = TOK // P
QT = S // P
A = 32
E0 = 16
NH, DH = 16, 8
HG = 4
NG = B * NH // HG
FF = 512
FT = FF // P
NE = 8
SUBJ, SE = 32, 64
VW = DH + 1
PARTS = 3
PRODUCTS = 8
UNITS = NG * QT
RING = 6
LAG = 5
LN_EPS = 1e-5
MASKED = -1e30
ROUND = 1.5 * 2.0 ** 23
TWO_PI = (6.28125, 0.00193500518798828125, 2 * math.pi - 6.28125 - 0.00193500518798828125)
PI_BELOW = 3.1415925

EARLY = (("ident", P), ("freq", 1), ("iota16", E0), ("row", 1), ("down", A))
LATE = (("w_ada", 2 * D), ("b_ada", 2), ("wq", D), ("wk", D), ("wv", D), ("wo", D), ("bq", 1), ("bk", 1),
        ("g2", 1), ("beta2", 1), ("ln_g", 1), ("ln_b", 1), ("router", NE), ("hyp_w2", D), ("hyp_b1", 1),
        ("hyp_b2", 1), ("sty_w1", D // 2), ("sty_b2", 2), ("b1", FT), ("exp_b1", NE * FT), ("w1", FF), ("w2", FF))
PACK32 = (("expert_w", E0 * A), ("expert_b", E0), ("emb", E0), ("down_b", 1), ("subj", SE), ("eye", A))
PACK64 = (("hyp_w1", D), ("sty_b1", 1), ("sty_w2", 2 * D))
ROWS = (("gamma", D), ("beta", D), ("bv", D), ("bo", D), ("b2", D))

(TURN_CTX0, TURN_CTX1, TURN_BACK, PROJECT, TURN_H, FF1_0, FF1_1, FF1_2, FF1_3, FF2, TURN_H3, ROUTE, TURN_GATES,
 GATED_BIAS) = STEPS = range(14)
FINISH_AT = (43, 45, 47, 49, 52, 54, 56, 58, 60, 62, 65, 67)
FINISH = {at: step for step, at in enumerate(FINISH_AT)}


def width(columns):
    return sum(n for _, n in columns)


def columns_of(tile, columns):
    out, at = {}, 0
    for name, n in columns:
        out[name] = tile[:, at:at + n]
        at += n
    return out


def build(nc, x_t, early_d, late_d, pack32_d, up_d, pack64_d, rows_d, ids_d, ang_d, bias_d, mask_d,
          w1_d, w2_d, eb2_d, out_d):
    with ExitStack() as ctx:
        def sb(name, shape, dt=F32):
            return ctx.enter_context(nc.sbuf_tensor(name, shape, dt))

        def sem(name):
            return ctx.enter_context(nc.semaphore(name))

        def sems(name, n=B):
            return [sem(f"{name}{i}") for i in range(n)]

        bank = [ctx.enter_context(nc.psum_tensor(f"bank{i}", [P, 512], F32)) for i in range(8)]
        score_ps, turned_ps, ctx_ps, aux_ps = bank[0:4], bank[4:6], bank[6], bank[7]

        q_dram = nc.dram_tensor("q_parts", (B, PRODUCTS, D, S), BF16).ap()
        k_dram = nc.dram_tensor("k_parts", (B, PRODUCTS, D, S), BF16).ap()

        early = sb("early", [P, width(EARLY)])
        late = sb("late", [P, width(LATE)])
        pack32 = sb("pack32", [A, width(PACK32)])
        pack64 = sb("pack64", [SE, width(PACK64)])
        rows = sb("rows", [P, width(ROWS)])
        up = sb("up", [A + 1, D])
        ids_i = sb("ids_i", [P, 6], I32)
        angles = sb("angles", [P, 4])
        eb2 = sb("eb2", [NE, D])
        C, L, W32, W64, R = (columns_of(early, EARLY), columns_of(late, LATE), columns_of(pack32, PACK32),
                             columns_of(pack64, PACK64), columns_of(rows, ROWS))
        ident = C["ident"]

        ring = sb("ring", [P, RING, HG, S])
        probs = sb("probs", [P, 2, HG, QT, S])
        q_st = sb("q_st", [P, NH // HG, 2, S], BF16)
        k_st = sb("k_st", [P, NH // HG, 2, S], BF16)
        v_all = sb("v_all", [P, NG, QT, HG, VW])
        v_st = sb("v_st", [P, 2, QT, HG, 32])
        mask = sb("mask", [P, NT, S], U8)
        mask_bf = sb("mask_bf", [P, QT, S], BF16)
        diag_masked = sb("diag_masked", [P, P], BF16)
        ctx_t = sb("ctx_t", [P, NH // HG, S])
        row_max = sb("row_max", [P, RING * HG])
        all_masked = sb("all_masked", [P, 3, NT])
        xt = sb("xt", [P, TOK])
        xn = sb("xn", [P, NT, D])
        zn = sb("zn", [P, NT, D])
        stats = sb("stats", [P, NT, 6])
        moments = sb("moments", [P, NT, 2])
        rstd = sb("rstd", [P, NT])
        minus_half = sb("minus_half", [P, QT])
        small = sb("small", [P, 64])
        ctx_r = sb("ctx_r", [P, 2, NH])
        ctx_n = sb("ctx_n", [P, QT, D])
        ctx_nt = sb("ctx_nt", [P, S])
        h_t = sb("h_t", [P, S])
        ff_g = sb("ff_g", [P, 2, S])
        ff_a = sb("ff_a", [P, FT, S])
        h3_t = sb("h3_t", [P, TOK])
        comb_t = ff_g[0:NE, :, :].rearrange("p a s -> p (a s)")
        route = sb("route", [P, 12, NT, NE])
        token = sb("token", [P, 8, NT])
        hot = sb("hot", [A, B, E0])
        hot_prod = sb("hot_prod", [A, 4, E0])
        style = sb("style", [P, 24])
        t_stats = sb("t_stats", [P, B, 6])
        t_mom = sb("t_mom", [P, B, 2])
        t_coef = sb("t_coef", [P, 4, B])
        b1_tanh = sb("b1_tanh", [P, FT])
        b1_half = sb("b1_half", [P, FT])

        flat = probs[:, :, :, :, :].rearrange("p a h k s -> p (a h k s)")
        qk_f = [flat[:, 8192 * b:8192 * b + 2048].rearrange("p (n c) -> p n c", n=4) for b in range(B)]
        parts = [flat[:, 8192 * b + 2048:8192 * b + 3584].bitcast(BF16)
                 .rearrange("p (i n s) -> p i n s", i=2, n=PARTS) for b in range(B)]
        sel_prod = flat[0:A, 4096:4096 + B * A * E0].rearrange("p (b o e) -> p b o e", b=B, o=A)
        sel_w = flat[0:A, 5120:5120 + B * A].rearrange("p (b o) -> p b o", b=B)
        ad_h = flat[0:A, 6144:6144 + TOK]
        ad_e = flat[0:A + 1, 12288:12288 + TOK]
        rot_a, rot_b, rot_c = (flat[:, 13312 + 256 * i:13568 + 256 * i].rearrange("p (b d) -> p b d", b=B)
                               for i in range(3))
        swapped = flat[:, 14336:14336 + NT * D].rearrange("p (t d) -> p t d", t=NT)
        w1_e = flat[:, 0:NE * FF].rearrange("p (e f) -> p e f", e=NE)
        w2_e = flat[:, NE * FF:2 * NE * FF].rearrange("p (e f d) -> p e f d", e=NE, f=FT)
        hid_e = ring[:, 0:4, :, :].rearrange("p (e u) h s -> p e (u h s)", e=2)[:, :, 0:FT * S].rearrange(
            "p e (f s) -> p e f s", f=FT)

        in_xt = sems("in_xt")
        in_early, in_ids, in_angles, in_p32, in_up, in_rows, in_late, in_p64, in_mask, in_eb2 = (
            sem(n) for n in ("in_early", "in_ids", "in_angles", "in_p32", "in_up", "in_rows", "in_late", "in_p64",
                             "in_mask", "in_eb2"))
        bias_in = sems("bias_in", RING)
        experts_in = sems("experts_in", NE)
        stacks_out = sems("stacks_out")
        stack_in = sems("stack_in", NH // HG)
        dve_step, pool_step = sem("dve_step"), sem("pool_step")
        (ids_ready, trig_ready, sin_done, silu_exp_done, silu_ready, ada_done, ada_ready, sel_ready, down_done,
         gelu_ready, expert_done, expert_ready, up_done, ones_ready, rot_ready, swap_done) = (
            sem(n) for n in ("ids_ready", "trig_ready", "sin_done", "silu_exp_done", "silu_ready", "ada_done",
                             "ada_ready", "sel_ready", "down_done", "gelu_ready", "expert_done", "expert_ready",
                             "up_done", "ones_ready", "rot_ready", "swap_done"))
        var_ready, rstd_ready, norm_ready = sems("var_ready"), sems("rstd_ready"), sems("norm_ready")
        turned, affine_done = sems("turned"), sems("affine_done")
        qk_proj, qk_float, part_hi, rest_ready, part_mid, part_lo, v_proj, v_ready, v_pad, primed = (
            sem(n) for n in ("qk_proj", "qk_float", "part_hi", "rest_ready", "part_mid", "part_lo", "v_proj",
                             "v_ready", "v_pad", "primed"))
        seeded = sems("seeded", HG)
        (qk_done, sum_done, shift_done, tr_done, exp_done, v_staged, pv_done, ctx_copied, mask_bf_ready) = (
            sem(n) for n in ("qk_done", "sum_done", "shift_done", "tr_done", "exp_done", "v_staged", "pv_done",
                             "ctx_copied", "mask_bf_ready"))
        hyp_in, hyp_mm, abs_ready, softplus_exp, softplus_done, gam_ready = (
            sem(n) for n in ("hyp_in", "hyp_mm", "abs_ready", "softplus_exp", "softplus_done", "gam_ready"))
        (ctx_turned, ctx_scaled, ctx_back, ctx_back_copied, wo_done, ff1_done, ff_half, ff_ready,
         ff2_done, t_var, t_rstd, route_in, logits_done, logit_max, logit_exp, comb_ready, comb_turned, comb_t_ready,
         eb2_done, base_added) = (
            sems(n) for n in ("ctx_turned", "ctx_scaled", "ctx_back", "ctx_back_copied", "wo_done", "ff1_done",
                              "ff_half", "ff_ready", "ff2_done", "t_var", "t_rstd", "route_in",
                              "logits_done", "logit_max", "logit_exp", "comb_ready", "comb_turned", "comb_t_ready",
                              "eb2_done", "base_added"))
        up_e_done, hid_ready, down_e_done, acc_done, out_written = (
            sem(n) for n in ("up_e_done", "hid_ready", "down_e_done", "acc_done", "out_written"))

        block = ctx.enter_context(nc.Block())

        def wait(eng, semaphore, value):
            if value > 0:
                eng.wait_ge(semaphore, value)

        def chained(eng, semaphore):
            count = [0]

            def link(instruction):
                count[0] += 1
                instruction.then_inc(semaphore, 1)
                eng.wait_ge(semaphore, count[0])

            return link

        def half(b):
            return slice(QT * b, QT * b + QT)

        def tokens(b):
            return slice(S * b, S * b + S)

        def seeded_by_vector(unit, j):
            if j == 2:
                return unit % 2 == 1 if unit < UNITS // B else 2 * unit >= FINISH_AT[TURN_H]
            return j == 0

        def seeded_by_tensor(unit, j):
            return j == 3 and unit >= UNITS // B

        id_f, dom, wrap, style_hot, style_cmp = (small[:, 0:6], small[:, 6:8], small[:, 8:10], small[:, 10:12],
                                                 small[:, 12:14])
        valid, ada, trig_x, trig_k = small[:, 14:16], small[:, 16:20], small[:, 20:26], small[:, 26:32]
        trig, neg_sin = small[:, 32:42], small[:, 42:46]
        silu_e, silu = small[:, 46:48], small[:, 48:50]
        emb_b = small[0:A, 50:54]
        seT, hid1, hid2, hid3 = style[0:SE, 0:2], style[:, 2:4], style[:, 4:6], style[0:SE, 6:8]
        gam, bet, soft_a, soft_e, soft_l = (style[:, 8:10], style[:, 10:12], style[:, 12:14], style[:, 14:16],
                                            style[:, 16:18])

        @block.sync
        def _(sp):
            sp.dma_start(early[:, :], early_d).then_inc(in_early, 16)
            for b in range(B):
                sp.dma_start(xt[:, tokens(b)], x_t[:, tokens(b)]).then_inc(in_xt[b], 16)
            sp.dma_start(up[:, :], up_d).then_inc(in_up, 16)
            sp.dma_start(rows[:, :], rows_d.partition_broadcast(P)).then_inc(in_rows, 16)
            sp.dma_start(late[:, :], late_d).then_inc(in_late, 16)
            sp.dma_start(pack64[:, :], pack64_d).then_inc(in_p64, 16)
            sp.dma_start(mask[:, :, :].rearrange("p (b t) k -> p b t k", b=B),
                         mask_d.rearrange("b (t p) k -> p b t k", p=P)).then_inc(in_mask, 16)

            def load_bias(unit):
                group, tile, slot = unit // QT, unit % QT, unit % RING
                sp.dma_start(ring[:, slot, :, :],
                             bias_d[group, :, tile * P:(tile + 1) * P, :].rearrange("h p k -> p h k")
                             ).then_inc(bias_in[slot], 16)

            def write_parts(b):
                for level, arrived in enumerate((part_hi, part_mid, part_lo)):
                    for kind, dram in enumerate((q_dram, k_dram)):
                        sp.wait_ge(arrived, 2 * b + kind + 1)
                        rows_of = (range(PARTS * level, min(PARTS * level + PARTS, PRODUCTS)) if kind == 0
                                   else range(level, PRODUCTS, PARTS))
                        dest = dram[b, rows_of.start:rows_of.stop:rows_of.step]
                        source = parts[b][:, kind, level:level + 1, :].to_broadcast([P, len(rows_of), S])
                        sp.dma_start(dest.rearrange("r d s -> d r s"), source).then_inc(stacks_out[b], 16)

            def load_stack(group):
                b, g = group // (NH // HG), group % (NH // HG)
                for stack, dram in ((q_st, q_dram), (k_st, k_dram)):
                    source = dram[b].rearrange("r (g h c t) s -> g h r c (t s)", g=NH // HG, h=2, c=DH)
                    for h in range(2):
                        sp.dma_start(stack[64 * h:64 * h + 64, g, :, :].rearrange("p t s -> p (t s)"),
                                     source[g, h]).then_inc(stack_in[g], 16)

            for u in range(RING):
                load_bias(u)
            sp.dma_start(eb2[:, :], eb2_d).then_inc(in_eb2, 16)
            write_parts(0)
            sp.wait_ge(stacks_out[0], 16 * 2 * PARTS)
            load_stack(0)
            load_stack(1)
            write_parts(1)
            load_stack(2)
            load_stack(3)
            sp.wait_ge(stacks_out[1], 16 * 2 * PARTS)
            for u in range(RING, UNITS):
                sp.wait_ge(tr_done, HG * (u - RING + 1))
                load_bias(u)
                group = (u + RING) // QT
                if (u + RING) % QT == 0 and NH // HG <= group < NG:
                    sp.wait_ge(qk_done, HG * QT * (group - NH // HG + 1))
                    load_stack(group)

            sp.wait_ge(pv_done, QT * (NG - 1))
            for e in range(NE):
                sp.dma_start(w1_e[:, e, :], w1_d[e]).then_inc(experts_in[e], 16)
                sp.dma_start(w2_e[:, e, :, :], w2_d[e].rearrange("(f p) d -> p f d", p=P)
                             ).then_inc(experts_in[e], 16)

            for b in range(B):
                sp.wait_ge(acc_done, NE * (b + 1))
                sp.dma_start(out_d[b].rearrange("(t p) d -> p t d", p=P), xn[:, half(b), :]).then_inc(out_written, 16)
            sp.wait_ge(out_written, 32)

        @block.gpsimd
        def _(pool):
            link = chained(pool, pool_step)
            link(pool.memset(minus_half[:, :], -0.5))
            pool.memset(ad_e[A:A + 1, :], 1.0).then_inc(ones_ready, 1)
            pool.wait_ge(ones_ready, 1)

            pool.wait_ge(ids_ready, 1)
            pool.wait_ge(in_early, 16)
            link(pool.tensor_scalar(trig_x[:, 0:2], trig_x[:, 0:2], C["freq"], 0.0, ALU.mult, ALU.add))
            link(pool.tensor_scalar(trig_k, trig_x, 1 / (2 * math.pi), ROUND, ALU.mult, ALU.add))
            link(pool.tensor_scalar(trig_k, trig_k, ROUND, 0.0, ALU.subtract, ALU.add))
            for part in TWO_PI:
                link(pool.tensor_scalar(trig[:, 0:6], trig_k, -part, 0.0, ALU.mult, ALU.add))
                link(pool.tensor_tensor(trig_x, trig_x, trig[:, 0:6], ALU.add))
            link(pool.tensor_scalar(trig_x, trig_x, PI_BELOW, -PI_BELOW, ALU.min, ALU.max))
            link(pool.tensor_scalar(trig_k, trig_x, 0.0, 2.0, ALU.max, ALU.mult))
            link(pool.tensor_tensor(trig_k, trig_x, trig_k, ALU.subtract))
            link(pool.tensor_scalar(trig_k, trig_k, math.pi / 2, 0.0, ALU.add, ALU.add))
            link(pool.tensor_copy(trig[0:SE, 0:2], trig_x[0:SE, 0:2]))
            link(pool.tensor_copy(trig[SE:P, 0:2], trig_k[SE:P, 0:2]))
            pool.tensor_copy(trig[:, 2:6], trig_x[:, 2:6])
            pool.tensor_copy(trig[:, 6:10], trig_k[:, 2:6]).then_inc(trig_ready, 1)

            pool.wait_ge(in_rows, 16)
            pool.wait_ge(sin_done, 1)
            link(pool.tensor_scalar(neg_sin, trig[:, 2:6], -1.0, 0.0, ALU.mult, ALU.add))

            def quads(ap):
                return ap.rearrange("p (i q e) -> p i q e", q=2, e=2)

            gamma, beta = quads(R["gamma"]), quads(R["beta"])

            def rotation(b):
                ra, rb, rc = (quads(r[:, b, :]) for r in (rot_a, rot_b, rot_c))
                for q in range(2):
                    cos = trig[:, 6 + 2 * q + b:7 + 2 * q + b]
                    sines = trig[:, 2 + 2 * q + b:3 + 2 * q + b], neg_sin[:, 2 * q + b:2 * q + b + 1]
                    pool.tensor_scalar(ra[:, :, q, :], gamma[:, :, q, :], cos, 0.0, ALU.mult, ALU.add)
                    for e in range(2):
                        pool.tensor_scalar(rb[:, :, q, e], gamma[:, :, q, 1 - e], sines[e], 0.0, ALU.mult, ALU.add)
                        last = pool.tensor_scalar(quads(swapped[:, QT * b, :])[:, :, q, e], beta[:, :, q, 1 - e],
                                                  sines[e], 0.0, ALU.mult, ALU.add)
                    last = pool.tensor_scalar(rc[:, :, q, :], beta[:, :, q, :], cos, 0.0, ALU.mult, ALU.add)
                link(last)
                link(pool.tensor_tensor(rot_c[:, b, :], rot_c[:, b, :], swapped[:, QT * b, :], ALU.add))
                pool.tensor_copy(small[:, 55:56], minus_half[:, 0:1]).then_inc(rot_ready, 1)

            def inverse_root(b, n):
                pool.wait_ge(var_ready[b], n + 1)
                pool.tensor_tensor(rstd[:, half(b)], rstd[:, half(b)], minus_half[:, :], ALU.pow
                                   ).then_inc(rstd_ready[b], 1)

            def swap(b):
                pool.wait_ge(norm_ready[b], 1)
                z = zn[:, half(b), :].rearrange("p t (i e) -> p t i e", e=2)
                o = swapped[:, half(b), :].rearrange("p t (i e) -> p t i e", e=2)
                w = rot_b[:, b:b + 1, :].to_broadcast([P, QT, D]).rearrange("p t (i e) -> p t i e", e=2)
                for e in range(2):
                    last = pool.tensor_tensor(o[:, :, :, e], z[:, :, :, 1 - e], w[:, :, :, e], ALU.mult)
                last.then_inc(swap_done, 1)

            rotation(0)
            swap(0)
            rotation(1)
            swap(1)
            pool.memset(v_st[:, :, :, :, :], 0.0).then_inc(v_pad, 1)
            pool.memset(v_all[:, :, :, :, :], 1.0).then_inc(v_pad, 1)
            pool.wait_ge(in_mask, 16)
            pool.tensor_scalar(diag_masked[:, :], ident, MASKED, 0.0, ALU.mult, ALU.add)
            pool.tensor_copy(mask_bf[:, :, :], mask[:, half(1), :]).then_inc(mask_bf_ready, 1)

            def shift(unit, j):
                slot, n = unit % RING, (unit % RING) * HG + j
                pool.wait_ge(sum_done, HG * unit + j + 1)
                pool.tensor_scalar(ring[:, slot, j, :], ring[:, slot, j, :], -1.0, row_max[:, n:n + 1],
                                   ALU.mult, ALU.add).then_inc(shift_done, 1)

            def finish(b, step):
                if step in (PROJECT, FF2):
                    inverse_root(b, 2 if step == PROJECT else 3)
                if step == TURN_H3:
                    pool.wait_ge(t_var[b], 1)
                    pool.tensor_tensor(t_coef[:, 0, b:b + 1], t_coef[:, 0, b:b + 1], minus_half[:, 0:1], ALU.pow
                                       ).then_inc(t_rstd[b], 1)

            for s in range(UNITS + LAG):
                for j in range(HG):
                    if s < UNITS:
                        shift(s, j)
                    if j % 2 and 2 * s + j // 2 - 1 in FINISH:
                        finish(0, FINISH[2 * s + j // 2 - 1])
            for step in STEPS:
                finish(1, step)

        @block.scalar
        def _(act):
            act.dma_start(ids_i[:, :], ids_d.partition_broadcast(P)).then_inc(in_ids, 16)
            act.dma_start(angles[:, :], ang_d.partition_broadcast(P)).then_inc(in_angles, 16)
            act.dma_start(pack32[:, :], pack32_d).then_inc(in_p32, 16)
            act.wait_ge(in_p32, 16)
            for b in range(B):
                act.wait_ge(down_done, b + 1)
                act.activation(ad_h[:, tokens(b)], bank[b][0:A, :], ACT.Gelu, bias=W32["down_b"]
                               ).then_inc(gelu_ready, 1)
            act.wait_ge(trig_ready, 1)
            act.activation(trig, trig, ACT.Sin).then_inc(sin_done, 1)
            act.wait_ge(sin_done, 1)
            act.activation(silu_e, trig[:, 0:2], ACT.Exp, scale=-1.0).then_inc(silu_exp_done, 1)

            def root(b, n):
                act.wait_ge(var_ready[b], n + 1)
                act.activation(rstd[:, half(b)], rstd[:, half(b)], ACT.Sqrt).then_inc(rstd_ready[b], 1)

            root(0, 0)
            act.wait_ge(in_late, 16)
            act.wait_ge(in_p64, 16)
            ps = bank[6]
            act.wait_ge(hyp_mm, 1)
            act.activation(seT, ps[0:SE, 0:2], ACT.Copy).then_inc(hyp_in, 1)
            act.wait_ge(hyp_mm, 2)
            act.activation(hid1, ps[:, 2:4], ACT.Relu, bias=L["hyp_b1"]).then_inc(hyp_in, 1)
            act.wait_ge(hyp_mm, 3)
            act.activation(hid2, ps[:, 4:6], ACT.Identity, bias=L["hyp_b2"]).then_inc(hyp_in, 1)
            act.wait_ge(hyp_mm, 4)
            act.activation(hid3, ps[0:SE, 6:8], ACT.Relu, bias=W64["sty_b1"]).then_inc(hyp_in, 1)
            act.wait_ge(hyp_mm, 5)
            act.activation(gam, ps[:, 8:10], ACT.Identity, bias=L["sty_b2"][:, 0:1])
            act.activation(bet, ps[:, 10:12], ACT.Identity, bias=L["sty_b2"][:, 1:2]).then_inc(hyp_in, 1)

            def affine(b):
                act.wait_ge(turned[b], 1)
                act.wait_ge(ada_ready, 1)
                act.activation(xt[:, tokens(b)], bank[(0, 4)[b]][:, :], ACT.Identity, bias=ada[:, 2 + b:3 + b],
                               scale=ada[:, b:b + 1]).then_inc(affine_done[b], 1)

            def split(b, level, arrived, done):
                for kind in range(2):
                    act.wait_ge(arrived, 2 * b + kind + 1)
                    act.activation(parts[b][:, kind, level, :], qk_f[b][:, 2 * kind + level, :], ACT.Copy
                                   ).then_inc(done, 1)

            root(0, 1)
            root(1, 0)
            affine(0)
            root(1, 1)
            split(0, 0, qk_float, part_hi)
            split(0, 1, rest_ready, part_mid)
            affine(1)
            split(1, 0, qk_float, part_hi)
            split(1, 1, rest_ready, part_mid)
            act.wait_ge(abs_ready, 1)
            act.activation(soft_e, soft_a, ACT.Exp, scale=-1.0).then_inc(softplus_exp, 1)
            act.wait_ge(softplus_exp, 1)
            act.activation(soft_l, soft_e, ACT.Ln, bias=1.0).then_inc(softplus_done, 1)

            def seed(unit, j):
                if unit == 0:
                    act.wait_ge(primed, 1)
                    act.wait_ge(in_mask, 16)
                else:
                    act.wait_ge(sum_done, HG * (unit - 1) + j + 1)
                act.activation(score_ps[j][:, :], mask[:, unit // (NG // B * QT) * QT + unit % QT, :], ACT.Copy,
                               scale=MASKED).then_inc(seeded[j], 1)

            def exp(unit, j):
                group, qt = unit // QT, unit % QT
                if qt == 0 and j == 0:
                    wait(act, pv_done, QT * (group - 1))
                if unit == QT and j == 0:
                    act.wait_ge(stacks_out[1], 16 * 2 * PARTS)
                act.wait_ge(tr_done, HG * unit + j + 1)
                act.activation(probs[:, group % 2, j, :, qt * P:(qt + 1) * P],
                               turned_ps[j % 2][:, :].rearrange("p (k q) -> p k q", k=QT),
                               ACT.Exp, scale=-1.0).then_inc(exp_done, 1)

            def copy_ctx(group):
                act.wait_ge(pv_done, QT * (group + 1))
                if group >= NG // B:
                    act.wait_ge(ctx_turned[0], 2)
                act.activation(ctx_t[:, group % (NG // B), :], ctx_ps[:, :], ACT.Copy).then_inc(ctx_copied, 1)

            def finish(b, step):
                if step == TURN_BACK:
                    act.wait_ge(ctx_back[b], 1)
                    wait(act, wo_done[0], b)
                    act.activation(ctx_nt[:, :], aux_ps[:, :], ACT.Copy).then_inc(ctx_back_copied[b], 1)
                if step in (TURN_H, TURN_H3):
                    scale, offset = (L["g2"], L["beta2"]) if step == TURN_H else (L["ln_g"], L["ln_b"])
                    act.wait_ge(turned[b], 2 if step == TURN_H else 3)
                    act.activation(h_t[:, :], aux_ps[:, :], ACT.Identity, bias=offset, scale=scale
                                   ).then_inc(affine_done[b], 1)
                if step in (FF1_0, FF1_1, FF1_2, FF1_3):
                    f = step - FF1_0
                    act.wait_ge(ff1_done[b], f + 1)
                    wait(act, ff_ready[b], f - 1)
                    act.activation(ff_g[:, f % 2, :], aux_ps[:, :], ACT.Tanh, bias=b1_tanh[:, f:f + 1], scale=0.851)
                    wait(act, ff2_done[0], b)
                    act.activation(ff_a[:, f, :], aux_ps[:, :], ACT.Identity, bias=b1_half[:, f:f + 1], scale=0.5
                                   ).then_inc(ff_half[b], 1)
                if step == ROUTE:
                    act.wait_ge(logit_max[b], 1)
                    act.activation(route[:, 1, half(b), :], route[:, 0, half(b), :], ACT.Exp).then_inc(logit_exp[b], 1)

            for j in range(HG):
                if not seeded_by_vector(0, j):
                    seed(0, j)
            for s in range(UNITS + LAG):
                if s % QT == 1 and s >= 2 * QT:
                    copy_ctx(s // QT - 2)
                for j in range(HG):
                    if 1 <= s <= UNITS:
                        exp(s - 1, j)
                    if s + 1 < UNITS and not seeded_by_vector(s + 1, j) and not seeded_by_tensor(s + 1, j):
                        seed(s + 1, j)
                    if j % 2 and 2 * s + j // 2 - 1 in FINISH:
                        finish(0, FINISH[2 * s + j // 2 - 1])
                if s % QT == 2 and s // QT < NG:
                    group = s // QT
                    wait(act, pv_done, QT * (group - 1))
                    act.wait_ge(v_ready, group // (NG // B) + 1)
                    act.wait_ge(v_pad, 1)
                    act.activation(v_st[:, group % 2, :, :, 0:VW].rearrange("p k h c -> p (k h) c"),
                                   v_all[:, group, :, :, :].rearrange("p k h c -> p (k h) c"),
                                   ACT.Copy).then_inc(v_staged, 1)
            copy_ctx(NG - 1)

            def hidden(c):
                for f in range(FT):
                    act.wait_ge(up_e_done, c * FT + f + 1)
                    wait(act, down_e_done, c - 1)
                    act.activation(hid_e[:, c % 2, f, :], bank[f][:, :], ACT.Relu,
                                   bias=L["exp_b1"][:, (c % NE) * FT + f:(c % NE) * FT + f + 1]).then_inc(hid_ready, 1)

            for step in STEPS[len(FINISH_AT):]:
                finish(0, step)
            hidden(0)
            for c in range(B * NE):
                if c + 1 < B * NE:
                    hidden(c + 1)
                for step in STEPS[2 * c:2 * c + 2]:
                    finish(1, step)

        @block.tensor
        def _(pe):
            def turn(b, dest):
                for t in range(QT):
                    last = pe.transpose(dest[:, t * P:(t + 1) * P], zn[:, QT * b + t, :], ident)
                last.then_inc(turned[b], 1)

            pe.wait_ge(in_early, 16)
            for b in range(B):
                pe.wait_ge(in_xt[b], 16)
                pe.matmul(bank[b][0:A, :], C["down"], xt[:, tokens(b)], start=True, stop=True).then_inc(down_done, 1)
            for b in range(B):
                for t in range(QT):
                    at = (QT * b + t) * P
                    pe.matmul(bank[4 + b][:, t * P:(t + 1) * P], xt[:, at:at + P], ident, start=(t == 0), stop=False,
                              skip_group_check=True)
            pe.wait_ge(in_up, 16)
            pe.wait_ge(ones_ready, 1)
            for b in range(B):
                pe.wait_ge(sel_ready, b + 1)
                pe.wait_ge(gelu_ready, b + 1)
                pe.matmul(bank[2 + b][0:A, :], sel_w[:, b, :], ad_h[:, tokens(b)], start=True, stop=True
                          ).then_inc(expert_done, 1)
                pe.wait_ge(expert_ready, b + 1)
                for t in range(QT):
                    at = (QT * b + t) * P
                    last = pe.matmul(bank[4 + b][:, t * P:(t + 1) * P], ad_e[:, at:at + P], up[:, :],
                                     start=False, stop=(t == QT - 1), skip_group_check=True)
                last.then_inc(up_done, 1)
            pe.wait_ge(in_late, 16)
            pe.wait_ge(silu_ready, 1)
            for i in range(2):
                last = pe.matmul(bank[7][:, 2 * i:2 * i + 2], L["w_ada"][:, i * D:(i + 1) * D], silu,
                                 start=True, stop=True)
            last.then_inc(ada_done, 1)
            pe.wait_ge(in_p32, 16)
            pe.wait_ge(in_p64, 16)
            steps = ((SE, W32["subj"], style_hot[0:SUBJ, :]), (P, W64["hyp_w1"], seT), (P, L["hyp_w2"], hid1),
                     (SE, L["sty_w1"], hid2))
            for i, (m, w, x) in enumerate(steps):
                pe.wait_ge(hyp_in, i + 1)
                pe.matmul(bank[6][0:m, 2 * i:2 * i + 2], w, x, start=True, stop=True).then_inc(hyp_mm, 1)
            pe.wait_ge(hyp_in, 5)
            for i in range(2):
                last = pe.matmul(bank[6][:, 8 + 2 * i:10 + 2 * i], W64["sty_w2"][:, i * D:(i + 1) * D], hid3,
                                 start=True, stop=True)
            last.then_inc(hyp_mm, 1)
            for b in range(B):
                pe.wait_ge(norm_ready[b], 2)
                turn(b, bank[(0, 4)[b]])
                pe.wait_ge(affine_done[b], 1)
                if b == 1:
                    pe.wait_ge(hyp_in, 6)
                for w, ps in (("wq", bank[(2, 5)[b]]), ("wk", bank[(3, 6)[b]])):
                    pe.matmul(ps[:, :], L[w], xt[:, tokens(b)], start=True, stop=True).then_inc(qk_proj, 1)
                for t in range(QT):
                    at = (QT * b + t) * P
                    last = pe.matmul(bank[(1, 7)[b]][:, t * P:(t + 1) * P], xt[:, at:at + P], L["wv"],
                                     start=True, stop=True)
                last.then_inc(v_proj, 1)
            pe.wait_ge(part_hi, 1)
            pe.wait_ge(qk_float, 2)
            pe.wait_ge(v_ready, 1)
            for j in range(HG):
                last = pe.matmul(score_ps[j][:, :], parts[0][:, 0, 0, 0:P], parts[0][:, 0, 0, :],
                                 start=True, stop=True)
            last.then_inc(primed, 1)

            def score(unit, j):
                group, qt, rows_of = unit // QT, unit % QT, slice(64 * (j % 2), 64 * (j % 2) + 64)
                if seeded_by_tensor(unit, j):
                    pe.wait_ge(sum_done, HG * (unit - 1) + j + 1)
                    pe.wait_ge(mask_bf_ready, 1)
                    pe.matmul(score_ps[j][:, :], diag_masked[:, :], mask_bf[:, qt, :], start=True, stop=False,
                              skip_group_check=True)
                else:
                    pe.wait_ge(seeded[j], unit + 1)
                if qt == 0 and j == 0:
                    pe.wait_ge(stack_in[group % (NH // HG)], 64 * (group // (NH // HG) + 1))
                pe.matmul(score_ps[j][:, :], q_st[rows_of, group % (NH // HG), j // 2, qt * P:(qt + 1) * P],
                          k_st[rows_of, group % (NH // HG), j // 2, :], start=False, stop=True,
                          skip_group_check=True).then_inc(qk_done, 1)

            def turn_scores(unit, j):
                pe.wait_ge(shift_done, HG * unit + j + 1)
                wait(pe, exp_done, HG * unit + j - 1)
                for k in range(QT):
                    last = pe.transpose(turned_ps[j % 2][:, k * P:(k + 1) * P],
                                        ring[:, unit % RING, j, k * P:(k + 1) * P], ident)
                last.then_inc(tr_done, 1)

            def values(group, k):
                if k == 0:
                    pe.wait_ge(exp_done, HG * QT * (group + 1))
                    pe.wait_ge(v_staged, group + 1)
                    wait(pe, ctx_copied, group)
                for j in range(HG):
                    last = pe.matmul(ctx_ps[32 * j:32 * j + 32, :], v_st[:, group % 2, k, j, :],
                                     probs[:, group % 2, j, k, :], start=(k == 0), stop=(k == QT - 1))
                last.then_inc(pv_done, 1)

            def finish(b, step):
                if step in (TURN_CTX0, TURN_CTX1):
                    part = step - TURN_CTX0
                    pe.wait_ge(ctx_copied, NG // B * (b + 1))
                    wait(pe, ctx_scaled[b], part)
                    wait(pe, base_added[0], b)
                    kept = ident.rearrange("p (h c) -> p h c", c=32)[:, :, 0:VW]
                    for t in range(2):
                        at = (2 * part + t) * P
                        for g in range(NH // HG):
                            to = (t * (NH // HG) + g) * HG * VW
                            last = pe.matmul(aux_ps[:, to:to + HG * VW].rearrange("p (h c) -> p h c", c=VW),
                                             ctx_t[:, g, at:at + P], kept, start=True, stop=True)
                    last.then_inc(ctx_turned[b], 1)
                if step == TURN_BACK:
                    pe.wait_ge(ctx_scaled[b], 2)
                    for t in range(QT):
                        last = pe.transpose(aux_ps[:, t * P:(t + 1) * P], ctx_n[:, t, :], ident)
                    last.then_inc(ctx_back[b], 1)
                if step == PROJECT:
                    pe.wait_ge(ctx_back_copied[b], 1)
                    for t in range(QT):
                        at, dest = (QT * b + t) * P, aux_ps[:, t * P:(t + 1) * P]
                        pe.matmul(dest, xt[:, at:at + P], ident, start=True, stop=False)
                        last = pe.matmul(dest, ctx_nt[:, t * P:(t + 1) * P], L["wo"], start=False, stop=True)
                    last.then_inc(wo_done[b], 1)
                if step in (TURN_H, TURN_H3):
                    pe.wait_ge(norm_ready[b], 3 if step == TURN_H else 4)
                    turn(b, aux_ps)
                if step in (FF1_0, FF1_1, FF1_2, FF1_3):
                    f = step - FF1_0
                    pe.wait_ge(affine_done[b], 2)
                    wait(pe, ff_half[b], f)
                    pe.matmul(aux_ps[:, :], L["w1"][:, f * P:(f + 1) * P], h_t[:, :], start=True, stop=True
                              ).then_inc(ff1_done[b], 1)
                if step == FF2:
                    pe.wait_ge(ff_ready[b], FT)
                    for t in range(QT):
                        for f in range(FT):
                            last = pe.matmul(aux_ps[:, t * P:(t + 1) * P], ff_a[:, f, t * P:(t + 1) * P],
                                             L["w2"][:, f * P:(f + 1) * P], start=(f == 0), stop=(f == FT - 1))
                    last.then_inc(ff2_done[b], 1)
                if step == ROUTE:
                    pe.wait_ge(route_in[b], 1)
                    for t in range(QT):
                        last = pe.matmul(aux_ps[:, t * NE:(t + 1) * NE], h3_t[:, (QT * b + t) * P:(QT * b + t + 1) * P],
                                         L["router"], start=True, stop=True)
                    last.then_inc(logits_done[b], 1)
                if step == TURN_GATES:
                    pe.wait_ge(comb_ready[b], 1)
                    for t in range(QT):
                        last = pe.transpose(aux_ps[0:NE, t * P:(t + 1) * P], route[:, 11, QT * b + t, :], ident)
                    last.then_inc(comb_turned[b], 1)
                if step == GATED_BIAS:
                    pe.wait_ge(comb_t_ready[b], 1)
                    pe.wait_ge(in_eb2, 16)
                    for t in range(QT):
                        last = pe.matmul(aux_ps[:, t * P:(t + 1) * P], comb_t[:, (QT * b + t) * P:(QT * b + t + 1) * P],
                                         eb2[:, :], start=True, stop=True)
                    last.then_inc(eb2_done[b], 1)

            pe.wait_ge(qk_float, 4)
            pe.wait_ge(v_ready, 2)
            for s in range(UNITS + LAG):
                for j in (0, 2):
                    if s < UNITS:
                        score(s, j)
                        score(s, j + 1)
                    if 1 <= s <= UNITS:
                        turn_scores(s - 1, j)
                        turn_scores(s - 1, j + 1)
                    if j == 2 and s >= LAG:
                        values((s - LAG) // QT, (s - LAG) % QT)
                    if 2 * s + j // 2 in FINISH:
                        finish(0, FINISH[2 * s + j // 2])

            def layer1(c):
                b, e = c // NE, c % NE
                pe.wait_ge(route_in[b], 1)
                if b == 0:
                    pe.wait_ge(experts_in[e], 32)
                if c == 0:
                    pe.wait_ge(sum_done, HG * UNITS)
                for f in range(FT):
                    wait(pe, hid_ready, (c - 1) * FT + f + 1)
                    pe.matmul(bank[f][:, :], w1_e[:, e, f * P:(f + 1) * P], h3_t[:, tokens(b)],
                              start=True, stop=True).then_inc(up_e_done, 1)

            def layer2(c):
                pe.wait_ge(hid_ready, (c + 1) * FT)
                wait(pe, acc_done, c - 1)
                for t in range(QT):
                    for f in range(FT):
                        last = pe.matmul(bank[4 + c % 2][:, t * P:(t + 1) * P],
                                         hid_e[:, c % 2, f, t * P:(t + 1) * P], w2_e[:, c % NE, f, :],
                                         start=(f == 0), stop=(f == FT - 1))
                last.then_inc(down_e_done, 1)

            layer1(0)
            finish(0, TURN_GATES)
            layer1(1)
            finish(0, GATED_BIAS)
            pe.wait_ge(exp_done, HG * UNITS)
            for c in range(B * NE):
                if 1 <= c < B * NE - 1:
                    layer1(c + 1)
                for step in STEPS[2 * c:2 * c + 1]:
                    finish(1, step)
                layer2(c)
                for step in STEPS[2 * c + 1:2 * c + 2]:
                    finish(1, step)

        @block.vector
        def _(dve):
            link = chained(dve, dve_step)

            dve.wait_ge(in_ids, 16)
            link(dve.tensor_copy(id_f, ids_i[:, :]))
            dve.tensor_scalar(trig_x[:, 0:2], id_f[:, 2:4], 0.01, 4000.0, ALU.mult, ALU.mult)
            dve.wait_ge(in_angles, 16)
            dve.tensor_copy(trig_x[:, 2:6], angles[:, :]).then_inc(ids_ready, 1)

            link(dve.tensor_scalar(dom, id_f[:, 0:2], 0.0, float(E0 - 1), ALU.max, ALU.min))
            link(dve.tensor_tensor(valid, dom, id_f[:, 0:2], ALU.is_equal))
            dve.wait_ge(in_early, 16)
            dve.wait_ge(in_p32, 16)
            for b in range(B):
                link(dve.tensor_scalar(hot[:, b, :], C["iota16"][0:A, :], dom[0:A, b:b + 1], None, ALU.is_equal))
                link(dve.tensor_tensor(sel_prod[:, b, :, :],
                                       W32["expert_w"].rearrange("a (o e) -> a o e", e=E0),
                                       hot[:, b:b + 1, :].to_broadcast([A, A, E0]), ALU.mult))
                link(dve.tensor_reduce(sel_w[:, b, :], sel_prod[:, b, :, :], AX_X, ALU.add))
                link(dve.tensor_tensor(sel_w[:, b, :], sel_w[:, b, :], W32["eye"], ALU.subtract))
                dve.scalar_tensor_tensor(sel_w[:, b, :], sel_w[:, b, :], valid[0:A, b:b + 1], W32["eye"],
                                         ALU.mult, ALU.add).then_inc(sel_ready, 1)
                dve.tensor_tensor(hot_prod[:, 2 * b, :], W32["expert_b"], hot[:, b, :], ALU.mult)
                link(dve.tensor_tensor(hot_prod[:, 2 * b + 1, :], W32["emb"], hot[:, b, :], ALU.mult))
                link(dve.tensor_reduce(emb_b[:, 2 * b:2 * b + 2], hot_prod[:, 2 * b:2 * b + 2, :], AX_X, ALU.add))
                link(dve.scalar_tensor_tensor(emb_b[:, 2 * b:2 * b + 1], emb_b[:, 2 * b:2 * b + 1],
                                              valid[0:A, b:b + 1], emb_b[:, 2 * b + 1:2 * b + 2],
                                              ALU.mult, ALU.add))
            link(dve.tensor_scalar(wrap, id_f[:, 4:6], 0.0, float(SUBJ), ALU.is_lt, ALU.mult))
            link(dve.tensor_tensor(style_cmp, id_f[:, 4:6], wrap, ALU.add))
            link(dve.tensor_scalar(style_cmp, style_cmp, 0.0, float(SUBJ - 1), ALU.max, ALU.min))
            dve.tensor_scalar(style_hot, style_cmp, C["row"], None, ALU.is_equal).then_inc(hyp_in, 1)

            def expert_out(b):
                dve.wait_ge(expert_done, b + 1)
                dve.tensor_scalar(ad_e[0:A, tokens(b)], bank[2 + b][0:A, :], emb_b[:, 2 * b:2 * b + 1],
                                  None, ALU.add).then_inc(expert_ready, 1)

            def moments_of(b, source=xn[:, :, :], first=0):
                for t in range(QT * b, QT * b + QT):
                    last = dve.bn_stats(stats[:, t, :], source[:, t - QT * b + first, :])
                link(last)
                for t in range(QT * b, QT * b + QT):
                    last = dve.bn_aggr(moments[:, t, :], stats[:, t, :])
                link(last)
                dve.tensor_scalar(rstd[:, half(b)], moments[:, half(b), 1], LN_EPS, None, ALU.add
                                  ).then_inc(var_ready[b], 1)

            def normalise(b, n):
                dve.wait_ge(rstd_ready[b], n + 1)
                if n < 2:
                    link(dve.reciprocal(rstd[:, half(b)], rstd[:, half(b)]))
                for t in range(QT * b, QT * b + QT):
                    source = tiles_of(bank[4 + b])[:, t - QT * b, :] if n == 0 else xn[:, t, :]
                    last = dve.tensor_scalar(zn[:, t, :], source, moments[:, t, 0:1], rstd[:, t:t + 1],
                                             ALU.subtract, ALU.mult)
                last.then_inc(norm_ready[b], 1)

            def tiles_of(ps):
                return ps[:, :].rearrange("p (t d) -> p t d", t=QT)

            def adapter_out(b):
                dve.wait_ge(up_done, b + 1)
                moments_of(b, tiles_of(bank[4 + b]))

            def rotate(b):
                dve.wait_ge(norm_ready[b], 1)
                dve.wait_ge(rot_ready, b + 1)
                link(dve.tensor_tensor(xn[:, half(b), :], zn[:, half(b), :],
                                       rot_a[:, b:b + 1, :].to_broadcast([P, QT, D]), ALU.mult))
                link(dve.tensor_tensor(xn[:, half(b), :], xn[:, half(b), :],
                                       rot_c[:, b:b + 1, :].to_broadcast([P, QT, D]), ALU.add))
                dve.wait_ge(swap_done, b + 1)
                link(dve.tensor_tensor(xn[:, half(b), :], xn[:, half(b), :], swapped[:, half(b), :], ALU.add))
                moments_of(b, first=QT * b)

            def q_and_k(b):
                for kind, (bias, scale) in enumerate(((L["bq"], 1 / math.sqrt(DH)), (L["bk"], 1.0))):
                    dve.wait_ge(qk_proj, 2 * b + kind + 1)
                    dve.tensor_scalar(qk_f[b][:, 2 * kind, :], bank[((2, 3), (5, 6))[b][kind]][:, :], bias, scale,
                                      ALU.add, ALU.mult).then_inc(qk_float, 1)

            def split(b, level, arrived, done):
                for kind in range(2):
                    dve.wait_ge(arrived, 2 * b + kind + 1)
                    dest = parts[b][:, kind, 2, :] if level else qk_f[b][:, 2 * kind + 1, :]
                    dve.tensor_tensor(dest, qk_f[b][:, 2 * kind + level, :], parts[b][:, kind, level, :],
                                      ALU.subtract).then_inc(done, 1)

            def values_of(b):
                dve.wait_ge(v_pad, 2)
                dve.wait_ge(v_proj, b + 1)
                for k in range(QT):
                    last = dve.tensor_tensor(
                        v_all[:, (NH // HG) * b:(NH // HG) * (b + 1), k, :, 0:DH],
                        bank[(1, 7)[b]][:, k * P:(k + 1) * P].rearrange("p (g h c) -> p g h c", g=NH // HG, h=HG),
                        R["bv"].rearrange("p (g h c) -> p g h c", g=NH // HG, h=HG), ALU.add)
                last.then_inc(v_ready, 1)

            expert_out(0)
            adapter_out(0)
            expert_out(1)
            dve.wait_ge(silu_exp_done, 1)
            link(dve.tensor_scalar(silu, silu_e, 1.0, None, ALU.add))
            link(dve.reciprocal(silu, silu))
            dve.tensor_tensor(silu, silu, trig[:, 0:2], ALU.mult).then_inc(silu_ready, 1)
            normalise(0, 0)
            rotate(0)
            adapter_out(1)
            normalise(0, 1)
            dve.wait_ge(ada_done, 1)
            link(dve.tensor_scalar(ada[:, 0:2], bank[7][:, 0:2], L["b_ada"][:, 0:1], 1.0, ALU.add, ALU.add))
            dve.tensor_scalar(ada[:, 2:4], bank[7][:, 2:4], L["b_ada"][:, 1:2], None, ALU.add
                              ).then_inc(ada_ready, 1)
            normalise(1, 0)
            rotate(1)
            q_and_k(0)
            normalise(1, 1)
            split(0, 0, part_hi, rest_ready)
            split(0, 1, part_mid, part_lo)
            values_of(0)
            dve.wait_ge(hyp_in, 6)
            dve.scalar_tensor_tensor(soft_a, gam, -1.0, gam, ALU.mult, ALU.max).then_inc(abs_ready, 1)
            dve.tensor_scalar(b1_tanh[:, :], L["b1"], 0.851, None, ALU.mult)
            link(dve.tensor_scalar(b1_half[:, :], L["b1"], 0.5, None, ALU.mult))
            q_and_k(1)
            split(1, 0, part_hi, rest_ready)
            split(1, 1, part_mid, part_lo)
            values_of(1)

            def seed(unit, j):
                if unit == 0:
                    dve.wait_ge(primed, 1)
                    dve.wait_ge(in_mask, 16)
                else:
                    dve.wait_ge(sum_done, HG * (unit - 1) + j + 1)
                dve.tensor_scalar(score_ps[j][:, :], mask[:, unit // (NG // B * QT) * QT + unit % QT, :], MASKED, None,
                                  ALU.mult).then_inc(seeded[j], 1)

            def add_bias(unit, j):
                slot, n = unit % RING, (unit % RING) * HG + j
                if j == 0:
                    dve.wait_ge(bias_in[slot], 16 * (unit // RING + 1))
                dve.wait_ge(qk_done, HG * unit + j + 1)
                dve.tensor_tensor_reduce(ring[:, slot, j, :], score_ps[j][:, :], ring[:, slot, j, :], 1.0,
                                         -3.0e38, ALU.add, ALU.max, row_max[:, n:n + 1]).then_inc(sum_done, 1)

            def rt(b, i):
                return route[:, i, half(b), :]

            def tok(b, i):
                return token[:, i, half(b)]

            def per_token(ap):
                return ap.unsqueeze(2).to_broadcast([P, QT, NE])

            logits = aux_ps[:, 0:QT * NE].rearrange("p (t e) -> p t e", e=NE)

            def top_two(b):
                dve.wait_ge(logit_exp[b], 1)
                link(dve.tensor_reduce(tok(b, 1), rt(b, 1), AX_X, ALU.add))
                link(dve.reciprocal(tok(b, 1), tok(b, 1)))
                link(dve.tensor_tensor(rt(b, 2), rt(b, 1), per_token(tok(b, 1)), ALU.mult))
                order = C["iota16"][:, 0:NE].unsqueeze(1).to_broadcast([P, QT, NE])
                left = rt(b, 2)
                for i in range(2):
                    top, first = tok(b, 2 + i), tok(b, 4 + i)
                    equal, key, hot_e = rt(b, 3 + 4 * i), rt(b, 4 + 4 * i), rt(b, 5 + 4 * i)
                    link(dve.tensor_reduce(top, left, AX_X, ALU.max))
                    link(dve.tensor_tensor(equal, left, per_token(top), ALU.is_equal))
                    link(dve.scalar_tensor_tensor(key, equal, 100.0, order, ALU.mult, ALU.subtract))
                    link(dve.tensor_reduce(first, key, AX_X, ALU.max))
                    link(dve.tensor_tensor(hot_e, key, per_token(first), ALU.is_equal))
                    if i == 0:
                        link(dve.scalar_tensor_tensor(rt(b, 6), hot_e, -2.0, left, ALU.mult, ALU.add))
                        left = rt(b, 6)
                link(dve.tensor_tensor(tok(b, 6), tok(b, 2), tok(b, 3), ALU.add))
                link(dve.reciprocal(tok(b, 6), tok(b, 6)))
                link(dve.tensor_tensor(rt(b, 10), rt(b, 5), rt(b, 9), ALU.add))
                link(dve.tensor_tensor(rt(b, 10), rt(b, 10), rt(b, 2), ALU.mult))
                dve.tensor_tensor(rt(b, 11), rt(b, 10), per_token(tok(b, 6)), ALU.mult).then_inc(comb_ready[b], 1)

            def finish(b, step):
                residual = xn[:, half(b), :]
                if step in (TURN_CTX0, TURN_CTX1):
                    part = step - TURN_CTX0
                    dve.wait_ge(ctx_turned[b], part + 1)
                    t0 = 2 * part
                    context = aux_ps[:, 0:2 * NH * VW].rearrange("p (h c) -> p h c", c=VW)
                    r = ctx_r[:, :, :].rearrange("p t h -> p (t h)")
                    link(dve.reciprocal(r, context[:, :, DH]))
                    link(dve.tensor_tensor(ctx_r[:, :, :], ctx_r[:, :, :],
                                           all_masked[:, 2, QT * b + t0:QT * b + t0 + 2].unsqueeze(2)
                                           .to_broadcast([P, 2, NH]), ALU.add))
                    link(dve.tensor_tensor(ctx_n[:, t0:t0 + 2, :].rearrange("p t (h c) -> p (t h) c", c=DH),
                                           context[:, :, 0:DH], r.unsqueeze(2).to_broadcast([P, 2 * NH, DH]),
                                           ALU.mult))
                    dve.tensor_copy(small[:, 54:55], ctx_r[:, 0, 0:1]).then_inc(ctx_scaled[b], 1)
                if step == PROJECT:
                    dve.wait_ge(wo_done[b], 1)
                    link(dve.tensor_tensor(residual, tiles_of(aux_ps), R["bo"].unsqueeze(1).to_broadcast([P, QT, D]),
                                           ALU.add))
                    moments_of(b, first=QT * b)
                if step == FF2:
                    dve.wait_ge(ff2_done[b], 1)
                    link(dve.tensor_tensor(residual, tiles_of(aux_ps), residual, ALU.add))
                    moments_of(b, first=QT * b)
                if step == ROUTE:
                    dve.wait_ge(logits_done[b], 1)
                    link(dve.tensor_reduce(tok(b, 0), logits, AX_X, ALU.max))
                    dve.tensor_tensor(rt(b, 0), logits, per_token(tok(b, 0)), ALU.subtract).then_inc(logit_max[b], 1)
                if step == TURN_GATES:
                    dve.wait_ge(comb_turned[b], 1)
                    dve.tensor_copy(comb_t[:, tokens(b)], aux_ps[0:NE, :]).then_inc(comb_t_ready[b], 1)
                if step == GATED_BIAS:
                    dve.wait_ge(eb2_done[b], 1)
                    dve.tensor_tensor(residual, tiles_of(aux_ps), residual, ALU.add).then_inc(base_added[b], 1)

            def settle(b, step):
                if step == PROJECT:
                    normalise(b, 2)
                if step in (FF1_0, FF1_1, FF1_2, FF1_3):
                    f = step - FF1_0
                    dve.wait_ge(ff_half[b], f + 1)
                    dve.scalar_tensor_tensor(ff_a[:, f, :], ff_g[:, f % 2, :], 1.0, ff_a[:, f, :],
                                             ALU.add, ALU.mult).then_inc(ff_ready[b], 1)
                if step == FF1_0:
                    dve.wait_ge(norm_ready[b], 3)
                    link(dve.tensor_tensor(xn[:, half(b), :], xn[:, half(b), :],
                                           R["b2"].unsqueeze(1).to_broadcast([P, QT, D]), ALU.add))
                if step == FF2:
                    normalise(b, 3)
                if step == TURN_H3:
                    dve.wait_ge(affine_done[b], 3)
                    link(dve.bn_stats(t_stats[:, b, :], h_t[:, :]))
                    link(dve.bn_aggr(t_mom[:, b, :], t_stats[:, b, :]))
                    dve.tensor_scalar(t_coef[:, 0, b:b + 1], t_mom[:, b, 1:2], 1e-8, None, ALU.add
                                      ).then_inc(t_var[b], 1)
                    dve.wait_ge(t_rstd[b], 1)
                    link(dve.tensor_tensor(t_coef[:, 1, b:b + 1], t_coef[:, 0, b:b + 1], gam[:, b:b + 1], ALU.mult))
                    link(dve.tensor_tensor(t_coef[:, 2, b:b + 1], t_coef[:, 1, b:b + 1], t_mom[:, b, 0:1], ALU.mult))
                    link(dve.tensor_tensor(t_coef[:, 3, b:b + 1], bet[:, b:b + 1], t_coef[:, 2, b:b + 1],
                                           ALU.subtract))
                    dve.tensor_scalar(h3_t[:, tokens(b)], h_t[:, :], t_coef[:, 1, b:b + 1], t_coef[:, 3, b:b + 1],
                                      ALU.mult, ALU.add).then_inc(route_in[b], 1)
                if step == ROUTE:
                    top_two(b)

            seed(0, 0)
            for s in range(UNITS + LAG):
                for j in range(HG):
                    if s < UNITS:
                        add_bias(s, j)
                        if j % 2 and s + 1 < UNITS and seeded_by_vector(s + 1, j - 1):
                            seed(s + 1, j - 1)
                    if j % 2 and 2 * s + j // 2 - 1 in FINISH:
                        finish(0, FINISH[2 * s + j // 2 - 1])
                    if j % 2 and 2 * s + j // 2 - 2 in FINISH:
                        settle(0, FINISH[2 * s + j // 2 - 2])
                if s < NT:
                    link(dve.tensor_reduce(all_masked[:, 0, s:s + 1], mask[:, s, :], AX_X, ALU.min))
                if s == NT:
                    link(dve.tensor_scalar(all_masked[:, 1, :], all_masked[:, 0, :], -1.0, 1.0, ALU.mult, ALU.add))
                    link(dve.reciprocal(all_masked[:, 2, :], all_masked[:, 1, :]))
                    link(dve.tensor_scalar(all_masked[:, 2, :], all_masked[:, 2, :], 0.0, None, ALU.mult))
                    dve.wait_ge(softplus_done, 1)
                    link(dve.tensor_scalar(gam, gam, 0.0, 1e-8, ALU.max, ALU.add))
                    link(dve.tensor_tensor(gam, gam, soft_l, ALU.add))
            for step in STEPS[len(FINISH_AT):]:
                finish(0, step)

            def add_expert(c):
                b, e = c // NE, c % NE
                dve.wait_ge(down_e_done, c + 1)
                if e == 0:
                    dve.wait_ge(base_added[b], 1)
                else:
                    dve.wait_ge(acc_done, c)
                for t in range(QT):
                    last = dve.scalar_tensor_tensor(
                        xn[:, QT * b + t, :], bank[4 + c % 2][:, t * P:(t + 1) * P],
                        route[:, 11, QT * b + t, e:e + 1], xn[:, QT * b + t, :], ALU.mult, ALU.add)
                last.then_inc(acc_done, 1)

            for c in range(B * NE):
                for step in STEPS[2 * c:2 * c + 1]:
                    finish(1, step)
                    settle(1, step)
                add_expert(c)
                for step in STEPS[2 * c + 1:2 * c + 2]:
                    finish(1, step)
                    settle(1, step)


def kernel(**inputs):
    import concourse.bacc as bacc
    from concourse.bass_utils import run_bass_kernel_spmd

    def arr(name):
        return np.ascontiguousarray(np.asarray(inputs[name]))

    def l0(name):
        return arr("L0_cond_" + name)

    def l2(name):
        return arr("L2_cond_" + name)

    def l3(name):
        return arr("L3_cond_" + name)

    def pack(columns, parts):
        out = [parts[name].reshape(parts[name].shape[0], -1) for name, _ in columns]
        assert [p.shape[1] for p in out] == [n for _, n in columns]
        return np.ascontiguousarray(np.concatenate(out, axis=1), dtype=np.float32)

    x = arr("x").reshape(TOK, D)
    f32 = np.float32
    half = D // 2
    freq = np.exp(np.arange(half, dtype=f32) * f32(-math.log(10000.0) / (half - 1)))
    early = pack(EARLY, {
        "ident": np.eye(P, dtype=f32), "freq": np.concatenate([freq, freq])[:, None],
        "iota16": np.tile(np.arange(E0, dtype=f32), (P, 1)), "row": np.arange(P, dtype=f32)[:, None],
        "down": l0("down_W").T})

    def stacked(columns):
        return columns.reshape(-1, NH // HG, 2, 2, DH).transpose(0, 1, 3, 4, 2).reshape(-1, D)

    late = pack(LATE, {
        "w_ada": l2("W_ada"), "b_ada": l2("b_ada").reshape(2, D).T, "wq": stacked(l2("Wq")), "wk": stacked(l2("Wk")),
        "wv": l2("Wv"), "wo": l2("Wo"), "bq": stacked(l2("bq")).T, "bk": stacked(l2("bk")).T,
        "g2": l2("g2")[:, None], "beta2": l2("beta2")[:, None], "ln_g": l3("ln_g")[:, None],
        "ln_b": l3("ln_b")[:, None], "router": l3("router_w"), "hyp_w2": l3("hyp_w2"),
        "hyp_b1": l3("hyp_b1")[:, None], "hyp_b2": l3("hyp_b2")[:, None], "sty_w1": l3("sty_w1"),
        "sty_b2": l3("sty_b2").reshape(2, D).T, "b1": l2("b1").reshape(FT, P).T,
        "exp_b1": l3("exp_b1").reshape(NE * FT, P).T, "w1": l2("W1"),
        "w2": l2("W2").reshape(FT, P, D).transpose(1, 0, 2)})
    pack32 = pack(PACK32, {
        "expert_w": l0("expert_W").transpose(2, 1, 0), "expert_b": l0("expert_b").T,
        "emb": l0("domain_emb").T, "down_b": l0("down_b")[:, None], "subj": l3("subj_emb"),
        "eye": np.eye(A, dtype=f32)})
    pack64 = pack(PACK64, {"hyp_w1": l3("hyp_w1"), "sty_b1": l3("sty_b1")[:, None], "sty_w2": l3("sty_w2")})
    rows = np.concatenate([l0("ln_gamma"), l0("ln_beta"), l2("bv"), l2("bo"), l2("b2")])
    arrays = {
        "x_t": np.ascontiguousarray(x.T), "early": early, "late": late, "pack32": pack32,
        "up": np.concatenate([l0("up_W").T, l0("up_b")[None, :]]), "pack64": pack64, "rows": rows,
        "ids": np.concatenate([arr("itok_B_0_15"), arr("itok_B_34_63"), arr("itok_B_6_14")]),
        "ang": np.concatenate([arr("condB_theta"), arr("condB_phi")]),
        "bias": arr("fside_Bx16xSxS_0").reshape(NG, HG, S, S),
        "mask": arr("mask_Bx1xSxS_bk0").reshape(B, S, S),
        "w1": l3("exp_w1"), "w2": l3("exp_w2"), "eb2": l3("exp_b2"),
    }
    nc = bacc.Bacc("TRN2", target_bir_lowering=False, num_devices=1)
    args = [nc.dram_tensor(f"in_{n}", a.shape, mybir.dt.from_np(a.dtype), kind="ExternalInput").ap()
            for n, a in arrays.items()]
    args.append(nc.dram_tensor("out", (B, S, D), F32, kind="ExternalOutput").ap())
    build(nc, *args)
    r = run_bass_kernel_spmd(nc, [{f"in_{n}": a for n, a in arrays.items()}], core_ids=[0])
    return r.results[0]["out"]
```

```python
import math
from contextlib import ExitStack

import numpy as np
import concourse.bass as bass
from concourse import mybir
from concourse.alu_op_type import AluOpType as ALU

F32 = mybir.dt.float32
BF16 = mybir.dt.bfloat16
F32R = mybir.dt.float32r
I32 = mybir.dt.int32
U8, U16 = mybir.dt.uint8, mybir.dt.uint16
ACT = mybir.ActivationFunctionType
AX_X = mybir.AxisListType.X

P = 128
B, S, D = 2, 512, 128
TOK = B * S
NT = TOK // P
QT = S // P
A = 32
E0 = 16
NH, DH = 16, 8
HG = 4
NG = B * NH // HG
FF = 512
FT = FF // P
NE = 8
SUBJ, SE = 32, 64
VW = DH + 1
PARTS = 3
PRODUCTS = 8
UNITS = NG * QT
RING = 6
LAG = 5
LN_EPS = 1e-5
MASKED = -1e30
ROUND = 1.5 * 2.0 ** 23
TWO_PI = (6.28125, 0.00193500518798828125, 2 * math.pi - 6.28125 - 0.00193500518798828125)
PI_BELOW = 3.1415925

EARLY = (("ident", P), ("freq", 1), ("iota16", E0), ("row", 1), ("down", A))
LATE = (("w_ada", 2 * D), ("b_ada", 2), ("wq", D), ("wk", D), ("wv", D), ("wo", D), ("bq", 1), ("bk", 1),
        ("g2", 1), ("beta2", 1), ("ln_g", 1), ("ln_b", 1), ("router", NE), ("hyp_w2", D), ("hyp_b1", 1),
        ("hyp_b2", 1), ("sty_w1", D // 2), ("sty_b2", 2), ("b1", FT), ("exp_b1", NE * FT), ("w1", FF), ("w2", FF))
PACK32 = (("expert_w", E0 * A), ("expert_b", E0), ("emb", E0), ("down_b", 1), ("subj", SE), ("eye", A))
PACK64 = (("hyp_w1", D), ("sty_b1", 1), ("sty_w2", 2 * D))
ROWS = (("gamma", D), ("beta", D), ("bv", D), ("bo", D), ("b2", D))

(TURN_CTX0, TURN_CTX1, TURN_BACK, PROJECT, TURN_H, FF1_0, FF1_1, FF1_2, FF1_3, FF2, TURN_H3, ROUTE, TURN_GATES,
 GATED_BIAS) = STEPS = range(14)
FINISH_AT = (44, 46, 48, 50, 53, 56, 58, 60, 62, 64, 67, 73)
AHEAD = 5
LATE_STEPS = STEPS[TURN_BACK:]
FINISH = {at: step for step, at in enumerate(FINISH_AT)}


def width(columns):
    return sum(n for _, n in columns)


def columns_of(tile, columns):
    out, at = {}, 0
    for name, n in columns:
        out[name] = tile[:, at:at + n]
        at += n
    return out


def build(nc, x_t, early_d, late_d, pack32_d, up_d, pack64_d, rows_d, ids_d, ang_d, bias_d, mask_d,
          w1_d, w2_d, eb2_d, out_d):
    with ExitStack() as ctx:
        def sb(name, shape, dt=F32):
            return ctx.enter_context(nc.sbuf_tensor(name, shape, dt))

        def sem(name):
            return ctx.enter_context(nc.semaphore(name))

        def sems(name, n=B):
            return [sem(f"{name}{i}") for i in range(n)]

        bank = [ctx.enter_context(nc.psum_tensor(f"bank{i}", [P, 512], F32)) for i in range(8)]
        score_ps, turned_ps, ctx_ps = bank[0:4], bank[4:6], bank[6]
        aux = (bank[7], bank[5])

        q_dram = nc.dram_tensor("q_parts", (B, PRODUCTS, D, S), BF16).ap()
        k_dram = nc.dram_tensor("k_parts", (B, PRODUCTS, D, S), BF16).ap()

        early = sb("early", [P, width(EARLY)])
        late = sb("late", [P, width(LATE)])
        pack32 = sb("pack32", [A, width(PACK32)])
        pack64 = sb("pack64", [SE, width(PACK64)])
        rows = sb("rows", [P, width(ROWS)])
        up = sb("up", [A + 1, D])
        ids_i = sb("ids_i", [P, 6], I32)
        angles = sb("angles", [P, 4])
        eb2 = sb("eb2", [NE, D])
        C, L, W32, W64, R = (columns_of(early, EARLY), columns_of(late, LATE), columns_of(pack32, PACK32),
                             columns_of(pack64, PACK64), columns_of(rows, ROWS))
        ident = C["ident"]

        q_st = sb("q_st", [P, NH // HG, 2, S], BF16)
        k_st = sb("k_st", [P, NH // HG, 2, S], BF16)
        v_all = sb("v_all", [P, NG, QT, HG, VW])
        v_st = sb("v_st", [P, 2, QT, HG, 32])
        mask = sb("mask", [P, NT, S], U8)
        mask_bf = sb("mask_bf", [P, QT, S], BF16)
        diag_masked = sb("diag_masked", [P, P], BF16)
        ctx_t = sb("ctx_t", [P, NH // HG, S])
        row_max = sb("row_max", [P, RING * HG])
        all_masked = sb("all_masked", [P, 3, NT])
        xt = sb("xt", [P, TOK])
        xn = sb("xn", [P, NT, D])
        zn = sb("zn", [P, NT, D])
        stats = sb("stats", [P, NT, 6])
        moments = sb("moments", [P, NT, 2])
        rstd = sb("rstd", [P, NT])
        minus_half = sb("minus_half", [P, QT])
        small = sb("small", [P, 64])
        ctx_r = sb("ctx_r", [P, 2, NH])
        ctx_n = sb("ctx_n", [P, QT, D])
        ctx_nt = sb("ctx_nt", [P, S])
        h_t = sb("h_t", [P, S])
        ff_g = sb("ff_g", [P, 2, S])
        ff_a = sb("ff_a", [P, FT, S])
        h3_t = sb("h3_t", [P, TOK])
        comb_t = ff_g[0:NE, :, :].rearrange("p a s -> p (a s)")
        eight = sb("eight", [NE, NE])
        route = sb("route", [P, 12, NT, NE])
        token = sb("token", [P, 8, NT])
        hot = sb("hot", [A, B, E0])
        hot_prod = sb("hot_prod", [A, 4, E0])
        style = sb("style", [P, 28])
        t_stats = sb("t_stats", [P, B, 6])
        t_mom = sb("t_mom", [P, B, 2])
        t_coef = sb("t_coef", [P, 4, B])
        b1_tanh, b1_half = style[:, 20:24], style[:, 24:28]

        with ExitStack() as scope:
            def shared(name, shape, dt=F32):
                return scope.enter_context(nc.sbuf_tensor(name, shape, dt))

            probs = shared("probs", [P, 2, HG, QT, S])
            ring = shared("ring", [P, RING, HG, S])
        with ExitStack() as scope:
            w_e = shared("w_e", [P, NE, 2, FF])
            hid = shared("hid", [P, 2, FT, S])
            w_hi = shared("w_hi", [P, NE, 2, FF])
            hid_hi = shared("hid_hi", [P, 2, FT, S])
            h3_parts = shared("h3_parts", [P, B, 2, S])
            gate = shared("gate", [P, 2, S])
            gates = shared("gates", [NE, 2, S])
        with ExitStack() as scope:
            w_rest = shared("w_rest", [P, NE, 2, FF])
            hid_rest = shared("hid_rest", [P, 2, FT, S])
        y_t = ctx_nt

        flat = probs[:, :, :, :, :].rearrange("p a h k s -> p (a h k s)")
        qk_f = [flat[:, 8192 * b:8192 * b + 2048].rearrange("p (n c) -> p n c", n=4) for b in range(B)]
        parts = [flat[:, 8192 * b + 2048:8192 * b + 3584].bitcast(BF16)
                 .rearrange("p (i n s) -> p i n s", i=2, n=PARTS) for b in range(B)]
        sel_prod = flat[0:A, 4096:4096 + B * A * E0].rearrange("p (b o e) -> p b o e", b=B, o=A)
        sel_w = flat[0:A, 5120:5120 + B * A].rearrange("p (b o) -> p b o", b=B)
        ad_h = flat[0:A, 6144:6144 + TOK]
        ad_e = flat[0:A + 1, 12288:12288 + TOK]
        rot_a, rot_b, rot_c = (flat[:, 13312 + 256 * i:13568 + 256 * i].rearrange("p (b d) -> p b d", b=B)
                               for i in range(3))
        swapped = flat[:, 14336:14336 + NT * D].rearrange("p (t d) -> p t d", t=NT)
        def rounded(ap):
            return ap.bitcast(F32R)

        in_xt = sems("in_xt")
        in_early, in_ids, in_angles, in_p32, in_up, in_rows, in_late, in_mask, in_eb2 = (
            sem(n) for n in ("in_early", "in_ids", "in_angles", "in_p32", "in_up", "in_rows", "in_late", 
                             "in_mask", "in_eb2"))
        bias_in = sems("bias_in", RING)
        experts_in = sems("experts_in", NE)
        stacks_out = sems("stacks_out")
        stack_in = sems("stack_in", NH // HG)
        dve_step, pool_step = sem("dve_step"), sem("pool_step")
        (ids_ready, trig_ready, sin_done, silu_exp_done, silu_ready, ada_done, ada_ready, sel_ready, down_done,
         gelu_ready, expert_done, expert_ready, up_done, ones_ready, rot_ready, swap_done) = (
            sem(n) for n in ("ids_ready", "trig_ready", "sin_done", "silu_exp_done", "silu_ready", "ada_done",
                             "ada_ready", "sel_ready", "down_done", "gelu_ready", "expert_done", "expert_ready",
                             "up_done", "ones_ready", "rot_ready", "swap_done"))
        var_ready, rstd_ready, norm_ready = sems("var_ready"), sems("rstd_ready"), sems("norm_ready")
        turned, affine_done = sems("turned"), sems("affine_done")
        qk_proj, qk_float, part_hi, rest_ready, part_mid, part_lo, v_proj, v_ready, v_pad, primed = (
            sem(n) for n in ("qk_proj", "qk_float", "part_hi", "rest_ready", "part_mid", "part_lo", "v_proj",
                             "v_ready", "v_pad", "primed"))
        seeded = sems("seeded", HG)
        (qk_done, sum_done, shift_done, tr_done, exp_done, v_staged, pv_done, ctx_copied, mask_bf_ready) = (
            sem(n) for n in ("qk_done", "sum_done", "shift_done", "tr_done", "exp_done", "v_staged", "pv_done",
                             "ctx_copied", "mask_bf_ready"))
        hyp_in, hyp_mm, abs_ready, softplus_exp, softplus_done, gam_ready = (
            sem(n) for n in ("hyp_in", "hyp_mm", "abs_ready", "softplus_exp", "softplus_done", "gam_ready"))
        (ctx_turned, ctx_scaled, ctx_back, ctx_back_copied, wo_done, ff1_done, ff_half, ff_ready,
         ff2_done, t_var, t_rstd, route_in, logits_done, logit_max, logit_exp, comb_ready, comb_turned, comb_t_ready,
         eb2_done, base_added) = (
            sems(n) for n in ("ctx_turned", "ctx_scaled", "ctx_back", "ctx_back_copied", "wo_done", "ff1_done",
                              "ff_half", "ff_ready", "ff2_done", "t_var", "t_rstd", "route_in",
                              "logits_done", "logit_max", "logit_exp", "comb_ready", "comb_turned", "comb_t_ready",
                              "eb2_done", "base_added"))
        gates_hi, gates_ready, h3_hi, h3_ready, y_copied, y_turned, y_added = (
            sems(n) for n in ("gates_hi", "gates_ready", "h3_hi", "h3_ready", "y_copied", "y_turned",
                              "y_added"))
        (hid_ready, eight_ready, w_hi_ready, w_ready, gate_done, gate_copied, up_e_done, hid_gated, hid_hi_ready,
         down_e_done, out_written) = (
            sem(n) for n in ("hid_ready", "eight_ready", "w_hi_ready", "w_ready", "gate_done", "gate_copied", "up_e_done",
                             "hid_gated", "hid_hi_ready", "down_e_done", "out_written"))

        block = ctx.enter_context(nc.Block())

        def wait(eng, semaphore, value):
            if value > 0:
                eng.wait_ge(semaphore, value)

        def chained(eng, semaphore):
            count = [0]

            def link(instruction):
                count[0] += 1
                instruction.then_inc(semaphore, 1)
                eng.wait_ge(semaphore, count[0])

            return link

        def half(b):
            return slice(QT * b, QT * b + QT)

        def tokens(b):
            return slice(S * b, S * b + S)

        def seeded_by_vector(unit, j):
            if j == 2:
                return unit % 2 == 1 if unit < UNITS // B else 2 * unit >= FINISH_AT[TURN_H]
            return j == 0

        def seeded_by_tensor(unit, j):
            return j == 3 and unit >= UNITS // B

        id_f, dom, wrap, style_hot, style_cmp = (small[:, 0:6], small[:, 6:8], small[:, 8:10], small[:, 10:12],
                                                 small[:, 12:14])
        valid, ada, trig_x, trig_k = small[:, 14:16], small[:, 16:20], small[:, 20:26], small[:, 26:32]
        trig, neg_sin = small[:, 32:42], small[:, 42:46]
        silu_e, silu = small[:, 46:48], small[:, 48:50]
        emb_b = small[0:A, 50:54]
        seT, hid1, hid2, hid3 = style[0:SE, 0:2], style[:, 2:4], style[:, 4:6], style[0:SE, 6:8]
        gam, bet, soft_a, soft_e, soft_l = (style[:, 8:10], style[:, 10:12], style[:, 12:14], style[:, 14:16],
                                            style[:, 16:18])

        @block.sync
        def _(sp):
            sp.dma_start(early[:, :], early_d).then_inc(in_early, 16)
            for b in range(B):
                sp.dma_start(xt[:, tokens(b)], x_t[:, tokens(b)]).then_inc(in_xt[b], 16)
            sp.dma_start(up[:, :], up_d).then_inc(in_up, 16)
            sp.dma_start(rows[:, :], rows_d.partition_broadcast(P)).then_inc(in_rows, 16)
            sp.dma_start(late[:, :], late_d).then_inc(in_late, 16)
            sp.dma_start(pack64[:, :], pack64_d).then_inc(in_late, 16)
            sp.dma_start(mask[:, :, :].rearrange("p (b t) k -> p b t k", b=B),
                         mask_d.rearrange("b (t p) k -> p b t k", p=P)).then_inc(in_mask, 16)

            def load_bias(unit):
                group, tile, slot = unit // QT, unit % QT, unit % RING
                sp.dma_start(ring[:, slot, :, :],
                             bias_d[group, :, tile * P:(tile + 1) * P, :].rearrange("h p k -> p h k")
                             ).then_inc(bias_in[slot], 16)

            def write_parts(b):
                for level, arrived in enumerate((part_hi, part_mid, part_lo)):
                    for kind, dram in enumerate((q_dram, k_dram)):
                        sp.wait_ge(arrived, 2 * b + kind + 1)
                        rows_of = (range(PARTS * level, min(PARTS * level + PARTS, PRODUCTS)) if kind == 0
                                   else range(level, PRODUCTS, PARTS))
                        dest = dram[b, rows_of.start:rows_of.stop:rows_of.step]
                        source = parts[b][:, kind, level:level + 1, :].to_broadcast([P, len(rows_of), S])
                        sp.dma_start(dest.rearrange("r d s -> d r s"), source).then_inc(stacks_out[b], 16)

            def load_stack(group):
                b, g = group // (NH // HG), group % (NH // HG)
                for stack, dram in ((q_st, q_dram), (k_st, k_dram)):
                    source = dram[b].rearrange("r (g h c t) s -> g h r c (t s)", g=NH // HG, h=2, c=DH)
                    for h in range(2):
                        sp.dma_start(stack[64 * h:64 * h + 64, g, :, :].rearrange("p t s -> p (t s)"),
                                     source[g, h]).then_inc(stack_in[g], 16)

            for u in range(RING):
                load_bias(u)
            sp.dma_start(eb2[:, :], eb2_d).then_inc(in_eb2, 16)
            write_parts(0)
            sp.wait_ge(stacks_out[0], 16 * 2 * PARTS)
            load_stack(0)
            load_stack(1)
            write_parts(1)
            load_stack(2)
            load_stack(3)
            sp.wait_ge(stacks_out[1], 16 * 2 * PARTS)
            for u in range(RING, UNITS):
                sp.wait_ge(tr_done, HG * (u - RING + 1))
                load_bias(u)
                group = (u + RING) // QT
                if (u + RING) % QT == 0 and NH // HG <= group < NG:
                    sp.wait_ge(qk_done, HG * QT * (group - NH // HG + 1))
                    load_stack(group)

            sp.wait_ge(pv_done, QT * (NG - 1))
            for e in range(NE):
                sp.dma_start(w_e[:, e, 0, :], w1_d[e]).then_inc(experts_in[e], 16)
                sp.dma_start(w_e[:, e, 1, :].rearrange("p (f d) -> p f d", f=FT),
                             w2_d[e].rearrange("(f p) d -> p f d", p=P)).then_inc(experts_in[e], 16)

            for b in range(B):
                sp.wait_ge(y_added[b], 1)
                sp.dma_start(out_d[b].rearrange("(t p) d -> p t d", p=P), xn[:, half(b), :]).then_inc(out_written, 16)
            sp.wait_ge(out_written, 32)

        @block.gpsimd
        def _(pool):
            link = chained(pool, pool_step)
            link(pool.memset(minus_half[:, :], -0.5))
            pool.memset(ad_e[A:A + 1, :], 1.0).then_inc(ones_ready, 1)
            pool.wait_ge(ones_ready, 1)

            pool.wait_ge(ids_ready, 1)
            pool.wait_ge(in_early, 16)
            link(pool.tensor_scalar(trig_x[:, 0:2], trig_x[:, 0:2], C["freq"], 0.0, ALU.mult, ALU.add))
            link(pool.tensor_scalar(trig_k, trig_x, 1 / (2 * math.pi), ROUND, ALU.mult, ALU.add))
            link(pool.tensor_scalar(trig_k, trig_k, ROUND, 0.0, ALU.subtract, ALU.add))
            for part in TWO_PI:
                link(pool.tensor_scalar(trig[:, 0:6], trig_k, -part, 0.0, ALU.mult, ALU.add))
                link(pool.tensor_tensor(trig_x, trig_x, trig[:, 0:6], ALU.add))
            link(pool.tensor_scalar(trig_x, trig_x, PI_BELOW, -PI_BELOW, ALU.min, ALU.max))
            link(pool.tensor_scalar(trig_k, trig_x, 0.0, 2.0, ALU.max, ALU.mult))
            link(pool.tensor_tensor(trig_k, trig_x, trig_k, ALU.subtract))
            link(pool.tensor_scalar(trig_k, trig_k, math.pi / 2, 0.0, ALU.add, ALU.add))
            link(pool.tensor_copy(trig[0:SE, 0:2], trig_x[0:SE, 0:2]))
            link(pool.tensor_copy(trig[SE:P, 0:2], trig_k[SE:P, 0:2]))
            pool.tensor_copy(trig[:, 2:6], trig_x[:, 2:6])
            pool.tensor_copy(trig[:, 6:10], trig_k[:, 2:6]).then_inc(trig_ready, 1)

            pool.wait_ge(in_rows, 16)
            pool.wait_ge(sin_done, 1)
            link(pool.tensor_scalar(neg_sin, trig[:, 2:6], -1.0, 0.0, ALU.mult, ALU.add))

            def quads(ap):
                return ap.rearrange("p (i q e) -> p i q e", q=2, e=2)

            gamma, beta = quads(R["gamma"]), quads(R["beta"])

            def rotation(b):
                ra, rb, rc = (quads(r[:, b, :]) for r in (rot_a, rot_b, rot_c))
                for q in range(2):
                    cos = trig[:, 6 + 2 * q + b:7 + 2 * q + b]
                    sines = trig[:, 2 + 2 * q + b:3 + 2 * q + b], neg_sin[:, 2 * q + b:2 * q + b + 1]
                    pool.tensor_scalar(ra[:, :, q, :], gamma[:, :, q, :], cos, 0.0, ALU.mult, ALU.add)
                    for e in range(2):
                        pool.tensor_scalar(rb[:, :, q, e], gamma[:, :, q, 1 - e], sines[e], 0.0, ALU.mult, ALU.add)
                        last = pool.tensor_scalar(quads(swapped[:, QT * b, :])[:, :, q, e], beta[:, :, q, 1 - e],
                                                  sines[e], 0.0, ALU.mult, ALU.add)
                    last = pool.tensor_scalar(rc[:, :, q, :], beta[:, :, q, :], cos, 0.0, ALU.mult, ALU.add)
                link(last)
                link(pool.tensor_tensor(rot_c[:, b, :], rot_c[:, b, :], swapped[:, QT * b, :], ALU.add))
                pool.tensor_copy(small[:, 55:56], minus_half[:, 0:1]).then_inc(rot_ready, 1)

            def inverse_root(b, n):
                pool.wait_ge(var_ready[b], n + 1)
                pool.tensor_tensor(rstd[:, half(b)], rstd[:, half(b)], minus_half[:, :], ALU.pow
                                   ).then_inc(rstd_ready[b], 1)

            def swap(b):
                pool.wait_ge(norm_ready[b], 1)
                z = zn[:, half(b), :].rearrange("p t (i e) -> p t i e", e=2)
                o = swapped[:, half(b), :].rearrange("p t (i e) -> p t i e", e=2)
                w = rot_b[:, b:b + 1, :].to_broadcast([P, QT, D]).rearrange("p t (i e) -> p t i e", e=2)
                for e in range(2):
                    last = pool.tensor_tensor(o[:, :, :, e], z[:, :, :, 1 - e], w[:, :, :, e], ALU.mult)
                last.then_inc(swap_done, 1)

            rotation(0)
            swap(0)
            rotation(1)
            swap(1)
            pool.memset(v_st[:, :, :, :, :], 0.0).then_inc(v_pad, 1)
            pool.memset(v_all[:, :, :, :, :], 1.0).then_inc(v_pad, 1)
            pool.wait_ge(in_mask, 16)
            pool.tensor_scalar(diag_masked[:, :], ident, MASKED, 0.0, ALU.mult, ALU.add)
            pool.tensor_copy(mask_bf[:, :, :], mask[:, half(1), :]).then_inc(mask_bf_ready, 1)

            def shift(unit, j):
                slot, n = unit % RING, (unit % RING) * HG + j
                pool.wait_ge(sum_done, HG * unit + j + 1)
                pool.tensor_scalar(ring[:, slot, j, :], ring[:, slot, j, :], -1.0, row_max[:, n:n + 1],
                                   ALU.mult, ALU.add).then_inc(shift_done, 1)

            def finish(b, step):
                if step in (PROJECT, FF2):
                    inverse_root(b, 2 if step == PROJECT else 3)
                if step == TURN_H3:
                    pool.wait_ge(t_var[b], 1)
                    pool.tensor_tensor(t_coef[:, 0, b:b + 1], t_coef[:, 0, b:b + 1], minus_half[:, 0:1], ALU.pow
                                       ).then_inc(t_rstd[b], 1)

            for s in range(UNITS + LAG + 2):
                for j in range(HG):
                    if s < UNITS:
                        shift(s, j)
                    if j % 2 and 2 * s + j // 2 - 1 in FINISH:
                        finish(0, FINISH[2 * s + j // 2 - 1])
            def rests(e):
                for layer in range(2):
                    pool.wait_ge(w_hi_ready, 2 * e + layer + 1)
                    pool.tensor_tensor(rounded(w_rest[:, e, layer, :]), w_e[:, e, layer, :], w_hi[:, e, layer, :],
                                       ALU.subtract).then_inc(w_ready, 1)

            for e in range(AHEAD):
                rests(e)
            for c in range(B * NE):
                if c + AHEAD < NE:
                    rests(c + AHEAD)
                for step in LATE_STEPS[2 * c:2 * c + 2]:
                    finish(1, step)

        @block.scalar
        def _(act):
            act.dma_start(ids_i[:, :], ids_d.partition_broadcast(P)).then_inc(in_ids, 16)
            act.dma_start(angles[:, :], ang_d.partition_broadcast(P)).then_inc(in_angles, 16)
            act.dma_start(pack32[:, :], pack32_d).then_inc(in_p32, 16)
            act.wait_ge(in_p32, 16)
            for b in range(B):
                act.wait_ge(down_done, b + 1)
                act.activation(ad_h[:, tokens(b)], bank[b][0:A, :], ACT.Gelu, bias=W32["down_b"]
                               ).then_inc(gelu_ready, 1)
            act.wait_ge(trig_ready, 1)
            act.activation(trig, trig, ACT.Sin).then_inc(sin_done, 1)
            act.wait_ge(sin_done, 1)
            act.activation(silu_e, trig[:, 0:2], ACT.Exp, scale=-1.0).then_inc(silu_exp_done, 1)

            def root(b, n):
                act.wait_ge(var_ready[b], n + 1)
                act.activation(rstd[:, half(b)], rstd[:, half(b)], ACT.Sqrt).then_inc(rstd_ready[b], 1)

            root(0, 0)
            act.wait_ge(in_late, 32)
            ps = bank[6]
            act.wait_ge(hyp_mm, 1)
            act.activation(seT, ps[0:SE, 0:2], ACT.Copy).then_inc(hyp_in, 1)
            act.wait_ge(hyp_mm, 2)
            act.activation(hid1, ps[:, 2:4], ACT.Relu, bias=L["hyp_b1"]).then_inc(hyp_in, 1)
            act.wait_ge(hyp_mm, 3)
            act.activation(hid2, ps[:, 4:6], ACT.Identity, bias=L["hyp_b2"]).then_inc(hyp_in, 1)
            act.wait_ge(hyp_mm, 4)
            act.activation(hid3, ps[0:SE, 6:8], ACT.Relu, bias=W64["sty_b1"]).then_inc(hyp_in, 1)
            act.wait_ge(hyp_mm, 5)
            act.activation(gam, ps[:, 8:10], ACT.Identity, bias=L["sty_b2"][:, 0:1])
            act.activation(bet, ps[:, 10:12], ACT.Identity, bias=L["sty_b2"][:, 1:2]).then_inc(hyp_in, 1)

            def affine(b):
                act.wait_ge(turned[b], 1)
                act.wait_ge(ada_ready, 1)
                act.activation(xt[:, tokens(b)], bank[(0, 4)[b]][:, :], ACT.Identity, bias=ada[:, 2 + b:3 + b],
                               scale=ada[:, b:b + 1]).then_inc(affine_done[b], 1)

            def split(b, level, arrived, done):
                for kind in range(2):
                    act.wait_ge(arrived, 2 * b + kind + 1)
                    act.activation(parts[b][:, kind, level, :], qk_f[b][:, 2 * kind + level, :], ACT.Copy
                                   ).then_inc(done, 1)

            root(0, 1)
            root(1, 0)
            affine(0)
            root(1, 1)
            split(0, 0, qk_float, part_hi)
            split(0, 1, rest_ready, part_mid)
            affine(1)
            split(1, 0, qk_float, part_hi)
            split(1, 1, rest_ready, part_mid)
            act.wait_ge(abs_ready, 1)
            act.activation(soft_e, soft_a, ACT.Exp, scale=-1.0).then_inc(softplus_exp, 1)
            act.wait_ge(softplus_exp, 1)
            act.activation(soft_l, soft_e, ACT.Ln, bias=1.0).then_inc(softplus_done, 1)

            def seed(unit, j):
                if unit == 0:
                    act.wait_ge(primed, 1)
                    act.wait_ge(in_mask, 16)
                else:
                    act.wait_ge(sum_done, HG * (unit - 1) + j + 1)
                act.activation(score_ps[j][:, :], mask[:, unit // (NG // B * QT) * QT + unit % QT, :], ACT.Copy,
                               scale=MASKED).then_inc(seeded[j], 1)

            def exp(unit, j):
                group, qt = unit // QT, unit % QT
                if qt == 0 and j == 0:
                    wait(act, pv_done, QT * (group - 1))
                if unit == QT and j == 0:
                    act.wait_ge(stacks_out[1], 16 * 2 * PARTS)
                act.wait_ge(tr_done, HG * unit + j + 1)
                act.activation(probs[:, group % 2, j, :, qt * P:(qt + 1) * P],
                               turned_ps[j % 2][:, :].rearrange("p (k q) -> p k q", k=QT),
                               ACT.Exp, scale=-1.0).then_inc(exp_done, 1)

            def copy_ctx(group):
                act.wait_ge(pv_done, QT * (group + 1))
                if group >= NG // B:
                    act.wait_ge(ctx_turned[0], 2)
                act.activation(ctx_t[:, group % (NG // B), :], ctx_ps[:, :], ACT.Copy).then_inc(ctx_copied, 1)

            def finish(b, step):
                if step == TURN_BACK:
                    act.wait_ge(ctx_back[b], 1)
                    wait(act, wo_done[0], b)
                    act.activation(ctx_nt[:, :], aux[b][:, :], ACT.Copy).then_inc(ctx_back_copied[b], 1)
                if step in (TURN_H, TURN_H3):
                    scale, offset = (L["g2"], L["beta2"]) if step == TURN_H else (L["ln_g"], L["ln_b"])
                    act.wait_ge(turned[b], 2 if step == TURN_H else 3)
                    act.activation(h_t[:, :], aux[b][:, :], ACT.Identity, bias=offset, scale=scale
                                   ).then_inc(affine_done[b], 1)
                if step in (FF1_0, FF1_1, FF1_2, FF1_3):
                    f = step - FF1_0
                    act.wait_ge(ff1_done[b], f + 1)
                    wait(act, ff_ready[b], f - 1)
                    act.activation(ff_g[:, f % 2, :], aux[b][:, :], ACT.Tanh, bias=b1_tanh[:, f:f + 1], scale=0.851)
                    wait(act, ff2_done[0], b)
                    act.activation(ff_a[:, f, :], aux[b][:, :], ACT.Identity, bias=b1_half[:, f:f + 1], scale=0.5
                                   ).then_inc(ff_half[b], 1)
                if step == ROUTE:
                    act.wait_ge(route_in[b], 1)
                    act.wait_ge(tr_done, HG * UNITS)
                    act.activation(rounded(h3_parts[:, b, 0, :]), h3_t[:, tokens(b)], ACT.Copy).then_inc(h3_hi[b], 1)
                    act.wait_ge(logit_max[b], 1)
                    act.activation(route[:, 1, half(b), :], route[:, 0, half(b), :], ACT.Exp).then_inc(logit_exp[b], 1)
                if step == TURN_GATES:
                    act.wait_ge(comb_t_ready[b], 1)
                    wait(act, gate_done, NE * b)
                    act.activation(rounded(gates[:, 0, :]), comb_t[:, tokens(b)], ACT.Copy).then_inc(gates_hi[b], 1)

            for j in range(HG):
                if not seeded_by_vector(0, j):
                    seed(0, j)
            for s in range(UNITS + LAG + 2):
                if s % QT == 1 and s >= 2 * QT:
                    copy_ctx(s // QT - 2)
                for j in range(HG):
                    if 1 <= s <= UNITS:
                        exp(s - 1, j)
                    if s + 1 < UNITS and not seeded_by_vector(s + 1, j) and not seeded_by_tensor(s + 1, j):
                        seed(s + 1, j)
                    if j % 2 and 2 * s + j // 2 - 1 in FINISH:
                        finish(0, FINISH[2 * s + j // 2 - 1])
                if s % QT == 2 and s // QT < NG:
                    group = s // QT
                    wait(act, pv_done, QT * (group - 1))
                    act.wait_ge(v_ready, group // (NG // B) + 1)
                    act.wait_ge(v_pad, 1)
                    act.activation(v_st[:, group % 2, :, :, 0:VW].rearrange("p k h c -> p (k h) c"),
                                   v_all[:, group, :, :, :].rearrange("p k h c -> p (k h) c"),
                                   ACT.Copy).then_inc(v_staged, 1)

            def high_parts(e):
                act.wait_ge(experts_in[e], 32)
                act.wait_ge(pv_done, QT * NG)
                for layer in range(2):
                    act.activation(rounded(w_hi[:, e, layer, :]), w_e[:, e, layer, :], ACT.Copy
                                   ).then_inc(w_hi_ready, 1)

            def copy_gate(c):
                act.wait_ge(gate_done, c + 1)
                wait(act, hid_gated, (c - 1) * FT)
                act.activation(gate[:, c % 2, :], bank[6][:, :], ACT.Copy).then_inc(gate_copied, 1)

            def hidden(c):
                for f in range(FT):
                    act.wait_ge(hid_gated, c * FT + f + 1)
                    act.activation(rounded(hid_hi[:, c % 2, f, :]), hid[:, c % 2, f, :], ACT.Relu
                                   ).then_inc(hid_hi_ready, 1)

            def copy_y(b):
                act.wait_ge(down_e_done, NE * (b + 1))
                wait(act, y_turned[0], b)
                act.activation(y_t[:, :], bank[4 + b][:, :], ACT.Copy).then_inc(y_copied[b], 1)

            for e in range(AHEAD):
                high_parts(e)
            for step in STEPS[len(FINISH_AT):]:
                finish(0, step)
            copy_gate(0)
            for c in range(B * NE):
                if c + AHEAD < NE:
                    high_parts(c + AHEAD)
                if c + 1 < B * NE:
                    copy_gate(c + 1)
                hidden(c)
                if c == NE:
                    copy_y(0)
                for step in LATE_STEPS[2 * c:2 * c + 2]:
                    finish(1, step)
            copy_y(1)

        @block.tensor
        def _(pe):
            def turn(b, dest):
                for t in range(QT):
                    last = pe.transpose(dest[:, t * P:(t + 1) * P], zn[:, QT * b + t, :], ident)
                last.then_inc(turned[b], 1)

            pe.wait_ge(in_early, 16)
            for b in range(B):
                pe.wait_ge(in_xt[b], 16)
                pe.matmul(bank[b][0:A, :], C["down"], xt[:, tokens(b)], start=True, stop=True).then_inc(down_done, 1)
            for b in range(B):
                for t in range(QT):
                    at = (QT * b + t) * P
                    pe.matmul(bank[4 + b][:, t * P:(t + 1) * P], xt[:, at:at + P], ident, start=(t == 0), stop=False,
                              skip_group_check=True)
            pe.wait_ge(in_up, 16)
            pe.wait_ge(ones_ready, 1)
            for b in range(B):
                pe.wait_ge(sel_ready, b + 1)
                pe.wait_ge(gelu_ready, b + 1)
                pe.matmul(bank[2 + b][0:A, :], sel_w[:, b, :], ad_h[:, tokens(b)], start=True, stop=True
                          ).then_inc(expert_done, 1)
                pe.wait_ge(expert_ready, b + 1)
                for t in range(QT):
                    at = (QT * b + t) * P
                    last = pe.matmul(bank[4 + b][:, t * P:(t + 1) * P], ad_e[:, at:at + P], up[:, :],
                                     start=False, stop=(t == QT - 1), skip_group_check=True)
                last.then_inc(up_done, 1)
            pe.wait_ge(in_late, 32)
            pe.wait_ge(silu_ready, 1)
            for i in range(2):
                last = pe.matmul(bank[7][:, 2 * i:2 * i + 2], L["w_ada"][:, i * D:(i + 1) * D], silu,
                                 start=True, stop=True)
            last.then_inc(ada_done, 1)
            pe.wait_ge(in_p32, 16)
            steps = ((SE, W32["subj"], style_hot[0:SUBJ, :]), (P, W64["hyp_w1"], seT), (P, L["hyp_w2"], hid1),
                     (SE, L["sty_w1"], hid2))
            for i, (m, w, x) in enumerate(steps):
                pe.wait_ge(hyp_in, i + 1)
                pe.matmul(bank[6][0:m, 2 * i:2 * i + 2], w, x, start=True, stop=True).then_inc(hyp_mm, 1)
            pe.wait_ge(hyp_in, 5)
            for i in range(2):
                last = pe.matmul(bank[6][:, 8 + 2 * i:10 + 2 * i], W64["sty_w2"][:, i * D:(i + 1) * D], hid3,
                                 start=True, stop=True)
            last.then_inc(hyp_mm, 1)
            for b in range(B):
                pe.wait_ge(norm_ready[b], 2)
                turn(b, bank[(0, 4)[b]])
                pe.wait_ge(affine_done[b], 1)
                if b == 1:
                    pe.wait_ge(hyp_in, 6)
                for w, ps in (("wq", bank[(2, 5)[b]]), ("wk", bank[(3, 6)[b]])):
                    pe.matmul(ps[:, :], L[w], xt[:, tokens(b)], start=True, stop=True).then_inc(qk_proj, 1)
                for t in range(QT):
                    at = (QT * b + t) * P
                    last = pe.matmul(bank[(1, 7)[b]][:, t * P:(t + 1) * P], xt[:, at:at + P], L["wv"],
                                     start=True, stop=True)
                last.then_inc(v_proj, 1)
            pe.wait_ge(part_hi, 1)
            pe.wait_ge(qk_float, 2)
            pe.wait_ge(v_ready, 1)
            for j in range(HG):
                last = pe.matmul(score_ps[j][:, :], parts[0][:, 0, 0, 0:P], parts[0][:, 0, 0, :],
                                 start=True, stop=True)
            last.then_inc(primed, 1)

            def score(unit, j):
                group, qt, rows_of = unit // QT, unit % QT, slice(64 * (j % 2), 64 * (j % 2) + 64)
                if seeded_by_tensor(unit, j):
                    pe.wait_ge(sum_done, HG * (unit - 1) + j + 1)
                    pe.wait_ge(mask_bf_ready, 1)
                    pe.matmul(score_ps[j][:, :], diag_masked[:, :], mask_bf[:, qt, :], start=True, stop=False,
                              skip_group_check=True)
                else:
                    pe.wait_ge(seeded[j], unit + 1)
                if qt == 0 and j == 0:
                    pe.wait_ge(stack_in[group % (NH // HG)], 64 * (group // (NH // HG) + 1))
                pe.matmul(score_ps[j][:, :], q_st[rows_of, group % (NH // HG), j // 2, qt * P:(qt + 1) * P],
                          k_st[rows_of, group % (NH // HG), j // 2, :], start=False, stop=True,
                          skip_group_check=True).then_inc(qk_done, 1)

            def turn_scores(unit, j):
                pe.wait_ge(shift_done, HG * unit + j + 1)
                wait(pe, exp_done, HG * unit + j - 1)
                for k in range(QT):
                    last = pe.transpose(turned_ps[j % 2][:, k * P:(k + 1) * P],
                                        ring[:, unit % RING, j, k * P:(k + 1) * P], ident)
                last.then_inc(tr_done, 1)

            def values(group, k):
                if k == 0:
                    pe.wait_ge(exp_done, HG * QT * (group + 1))
                    pe.wait_ge(v_staged, group + 1)
                    wait(pe, ctx_copied, group)
                for j in range(HG):
                    last = pe.matmul(ctx_ps[32 * j:32 * j + 32, :], v_st[:, group % 2, k, j, :],
                                     probs[:, group % 2, j, k, :], start=(k == 0), stop=(k == QT - 1))
                last.then_inc(pv_done, 1)

            def finish(b, step):
                if step in (TURN_CTX0, TURN_CTX1):
                    part = step - TURN_CTX0
                    pe.wait_ge(ctx_copied, NG // B * (b + 1))
                    wait(pe, ctx_scaled[b], part)
                    wait(pe, exp_done, HG * UNITS * b)
                    kept = ident.rearrange("p (h c) -> p h c", c=32)[:, :, 0:VW]
                    for t in range(2):
                        at = (2 * part + t) * P
                        for g in range(NH // HG):
                            to = (t * (NH // HG) + g) * HG * VW
                            last = pe.matmul(aux[b][:, to:to + HG * VW].rearrange("p (h c) -> p h c", c=VW),
                                             ctx_t[:, g, at:at + P], kept, start=True, stop=True)
                    last.then_inc(ctx_turned[b], 1)
                if step == TURN_BACK:
                    pe.wait_ge(ctx_scaled[b], 2)
                    for t in range(QT):
                        last = pe.transpose(aux[b][:, t * P:(t + 1) * P], ctx_n[:, t, :], ident)
                    last.then_inc(ctx_back[b], 1)
                if step == PROJECT:
                    pe.wait_ge(ctx_back_copied[b], 1)
                    for t in range(QT):
                        at, dest = (QT * b + t) * P, aux[b][:, t * P:(t + 1) * P]
                        pe.matmul(dest, xt[:, at:at + P], ident, start=True, stop=False)
                        last = pe.matmul(dest, ctx_nt[:, t * P:(t + 1) * P], L["wo"], start=False, stop=True)
                    last.then_inc(wo_done[b], 1)
                if step in (TURN_H, TURN_H3):
                    pe.wait_ge(norm_ready[b], 3 if step == TURN_H else 4)
                    turn(b, aux[b])
                if step in (FF1_0, FF1_1, FF1_2, FF1_3):
                    f = step - FF1_0
                    pe.wait_ge(affine_done[b], 2)
                    wait(pe, ff_half[b], f)
                    pe.matmul(aux[b][:, :], L["w1"][:, f * P:(f + 1) * P], h_t[:, :], start=True, stop=True
                              ).then_inc(ff1_done[b], 1)
                if step == FF2:
                    pe.wait_ge(ff_ready[b], FT)
                    for t in range(QT):
                        for f in range(FT):
                            last = pe.matmul(aux[b][:, t * P:(t + 1) * P], ff_a[:, f, t * P:(t + 1) * P],
                                             L["w2"][:, f * P:(f + 1) * P], start=(f == 0), stop=(f == FT - 1))
                    last.then_inc(ff2_done[b], 1)
                if step == ROUTE:
                    pe.wait_ge(route_in[b], 1)
                    for t in range(QT):
                        last = pe.matmul(aux[b][:, t * NE:(t + 1) * NE], h3_t[:, (QT * b + t) * P:(QT * b + t + 1) * P],
                                         L["router"], start=True, stop=True)
                    last.then_inc(logits_done[b], 1)
                if step == TURN_GATES:
                    pe.wait_ge(comb_ready[b], 1)
                    for t in range(QT):
                        last = pe.transpose(aux[b][0:NE, t * P:(t + 1) * P], route[:, 11, QT * b + t, :], ident)
                    last.then_inc(comb_turned[b], 1)
                if step == GATED_BIAS:
                    pe.wait_ge(comb_t_ready[b], 1)
                    pe.wait_ge(in_eb2, 16)
                    for t in range(QT):
                        last = pe.matmul(aux[b][:, t * P:(t + 1) * P], comb_t[:, (QT * b + t) * P:(QT * b + t + 1) * P],
                                         eb2[:, :], start=True, stop=True)
                    last.then_inc(eb2_done[b], 1)

            pe.wait_ge(qk_float, 4)
            pe.wait_ge(v_ready, 2)
            for s in range(UNITS + LAG):
                for j in (0, 2):
                    if s < UNITS:
                        score(s, j)
                        score(s, j + 1)
                    if 1 <= s <= UNITS:
                        turn_scores(s - 1, j)
                        turn_scores(s - 1, j + 1)
                    if j == 2 and s >= LAG:
                        values((s - LAG) // QT, (s - LAG) % QT)
                    if 2 * s + j // 2 in FINISH:
                        finish(0, FINISH[2 * s + j // 2])

            def product(out, w, w_rest, x, x_rest, first, last):
                pe.matmul(out, rounded(w), rounded(x), start=first, stop=False)
                pe.matmul(out, rounded(w_rest), rounded(x), start=False, stop=False)
                return pe.matmul(out, rounded(w), rounded(x_rest), start=False, stop=last)

            def spread_gates(c):
                b, e = c // NE, c % NE
                pe.wait_ge(gates_ready[b], 1)
                pe.wait_ge(eight_ready, 1)
                wait(pe, gate_copied, c)
                row = rounded(eight[:, e:e + 1]).to_broadcast([NE, P])
                pe.matmul(bank[6][:, :], row, rounded(gates[:, 0, :]), start=True, stop=False)
                pe.matmul(bank[6][:, :], row, rounded(gates[:, 1, :]), start=False, stop=True).then_inc(gate_done, 1)

            def layer1(c):
                b, e = c // NE, c % NE
                pe.wait_ge(h3_ready[b], 1)
                pe.wait_ge(w_ready, 2 * e + 1)
                if c == 0:
                    pe.wait_ge(sum_done, HG * UNITS)
                for f in range(FT):
                    wait(pe, hid_gated, (c - 1) * FT + f + 1)
                    cols = slice(f * P, (f + 1) * P)
                    product(bank[f][:, :], w_hi[:, e, 0, cols], w_rest[:, e, 0, cols], h3_parts[:, b, 0, :],
                            h3_parts[:, b, 1, :], True, True).then_inc(up_e_done, 1)

            def layer2(c):
                b, e = c // NE, c % NE
                pe.wait_ge(w_ready, 2 * e + 2)
                for f in range(FT):
                    pe.wait_ge(hid_ready, c * FT + f + 1)
                    cols = slice(f * P, (f + 1) * P)
                    last = product(bank[4 + b][:, :], w_hi[:, e, 1, cols], w_rest[:, e, 1, cols], hid_hi[:, c % 2, f, :],
                                   hid_rest[:, c % 2, f, :], e == 0 and f == 0, e == NE - 1 and f == FT - 1)
                last.then_inc(down_e_done, 1)

            def turn_out(b):
                pe.wait_ge(y_copied[b], 1)
                for t in range(QT):
                    last = pe.transpose(bank[4 + b][:, t * P:(t + 1) * P], y_t[:, t * P:(t + 1) * P], ident)
                last.then_inc(y_turned[b], 1)

            finish(1, TURN_CTX0)
            finish(1, TURN_CTX1)
            finish(0, TURN_GATES)
            layer1(0)
            spread_gates(0)
            finish(0, GATED_BIAS)
            spread_gates(1)
            for c in range(B * NE):
                if c + 1 < B * NE:
                    layer1(c + 1)
                if c + 2 < B * NE:
                    spread_gates(c + 2)
                if c == NE:
                    turn_out(0)
                for step in LATE_STEPS[2 * c:2 * c + 1]:
                    finish(1, step)
                layer2(c)
                for step in LATE_STEPS[2 * c + 1:2 * c + 2]:
                    finish(1, step)
            turn_out(1)

        @block.vector
        def _(dve):
            link = chained(dve, dve_step)

            dve.wait_ge(in_ids, 16)
            link(dve.tensor_copy(id_f, ids_i[:, :]))
            dve.tensor_scalar(trig_x[:, 0:2], id_f[:, 2:4], 0.01, 4000.0, ALU.mult, ALU.mult)
            dve.wait_ge(in_angles, 16)
            dve.tensor_copy(trig_x[:, 2:6], angles[:, :]).then_inc(ids_ready, 1)

            link(dve.tensor_scalar(dom, id_f[:, 0:2], 0.0, float(E0 - 1), ALU.max, ALU.min))
            link(dve.tensor_tensor(valid, dom, id_f[:, 0:2], ALU.is_equal))
            dve.wait_ge(in_early, 16)
            dve.wait_ge(in_p32, 16)
            for b in range(B):
                link(dve.tensor_scalar(hot[:, b, :], C["iota16"][0:A, :], dom[0:A, b:b + 1], None, ALU.is_equal))
                link(dve.tensor_tensor(sel_prod[:, b, :, :],
                                       W32["expert_w"].rearrange("a (o e) -> a o e", e=E0),
                                       hot[:, b:b + 1, :].to_broadcast([A, A, E0]), ALU.mult))
                link(dve.tensor_reduce(sel_w[:, b, :], sel_prod[:, b, :, :], AX_X, ALU.add))
                link(dve.tensor_tensor(sel_w[:, b, :], sel_w[:, b, :], W32["eye"], ALU.subtract))
                dve.scalar_tensor_tensor(sel_w[:, b, :], sel_w[:, b, :], valid[0:A, b:b + 1], W32["eye"],
                                         ALU.mult, ALU.add).then_inc(sel_ready, 1)
                dve.tensor_tensor(hot_prod[:, 2 * b, :], W32["expert_b"], hot[:, b, :], ALU.mult)
                link(dve.tensor_tensor(hot_prod[:, 2 * b + 1, :], W32["emb"], hot[:, b, :], ALU.mult))
                link(dve.tensor_reduce(emb_b[:, 2 * b:2 * b + 2], hot_prod[:, 2 * b:2 * b + 2, :], AX_X, ALU.add))
                link(dve.scalar_tensor_tensor(emb_b[:, 2 * b:2 * b + 1], emb_b[:, 2 * b:2 * b + 1],
                                              valid[0:A, b:b + 1], emb_b[:, 2 * b + 1:2 * b + 2],
                                              ALU.mult, ALU.add))
            link(dve.tensor_scalar(wrap, id_f[:, 4:6], 0.0, float(SUBJ), ALU.is_lt, ALU.mult))
            link(dve.tensor_tensor(style_cmp, id_f[:, 4:6], wrap, ALU.add))
            link(dve.tensor_scalar(style_cmp, style_cmp, 0.0, float(SUBJ - 1), ALU.max, ALU.min))
            dve.tensor_scalar(style_hot, style_cmp, C["row"], None, ALU.is_equal).then_inc(hyp_in, 1)

            def expert_out(b):
                dve.wait_ge(expert_done, b + 1)
                dve.tensor_scalar(ad_e[0:A, tokens(b)], bank[2 + b][0:A, :], emb_b[:, 2 * b:2 * b + 1],
                                  None, ALU.add).then_inc(expert_ready, 1)

            def moments_of(b, source=xn[:, :, :], first=0):
                for t in range(QT * b, QT * b + QT):
                    last = dve.bn_stats(stats[:, t, :], source[:, t - QT * b + first, :])
                link(last)
                for t in range(QT * b, QT * b + QT):
                    last = dve.bn_aggr(moments[:, t, :], stats[:, t, :])
                link(last)
                dve.tensor_scalar(rstd[:, half(b)], moments[:, half(b), 1], LN_EPS, None, ALU.add
                                  ).then_inc(var_ready[b], 1)

            def normalise(b, n):
                dve.wait_ge(rstd_ready[b], n + 1)
                if n < 2:
                    link(dve.reciprocal(rstd[:, half(b)], rstd[:, half(b)]))
                for t in range(QT * b, QT * b + QT):
                    source = tiles_of(bank[4 + b])[:, t - QT * b, :] if n == 0 else xn[:, t, :]
                    last = dve.tensor_scalar(zn[:, t, :], source, moments[:, t, 0:1], rstd[:, t:t + 1],
                                             ALU.subtract, ALU.mult)
                last.then_inc(norm_ready[b], 1)

            def tiles_of(ps):
                return ps[:, :].rearrange("p (t d) -> p t d", t=QT)

            def adapter_out(b):
                dve.wait_ge(up_done, b + 1)
                moments_of(b, tiles_of(bank[4 + b]))

            def rotate(b):
                dve.wait_ge(norm_ready[b], 1)
                dve.wait_ge(rot_ready, b + 1)
                link(dve.tensor_tensor(xn[:, half(b), :], zn[:, half(b), :],
                                       rot_a[:, b:b + 1, :].to_broadcast([P, QT, D]), ALU.mult))
                link(dve.tensor_tensor(xn[:, half(b), :], xn[:, half(b), :],
                                       rot_c[:, b:b + 1, :].to_broadcast([P, QT, D]), ALU.add))
                dve.wait_ge(swap_done, b + 1)
                link(dve.tensor_tensor(xn[:, half(b), :], xn[:, half(b), :], swapped[:, half(b), :], ALU.add))
                moments_of(b, first=QT * b)

            def q_and_k(b):
                for kind, (bias, scale) in enumerate(((L["bq"], 1 / math.sqrt(DH)), (L["bk"], 1.0))):
                    dve.wait_ge(qk_proj, 2 * b + kind + 1)
                    dve.tensor_scalar(qk_f[b][:, 2 * kind, :], bank[((2, 3), (5, 6))[b][kind]][:, :], bias, scale,
                                      ALU.add, ALU.mult).then_inc(qk_float, 1)

            def split(b, level, arrived, done):
                for kind in range(2):
                    dve.wait_ge(arrived, 2 * b + kind + 1)
                    dest = parts[b][:, kind, 2, :] if level else qk_f[b][:, 2 * kind + 1, :]
                    dve.tensor_tensor(dest, qk_f[b][:, 2 * kind + level, :], parts[b][:, kind, level, :],
                                      ALU.subtract).then_inc(done, 1)

            def values_of(b):
                dve.wait_ge(v_pad, 2)
                dve.wait_ge(v_proj, b + 1)
                for k in range(QT):
                    last = dve.tensor_tensor(
                        v_all[:, (NH // HG) * b:(NH // HG) * (b + 1), k, :, 0:DH],
                        bank[(1, 7)[b]][:, k * P:(k + 1) * P].rearrange("p (g h c) -> p g h c", g=NH // HG, h=HG),
                        R["bv"].rearrange("p (g h c) -> p g h c", g=NH // HG, h=HG), ALU.add)
                last.then_inc(v_ready, 1)

            expert_out(0)
            adapter_out(0)
            expert_out(1)
            dve.wait_ge(silu_exp_done, 1)
            link(dve.tensor_scalar(silu, silu_e, 1.0, None, ALU.add))
            link(dve.reciprocal(silu, silu))
            dve.tensor_tensor(silu, silu, trig[:, 0:2], ALU.mult).then_inc(silu_ready, 1)
            normalise(0, 0)
            rotate(0)
            adapter_out(1)
            normalise(0, 1)
            dve.wait_ge(ada_done, 1)
            link(dve.tensor_scalar(ada[:, 0:2], bank[7][:, 0:2], L["b_ada"][:, 0:1], 1.0, ALU.add, ALU.add))
            dve.tensor_scalar(ada[:, 2:4], bank[7][:, 2:4], L["b_ada"][:, 1:2], None, ALU.add
                              ).then_inc(ada_ready, 1)
            normalise(1, 0)
            rotate(1)
            q_and_k(0)
            normalise(1, 1)
            split(0, 0, part_hi, rest_ready)
            split(0, 1, part_mid, part_lo)
            values_of(0)
            dve.wait_ge(hyp_in, 6)
            dve.scalar_tensor_tensor(soft_a, gam, -1.0, gam, ALU.mult, ALU.max).then_inc(abs_ready, 1)
            dve.tensor_scalar(b1_tanh[:, :], L["b1"], 0.851, None, ALU.mult)
            link(dve.tensor_scalar(b1_half[:, :], L["b1"], 0.5, None, ALU.mult))
            q_and_k(1)
            split(1, 0, part_hi, rest_ready)
            split(1, 1, part_mid, part_lo)
            values_of(1)

            def seed(unit, j):
                if unit == 0:
                    dve.wait_ge(primed, 1)
                    dve.wait_ge(in_mask, 16)
                else:
                    dve.wait_ge(sum_done, HG * (unit - 1) + j + 1)
                dve.tensor_scalar(score_ps[j][:, :], mask[:, unit // (NG // B * QT) * QT + unit % QT, :], MASKED, None,
                                  ALU.mult).then_inc(seeded[j], 1)

            def add_bias(unit, j):
                slot, n = unit % RING, (unit % RING) * HG + j
                if j == 0:
                    dve.wait_ge(bias_in[slot], 16 * (unit // RING + 1))
                dve.wait_ge(qk_done, HG * unit + j + 1)
                dve.tensor_tensor_reduce(ring[:, slot, j, :], score_ps[j][:, :], ring[:, slot, j, :], 1.0,
                                         -3.0e38, ALU.add, ALU.max, row_max[:, n:n + 1]).then_inc(sum_done, 1)

            def rt(b, i):
                return route[:, i, half(b), :]

            def tok(b, i):
                return token[:, i, half(b)]

            def per_token(ap):
                return ap.unsqueeze(2).to_broadcast([P, QT, NE])

            def top_two(b):
                dve.wait_ge(logit_exp[b], 1)
                link(dve.tensor_reduce(tok(b, 1), rt(b, 1), AX_X, ALU.add))
                link(dve.reciprocal(tok(b, 1), tok(b, 1)))
                link(dve.tensor_tensor(rt(b, 2), rt(b, 1), per_token(tok(b, 1)), ALU.mult))
                order = C["iota16"][:, 0:NE].unsqueeze(1).to_broadcast([P, QT, NE])
                left = rt(b, 2)
                for i in range(2):
                    top, first = tok(b, 2 + i), tok(b, 4 + i)
                    equal, key, hot_e = rt(b, 3 + 4 * i), rt(b, 4 + 4 * i), rt(b, 5 + 4 * i)
                    link(dve.tensor_reduce(top, left, AX_X, ALU.max))
                    link(dve.tensor_tensor(equal, left, per_token(top), ALU.is_equal))
                    link(dve.scalar_tensor_tensor(key, equal, 100.0, order, ALU.mult, ALU.subtract))
                    link(dve.tensor_reduce(first, key, AX_X, ALU.max))
                    link(dve.tensor_tensor(hot_e, key, per_token(first), ALU.is_equal))
                    if i == 0:
                        link(dve.scalar_tensor_tensor(rt(b, 6), hot_e, -2.0, left, ALU.mult, ALU.add))
                        left = rt(b, 6)
                link(dve.tensor_tensor(tok(b, 6), tok(b, 2), tok(b, 3), ALU.add))
                link(dve.reciprocal(tok(b, 6), tok(b, 6)))
                link(dve.tensor_tensor(rt(b, 10), rt(b, 5), rt(b, 9), ALU.add))
                link(dve.tensor_tensor(rt(b, 10), rt(b, 10), rt(b, 2), ALU.mult))
                dve.tensor_tensor(rt(b, 11), rt(b, 10), per_token(tok(b, 6)), ALU.mult).then_inc(comb_ready[b], 1)

            def finish(b, step):
                residual = xn[:, half(b), :]
                if step in (TURN_CTX0, TURN_CTX1):
                    part = step - TURN_CTX0
                    dve.wait_ge(ctx_turned[b], part + 1)
                    t0 = 2 * part
                    context = aux[b][:, 0:2 * NH * VW].rearrange("p (h c) -> p h c", c=VW)
                    r = ctx_r[:, :, :].rearrange("p t h -> p (t h)")
                    link(dve.reciprocal(r, context[:, :, DH]))
                    link(dve.tensor_tensor(ctx_r[:, :, :], ctx_r[:, :, :],
                                           all_masked[:, 2, QT * b + t0:QT * b + t0 + 2].unsqueeze(2)
                                           .to_broadcast([P, 2, NH]), ALU.add))
                    link(dve.tensor_tensor(ctx_n[:, t0:t0 + 2, :].rearrange("p t (h c) -> p (t h) c", c=DH),
                                           context[:, :, 0:DH], r.unsqueeze(2).to_broadcast([P, 2 * NH, DH]),
                                           ALU.mult))
                    dve.tensor_copy(small[:, 54:55], ctx_r[:, 0, 0:1]).then_inc(ctx_scaled[b], 1)
                if step == PROJECT:
                    dve.wait_ge(wo_done[b], 1)
                    link(dve.tensor_tensor(residual, tiles_of(aux[b]), R["bo"].unsqueeze(1).to_broadcast([P, QT, D]),
                                           ALU.add))
                    moments_of(b, first=QT * b)
                if step == FF2:
                    dve.wait_ge(ff2_done[b], 1)
                    link(dve.tensor_tensor(residual, tiles_of(aux[b]), residual, ALU.add))
                    moments_of(b, first=QT * b)
                if step == ROUTE:
                    dve.wait_ge(logits_done[b], 1)
                    logits = aux[b][:, 0:QT * NE].rearrange("p (t e) -> p t e", e=NE)
                    link(dve.tensor_reduce(tok(b, 0), logits, AX_X, ALU.max))
                    dve.tensor_tensor(rt(b, 0), logits, per_token(tok(b, 0)), ALU.subtract).then_inc(logit_max[b], 1)
                if step == TURN_GATES:
                    dve.wait_ge(comb_turned[b], 1)
                    dve.tensor_copy(comb_t[:, tokens(b)], aux[b][0:NE, :]).then_inc(comb_t_ready[b], 1)
                if step == GATED_BIAS:
                    dve.wait_ge(eb2_done[b], 1)
                    dve.tensor_tensor(residual, tiles_of(aux[b]), residual, ALU.add).then_inc(base_added[b], 1)

            def settle(b, step):
                if step == PROJECT:
                    normalise(b, 2)
                if step in (FF1_0, FF1_1, FF1_2, FF1_3):
                    f = step - FF1_0
                    dve.wait_ge(ff_half[b], f + 1)
                    dve.scalar_tensor_tensor(ff_a[:, f, :], ff_g[:, f % 2, :], 1.0, ff_a[:, f, :],
                                             ALU.add, ALU.mult).then_inc(ff_ready[b], 1)
                if step == FF1_0:
                    dve.wait_ge(norm_ready[b], 3)
                    link(dve.tensor_tensor(xn[:, half(b), :], xn[:, half(b), :],
                                           R["b2"].unsqueeze(1).to_broadcast([P, QT, D]), ALU.add))
                if step == FF2:
                    normalise(b, 3)
                if step == TURN_H3:
                    dve.wait_ge(affine_done[b], 3)
                    link(dve.bn_stats(t_stats[:, b, :], h_t[:, :]))
                    link(dve.bn_aggr(t_mom[:, b, :], t_stats[:, b, :]))
                    dve.tensor_scalar(t_coef[:, 0, b:b + 1], t_mom[:, b, 1:2], 1e-8, None, ALU.add
                                      ).then_inc(t_var[b], 1)
                    dve.wait_ge(t_rstd[b], 1)
                    link(dve.tensor_tensor(t_coef[:, 1, b:b + 1], t_coef[:, 0, b:b + 1], gam[:, b:b + 1], ALU.mult))
                    link(dve.tensor_tensor(t_coef[:, 2, b:b + 1], t_coef[:, 1, b:b + 1], t_mom[:, b, 0:1], ALU.mult))
                    link(dve.tensor_tensor(t_coef[:, 3, b:b + 1], bet[:, b:b + 1], t_coef[:, 2, b:b + 1],
                                           ALU.subtract))
                    dve.tensor_scalar(h3_t[:, tokens(b)], h_t[:, :], t_coef[:, 1, b:b + 1], t_coef[:, 3, b:b + 1],
                                      ALU.mult, ALU.add).then_inc(route_in[b], 1)
                if step == ROUTE:
                    dve.wait_ge(h3_hi[b], 1)
                    dve.tensor_tensor(rounded(h3_parts[:, b, 1, :]), h3_t[:, tokens(b)], h3_parts[:, b, 0, :],
                                      ALU.subtract).then_inc(h3_ready[b], 1)
                    top_two(b)
                if step == TURN_GATES:
                    dve.wait_ge(gates_hi[b], 1)
                    dve.tensor_tensor(rounded(gates[:, 1, :]), comb_t[:, tokens(b)], gates[:, 0, :], ALU.subtract
                                      ).then_inc(gates_ready[b], 1)

            seed(0, 0)
            for s in range(UNITS + LAG + 2):
                for j in range(HG):
                    if s < UNITS:
                        add_bias(s, j)
                        if j % 2 and s + 1 < UNITS and seeded_by_vector(s + 1, j - 1):
                            seed(s + 1, j - 1)
                    if j % 2 and 2 * s + j // 2 - 1 in FINISH:
                        finish(0, FINISH[2 * s + j // 2 - 1])
                    if s == UNITS + LAG and j == 1:
                        finish(1, TURN_CTX0)
                    if j % 2 and 2 * s + j // 2 - 2 in FINISH:
                        settle(0, FINISH[2 * s + j // 2 - 2])
                if s == NT + 1:
                    dve.tensor_copy(rounded(eight[:, :]), ident[0:NE, 0:NE]).then_inc(eight_ready, 1)
                if s < NT:
                    link(dve.tensor_reduce(all_masked[:, 0, s:s + 1], mask[:, s, :].bitcast(U16), AX_X, ALU.min))
                if s == NT:
                    link(dve.tensor_scalar(all_masked[:, 1, :], all_masked[:, 0, :], 257.0, None, ALU.subtract))
                    link(dve.reciprocal(all_masked[:, 2, :], all_masked[:, 1, :]))
                    link(dve.tensor_scalar(all_masked[:, 2, :], all_masked[:, 2, :], 0.0, None, ALU.mult))
                    dve.wait_ge(softplus_done, 1)
                    link(dve.tensor_scalar(gam, gam, 0.0, 1e-8, ALU.max, ALU.add))
                    link(dve.tensor_tensor(gam, gam, soft_l, ALU.add))
            finish(0, TURN_GATES)
            settle(0, TURN_GATES)
            finish(1, TURN_CTX1)
            finish(0, GATED_BIAS)

            def gated(c, f):
                dve.wait_ge(up_e_done, c * FT + f + 1)
                if f == 0:
                    dve.wait_ge(gate_copied, c + 1)
                    wait(dve, down_e_done, c - 1)
                dve.scalar_tensor_tensor(hid[:, c % 2, f, :], bank[f][:, :],
                                         L["exp_b1"][:, (c % NE) * FT + f:(c % NE) * FT + f + 1],
                                         gate[:, c % 2, :], ALU.add, ALU.mult).then_inc(hid_gated, 1)

            def rest(c, f):
                dve.wait_ge(hid_hi_ready, c * FT + f + 1)
                dve.scalar_tensor_tensor(rounded(hid_rest[:, c % 2, f, :]), hid[:, c % 2, f, :], 0.0,
                                         hid_hi[:, c % 2, f, :], ALU.max, ALU.subtract).then_inc(hid_ready, 1)

            def add_y(b):
                dve.wait_ge(base_added[b], 1)
                dve.wait_ge(y_turned[b], 1)
                dve.tensor_tensor(xn[:, half(b), :], tiles_of(bank[4 + b]), xn[:, half(b), :], ALU.add
                                  ).then_inc(y_added[b], 1)

            for f in range(FT):
                gated(0, f)
            for c in range(B * NE):
                for f in range(FT):
                    rest(c, f)
                if c == NE:
                    add_y(0)
                for step in LATE_STEPS[2 * c:2 * c + 1]:
                    finish(1, step)
                    settle(1, step)
                if c + 1 < B * NE:
                    for f in range(FT):
                        gated(c + 1, f)
                for step in LATE_STEPS[2 * c + 1:2 * c + 2]:
                    finish(1, step)
                    settle(1, step)
            add_y(1)


def kernel(**inputs):
    import concourse.bacc as bacc
    from concourse.bass_utils import run_bass_kernel_spmd

    def arr(name):
        return np.ascontiguousarray(np.asarray(inputs[name]))

    def l0(name):
        return arr("L0_cond_" + name)

    def l2(name):
        return arr("L2_cond_" + name)

    def l3(name):
        return arr("L3_cond_" + name)

    def pack(columns, parts):
        out = [parts[name].reshape(parts[name].shape[0], -1) for name, _ in columns]
        assert [p.shape[1] for p in out] == [n for _, n in columns]
        return np.ascontiguousarray(np.concatenate(out, axis=1), dtype=np.float32)

    x = arr("x").reshape(TOK, D)
    f32 = np.float32
    half = D // 2
    freq = np.exp(np.arange(half, dtype=f32) * f32(-math.log(10000.0) / (half - 1)))
    early = pack(EARLY, {
        "ident": np.eye(P, dtype=f32), "freq": np.concatenate([freq, freq])[:, None],
        "iota16": np.tile(np.arange(E0, dtype=f32), (P, 1)), "row": np.arange(P, dtype=f32)[:, None],
        "down": l0("down_W").T})

    def stacked(columns):
        return columns.reshape(-1, NH // HG, 2, 2, DH).transpose(0, 1, 3, 4, 2).reshape(-1, D)

    late = pack(LATE, {
        "w_ada": l2("W_ada"), "b_ada": l2("b_ada").reshape(2, D).T, "wq": stacked(l2("Wq")), "wk": stacked(l2("Wk")),
        "wv": l2("Wv"), "wo": l2("Wo"), "bq": stacked(l2("bq")).T, "bk": stacked(l2("bk")).T,
        "g2": l2("g2")[:, None], "beta2": l2("beta2")[:, None], "ln_g": l3("ln_g")[:, None],
        "ln_b": l3("ln_b")[:, None], "router": l3("router_w"), "hyp_w2": l3("hyp_w2"),
        "hyp_b1": l3("hyp_b1")[:, None], "hyp_b2": l3("hyp_b2")[:, None], "sty_w1": l3("sty_w1"),
        "sty_b2": l3("sty_b2").reshape(2, D).T, "b1": l2("b1").reshape(FT, P).T,
        "exp_b1": l3("exp_b1").reshape(NE * FT, P).T, "w1": l2("W1"),
        "w2": l2("W2").reshape(FT, P, D).transpose(1, 0, 2)})
    pack32 = pack(PACK32, {
        "expert_w": l0("expert_W").transpose(2, 1, 0), "expert_b": l0("expert_b").T,
        "emb": l0("domain_emb").T, "down_b": l0("down_b")[:, None], "subj": l3("subj_emb"),
        "eye": np.eye(A, dtype=f32)})
    pack64 = pack(PACK64, {"hyp_w1": l3("hyp_w1"), "sty_b1": l3("sty_b1")[:, None], "sty_w2": l3("sty_w2")})
    rows = np.concatenate([l0("ln_gamma"), l0("ln_beta"), l2("bv"), l2("bo"), l2("b2")])
    arrays = {
        "x_t": np.ascontiguousarray(x.T), "early": early, "late": late, "pack32": pack32,
        "up": np.concatenate([l0("up_W").T, l0("up_b")[None, :]]), "pack64": pack64, "rows": rows,
        "ids": np.concatenate([arr("itok_B_0_15"), arr("itok_B_34_63"), arr("itok_B_6_14")]),
        "ang": np.concatenate([arr("condB_theta"), arr("condB_phi")]),
        "bias": arr("fside_Bx16xSxS_0").reshape(NG, HG, S, S),
        "mask": arr("mask_Bx1xSxS_bk0").reshape(B, S, S),
        "w1": l3("exp_w1"), "w2": l3("exp_w2"), "eb2": l3("exp_b2"),
    }
    nc = bacc.Bacc("TRN2", target_bir_lowering=False, num_devices=1)
    args = [nc.dram_tensor(f"in_{n}", a.shape, mybir.dt.from_np(a.dtype), kind="ExternalInput").ap()
            for n, a in arrays.items()]
    args.append(nc.dram_tensor("out", (B, S, D), F32, kind="ExternalOutput").ap())
    build(nc, *args)
    r = run_bass_kernel_spmd(nc, [{f"in_{n}": a for n, a in arrays.items()}], core_ids=[0])
    return r.results[0]["out"]
```
